# Optimizing a Trainium2 kernel written in Bass

```python
import numpy as np
import jax
import jax.numpy as jnp

def _softmax(x, axis=-1):
    return jax.nn.softmax(x, axis=axis)

def _gelu(x):
    return jax.nn.gelu(x, approximate=True)

def _silu(x):
    return jax.nn.silu(x)

def _sigmoid(x):
    return jax.nn.sigmoid(x)

def _layernorm(x, axis=-1, eps=1e-05):
    m = jnp.mean(x, axis=axis, keepdims=True)
    v = jnp.var(x, axis=axis, keepdims=True)
    return (x - m) / jnp.sqrt(v + eps)

def _scatter_add(tgt, idx, src, axis=0):
    return tgt.at[idx].add(src)

def _segment_sum(src, seg, n):
    return jax.ops.segment_sum(src, seg, n)
kernel_name = 'mk_flamingo_gated_d4_seqx_r8_ac9643'

def setup_inputs(seed: int=0):
    np.random.seed(seed)
    _w = jnp.asarray

    def _rec_inputs():
        import jax
        import jax.numpy as jnp
        _rk = jax.random.key(seed)
        x = -0.0003929 + 0.9999 * jax.random.normal(jax.random.fold_in(_rk, 1), (4, 256, 512), jnp.float32)
        _lenS = 256 - jax.random.randint(jax.random.fold_in(_rk, 7), (4,), 0, max(1, 256 // 4) + 1, jnp.int32)
        _lenS2 = 64 - jax.random.randint(jax.random.fold_in(_rk, 8), (4,), 0, max(1, 64 // 4) + 1, jnp.int32)
        _ctx_4096P = jax.random.normal(jax.random.fold_in(_rk, 11), (4, 16, 512), jnp.float32)
        _ctx_4096c = jax.random.dirichlet(jax.random.fold_in(_rk, 511), 0.3 * jnp.ones((16,), jnp.float32), (4, 64))
        _ctx_4096t = jnp.einsum('bsk,bkd->bsd', _ctx_4096c, _ctx_4096P)
        _ctx_4096t = _ctx_4096t * jax.lax.rsqrt(jnp.mean(jnp.square(_ctx_4096t)) + 1e-12) * 0.953939
        ctx_4096 = 2.81802e-05 + 1.00001 * (_ctx_4096t + 0.3 * jax.random.normal(jax.random.fold_in(_rk, 611), (4, 64, 512), jnp.float32))
        _validS = jnp.arange(256)[None, :] < _lenS[:, None]
        _validS2 = jnp.arange(64)[None, :] < _lenS2[:, None]
        _causal = jnp.tril(jnp.ones((256, 256), dtype=bool))
        mask_1x1xSxS2_ff0 = jnp.where(jnp.ones((1, 1, 256, 64), dtype=bool), 0.0, -1000000000.0).astype(jnp.float32)
        _g = jax.random.normal(jax.random.fold_in(_rk, 9001), (2, 4), jnp.float32)
        _g = jnp.sign(_g) * jnp.maximum(jnp.abs(_g), 1.0) + (_g == 0) * 1.0
        g_xattn = _g[0]
        g_ffn = _g[1]
        return (x, ctx_4096, mask_1x1xSxS2_ff0, g_xattn, g_ffn)
    x, ctx_4096, mask_1x1xSxS2_ff0, g_xattn, g_ffn = _rec_inputs()

    def _L0_xattn_setup():
        import jax, jax.numpy as jnp
        import numpy as np
        B, S, F = (2, 256, 512)
        HQ, HKV, D = (32, 8, 128)
        REP = HQ // HKV
        key = jax.random.key(seed)
        ks = jax.random.split(key, 6)
        scale = 0.02
        return {'query': jax.random.normal(ks[0], (B, S, F), jnp.float32), 'value': jax.random.normal(ks[1], (B, S, F), jnp.float32), 'wq': jax.random.normal(ks[2], (F, HQ * D), jnp.float32) * scale, 'wk': jax.random.normal(ks[3], (F, HKV * D), jnp.float32) * scale, 'wv': jax.random.normal(ks[4], (F, HKV * D), jnp.float32) * scale, 'wo': jax.random.normal(ks[5], (HQ * D, F), jnp.float32) * scale}
    _L0_xattn_all = _L0_xattn_setup()
    _L0_xattn_in = {k: v for k, v in _L0_xattn_all.items() if k in ('wq', 'wk', 'wv', 'wo')}
    del _L0_xattn_all

    def _L0_ffn_setup():
        import jax, jax.numpy as jnp
        import numpy as np
        OUT_FEATURES = 512
        IN_FEATURES = 512
        GROUP_SIZE = 64
        PACKED_NUMEL = OUT_FEATURES * IN_FEATURES // 2
        N_GROUPS = OUT_FEATURES * IN_FEATURES // GROUP_SIZE
        key = jax.random.key(seed)
        k_x, k_w, k_s, k_z = jax.random.split(key, 4)
        x = jax.random.normal(k_x, (2, 256, IN_FEATURES), dtype=jnp.float32)
        W_q = jax.random.randint(k_w, (PACKED_NUMEL,), 0, 32, dtype=jnp.int32).astype(jnp.uint8)
        scale = jax.random.uniform(k_s, (N_GROUPS, 1), dtype=jnp.float32) * 0.1 + 0.001
        zero = jax.random.uniform(k_z, (N_GROUPS, 1), dtype=jnp.float32) * 15.0
        return {'x': x, 'W_q': W_q, 'scale': scale, 'zero': zero}
    _L0_ffn_all = _L0_ffn_setup()
    _L0_ffn_in = {k: v for k, v in _L0_ffn_all.items() if k in ('W_q', 'scale', 'zero')}
    del _L0_ffn_all

    def _L1_xattn_setup():
        import jax, jax.numpy as jnp
        import numpy as np
        HIDDEN = 512
        N_HEADS = 32
        N_KV_HEADS = 8
        HEAD_DIM = HIDDEN // N_HEADS
        N_REP = N_HEADS // N_KV_HEADS
        EPS = 1e-05

        def _rmsnorm(x, w):
            xf = x.astype(jnp.float32)
            var = jnp.mean(xf * xf, axis=-1, keepdims=True)
            return (xf * jax.lax.rsqrt(var + EPS)).astype(x.dtype) * w
        key = jax.random.key(seed)
        ks = jax.random.split(key, 7)
        B, Q, K = (2, 128, 256)
        scale = 0.02
        return {'hidden_states': jax.random.normal(ks[0], (B, Q, HIDDEN), jnp.float32), 'encoder_hidden_states': jax.random.normal(ks[1], (B, K, HIDDEN), jnp.float32), 'wq': jax.random.normal(ks[2], (N_HEADS * HEAD_DIM, HIDDEN), jnp.float32) * scale, 'wk': jax.random.normal(ks[3], (N_KV_HEADS * HEAD_DIM, HIDDEN), jnp.float32) * scale, 'wv': jax.random.normal(ks[4], (N_KV_HEADS * HEAD_DIM, HIDDEN), jnp.float32) * scale, 'wo': jax.random.normal(ks[5], (HIDDEN, N_HEADS * HEAD_DIM), jnp.float32) * scale, 'ln_w': jnp.ones((HIDDEN,), jnp.float32)}
    _L1_xattn_all = _L1_xattn_setup()
    _L1_xattn_in = {k: v for k, v in _L1_xattn_all.items() if k in ('wq', 'wk', 'wv', 'wo', 'ln_w')}
    del _L1_xattn_all

    def _L1_ffn_setup():
        import jax, jax.numpy as jnp
        import numpy as np
        N_EXPERTS = 28
        TOP_K = 2
        RANK = 8
        LORA_ALPHA = 16
        SCALING = LORA_ALPHA / RANK
        TEMP = 1.0
        key = jax.random.key(seed)
        ks = jax.random.split(key, 5)
        B, S, D_IN, D_OUT = (4, 256, 512, 512)
        x = jax.random.normal(ks[0], (B, S, D_IN), dtype=jnp.float32)
        base_W = jax.random.normal(ks[1], (D_OUT, D_IN), dtype=jnp.float32) * (1.0 / np.sqrt(D_IN))
        gate_W = jax.random.normal(ks[2], (N_EXPERTS, D_IN), dtype=jnp.float32) * (1.0 / np.sqrt(D_IN))
        lora_A = jax.random.normal(ks[3], (N_EXPERTS, RANK, D_IN), dtype=jnp.float32) * (1.0 / np.sqrt(D_IN))
        lora_B = jax.random.normal(ks[4], (N_EXPERTS, D_OUT, RANK), dtype=jnp.float32) * 0.01
        return {'x': x, 'base_W': base_W, 'gate_W': gate_W, 'lora_A': lora_A, 'lora_B': lora_B}
    _L1_ffn_all = _L1_ffn_setup()
    _L1_ffn_in = {k: v for k, v in _L1_ffn_all.items() if k in ('base_W', 'gate_W', 'lora_A', 'lora_B')}
    del _L1_ffn_all

    def _L2_xattn_setup():
        import jax, jax.numpy as jnp
        import numpy as np
        TEXT_DIM = 512
        FEATURE_DIM = 512

        def _xavier_uniform(key, shape):
            fan_in, fan_out = (shape[1], shape[0])
            limit = float(np.sqrt(6.0 / (fan_in + fan_out)))
            return jax.random.uniform(key, shape, jnp.float32, -limit, limit)
        key = jax.random.key(seed)
        k1, k2, k3, k4 = jax.random.split(key, 4)
        text = jax.random.normal(k1, (8, 256, TEXT_DIM), jnp.float32)
        features = jax.random.normal(k2, (8, 72, FEATURE_DIM), jnp.float32)
        Wq = _xavier_uniform(k3, (FEATURE_DIM, TEXT_DIM))
        bq = jnp.zeros((FEATURE_DIM,), jnp.float32)
        Wk = _xavier_uniform(k4, (FEATURE_DIM, FEATURE_DIM))
        bk = jnp.zeros((FEATURE_DIM,), jnp.float32)
        return {'text': text, 'features': features, 'Wq': Wq, 'bq': bq, 'Wk': Wk, 'bk': bk}
    _L2_xattn_all = _L2_xattn_setup()
    _L2_xattn_in = {k: v for k, v in _L2_xattn_all.items() if k in ('Wq', 'bq', 'Wk', 'bk')}
    del _L2_xattn_all

    def _L2_ffn_setup():
        import jax, jax.numpy as jnp
        import numpy as np
        NF4_CODE = jnp.array([-1.0, -0.6961928009986877, -0.5250730514526367, -0.39491748809814453, -0.28444138169288635, -0.18477343022823334, -0.09105003625154495, 0.0, 0.07958029955625534, 0.16093020141124725, 0.24611230194568634, 0.33791524171829224, 0.44070982933044434, 0.5626170039176941, 0.7229568362236023, 1.0], dtype=jnp.float32)
        BLOCKSIZE = 64

        def nf4_quant_dequant(w):
            shape = w.shape
            flat = w.reshape(-1, BLOCKSIZE)
            absmax = jnp.max(jnp.abs(flat), axis=1, keepdims=True)
            normalized = flat / jnp.where(absmax == 0, 1.0, absmax)
            bounds = (NF4_CODE[:-1] + NF4_CODE[1:]) * 0.5
            idx = jnp.searchsorted(bounds, normalized)
            return (NF4_CODE[idx] * absmax).reshape(shape)
        key = jax.random.key(seed)
        k1, k2, k3, kx = jax.random.split(key, 4)
        D, H = (512, 1376)
        scale = 0.02
        w1 = jax.random.normal(k1, (H, D), jnp.float32) * scale
        w2 = jax.random.normal(k2, (H, D), jnp.float32) * scale
        w3 = jax.random.normal(k3, (D, H), jnp.float32) * scale
        x = jax.random.normal(kx, (2, 256, D), jnp.float32)
        return {'x': x, 'w1': w1, 'w2': w2, 'w3': w3}
    _L2_ffn_all = _L2_ffn_setup()
    _L2_ffn_in = {k: v for k, v in _L2_ffn_all.items() if k in ('w1', 'w2', 'w3')}
    del _L2_ffn_all

    def _L3_xattn_setup():
        import jax, jax.numpy as jnp
        import numpy as np
        NUM_HEADS = 32
        NUM_KV_HEADS = 8
        HEAD_DIM = 128
        HIDDEN = 512
        EPS = 1e-05

        def rmsnorm(x, w, eps=EPS):
            xf = x.astype(jnp.float32)
            var = jnp.mean(xf * xf, axis=-1, keepdims=True)
            return w * (xf * jax.lax.rsqrt(var + eps)).astype(x.dtype)
        key = jax.random.key(seed)
        ks = jax.random.split(key, 10)
        B, Q, KV = (1, 128, 6404)
        s = 1.0 / np.sqrt(HIDDEN)
        return {'hidden_states': jax.random.normal(ks[0], (B, Q, HIDDEN), jnp.float32), 'cross_attention_states': jax.random.normal(ks[1], (B, KV, HIDDEN), jnp.float32), 'attention_mask': jnp.zeros((B, 1, Q, KV), jnp.float32), 'q_proj_w': jax.random.normal(ks[2], (NUM_HEADS * HEAD_DIM, HIDDEN), jnp.float32) * s, 'k_proj_w': jax.random.normal(ks[3], (NUM_KV_HEADS * HEAD_DIM, HIDDEN), jnp.float32) * s, 'v_proj_w': jax.random.normal(ks[4], (NUM_KV_HEADS * HEAD_DIM, HIDDEN), jnp.float32) * s, 'o_proj_w': jax.random.normal(ks[5], (HIDDEN, NUM_HEADS * HEAD_DIM), jnp.float32) * s, 'q_norm_w': jnp.ones((HEAD_DIM,), jnp.float32), 'k_norm_w': jnp.ones((HEAD_DIM,), jnp.float32)}
    _L3_xattn_all = _L3_xattn_setup()
    _L3_xattn_in = {k: v for k, v in _L3_xattn_all.items() if k in ('q_proj_w', 'k_proj_w', 'v_proj_w', 'o_proj_w', 'q_norm_w', 'k_norm_w')}
    del _L3_xattn_all

    def _L3_ffn_setup():
        import jax, jax.numpy as jnp
        import numpy as np
        N_STREAMS = 4
        DIM = 128
        SINKHORN_ITERS = 50
        SINKHORN_TAU = 0.1
        RMS_EPS = 1.1920929e-07

        def sinkhorn_log(logits, num_iters=SINKHORN_ITERS, tau=SINKHORN_TAU):
            Z = logits / tau
            u0 = jnp.zeros(Z.shape[:-1], Z.dtype)
            v0 = jnp.zeros_like(u0)

            def step(carry, _):
                u, v = carry
                u = -jax.nn.logsumexp(Z + v[..., None, :], axis=-1)
                v = -jax.nn.logsumexp(Z + u[..., :, None], axis=-2)
                return ((u, v), None)
            (u, v), _ = jax.lax.scan(step, (u0, v0), None, length=num_iters)
            return jnp.exp(Z + u[..., :, None] + v[..., None, :])
        key = jax.random.key(seed)
        ks = jax.random.split(key, 6)
        B, T = (4, 256)
        n, C = (N_STREAMS, DIM)
        wd = n * C
        x = jax.random.normal(ks[0], (B, T, wd), dtype=jnp.float32)
        W_res = 0.01 * jax.random.normal(ks[1], (n * n, wd), dtype=jnp.float32)
        W_pre = 0.01 * jax.random.normal(ks[2], (n, wd), dtype=jnp.float32)
        W_post = 0.01 * jax.random.normal(ks[3], (n, wd), dtype=jnp.float32)
        H_res_base = jnp.full((n, n), -0.5, dtype=jnp.float32)
        H_res_base = H_res_base.at[jnp.arange(n), jnp.arange(n)].set(0.0)
        H_pre_base = jnp.zeros((n,), dtype=jnp.float32).at[0].set(1.0)
        H_post_base = jnp.zeros((n,), dtype=jnp.float32)
        gate = jnp.array([5.0], dtype=jnp.float32)
        W_branch = 1.0 / np.sqrt(C) * jax.random.normal(ks[4], (C, C), dtype=jnp.float32)
        return {'x': x, 'W_res': W_res, 'W_pre': W_pre, 'W_post': W_post, 'H_res_base': H_res_base, 'H_pre_base': H_pre_base, 'H_post_base': H_post_base, 'gate': gate, 'W_branch': W_branch}
    _L3_ffn_all = _L3_ffn_setup()
    _L3_ffn_in = {k: v for k, v in _L3_ffn_all.items() if k in ('W_res', 'W_pre', 'W_post', 'H_res_base', 'H_pre_base', 'H_post_base', 'gate', 'W_branch')}
    del _L3_ffn_all
    return {'x': x, 'ctx_4096': ctx_4096, 'mask_1x1xSxS2_ff0': mask_1x1xSxS2_ff0, 'g_xattn': g_xattn, 'g_ffn': g_ffn, 'L0_xattn_wq': _L0_xattn_in['wq'], 'L0_xattn_wk': _L0_xattn_in['wk'], 'L0_xattn_wv': _L0_xattn_in['wv'], 'L0_xattn_wo': _L0_xattn_in['wo'], 'L0_ffn_W_q': _L0_ffn_in['W_q'], 'L0_ffn_scale': _L0_ffn_in['scale'], 'L0_ffn_zero': _L0_ffn_in['zero'], 'L1_xattn_wq': _L1_xattn_in['wq'], 'L1_xattn_wk': _L1_xattn_in['wk'], 'L1_xattn_wv': _L1_xattn_in['wv'], 'L1_xattn_wo': _L1_xattn_in['wo'], 'L1_xattn_ln_w': _L1_xattn_in['ln_w'], 'L1_ffn_base_W': _L1_ffn_in['base_W'], 'L1_ffn_gate_W': _L1_ffn_in['gate_W'], 'L1_ffn_lora_A': _L1_ffn_in['lora_A'], 'L1_ffn_lora_B': _L1_ffn_in['lora_B'], 'L2_xattn_Wq': _L2_xattn_in['Wq'], 'L2_xattn_bq': _L2_xattn_in['bq'], 'L2_xattn_Wk': _L2_xattn_in['Wk'], 'L2_xattn_bk': _L2_xattn_in['bk'], 'L2_ffn_w1': _L2_ffn_in['w1'], 'L2_ffn_w2': _L2_ffn_in['w2'], 'L2_ffn_w3': _L2_ffn_in['w3'], 'L3_xattn_q_proj_w': _L3_xattn_in['q_proj_w'], 'L3_xattn_k_proj_w': _L3_xattn_in['k_proj_w'], 'L3_xattn_v_proj_w': _L3_xattn_in['v_proj_w'], 'L3_xattn_o_proj_w': _L3_xattn_in['o_proj_w'], 'L3_xattn_q_norm_w': _L3_xattn_in['q_norm_w'], 'L3_xattn_k_norm_w': _L3_xattn_in['k_norm_w'], 'L3_ffn_W_res': _L3_ffn_in['W_res'], 'L3_ffn_W_pre': _L3_ffn_in['W_pre'], 'L3_ffn_W_post': _L3_ffn_in['W_post'], 'L3_ffn_H_res_base': _L3_ffn_in['H_res_base'], 'L3_ffn_H_pre_base': _L3_ffn_in['H_pre_base'], 'L3_ffn_H_post_base': _L3_ffn_in['H_post_base'], 'L3_ffn_gate': _L3_ffn_in['gate'], 'L3_ffn_W_branch': _L3_ffn_in['W_branch']}

def reference(x, ctx_4096, mask_1x1xSxS2_ff0, g_xattn, g_ffn, L0_xattn_wq, L0_xattn_wk, L0_xattn_wv, L0_xattn_wo, L0_ffn_W_q, L0_ffn_scale, L0_ffn_zero, L1_xattn_wq, L1_xattn_wk, L1_xattn_wv, L1_xattn_wo, L1_xattn_ln_w, L1_ffn_base_W, L1_ffn_gate_W, L1_ffn_lora_A, L1_ffn_lora_B, L2_xattn_Wq, L2_xattn_bq, L2_xattn_Wk, L2_xattn_bk, L2_ffn_w1, L2_ffn_w2, L2_ffn_w3, L3_xattn_q_proj_w, L3_xattn_k_proj_w, L3_xattn_v_proj_w, L3_xattn_o_proj_w, L3_xattn_q_norm_w, L3_xattn_k_norm_w, L3_ffn_W_res, L3_ffn_W_pre, L3_ffn_W_post, L3_ffn_H_res_base, L3_ffn_H_pre_base, L3_ffn_H_post_base, L3_ffn_gate, L3_ffn_W_branch):
    import jax
    import jax.numpy as jnp

    def _L0_xattn_ref(query, value, wq, wk, wv, wo):
        import jax, jax.numpy as jnp
        import numpy as np
        B, S, F = (2, 256, 512)
        HQ, HKV, D = (32, 8, 128)
        REP = HQ // HKV
        key = value
        b, tq, _ = query.shape
        tk = key.shape[1]
        q = (query @ wq).reshape(b, tq, HQ, D)
        k = (key @ wk).reshape(b, tk, HKV, D)
        v = (value @ wv).reshape(b, tk, HKV, D)
        k = jnp.repeat(k, REP, axis=2)
        v = jnp.repeat(v, REP, axis=2)
        q = q * (1.0 / jnp.sqrt(jnp.asarray(D, q.dtype)))
        scores = jnp.einsum('bqhd,bkhd->bhqk', q, k)
        probs = jax.nn.softmax(scores, axis=-1)
        out = jnp.einsum('bhqk,bkhd->bqhd', probs, v).reshape(b, tq, HQ * D)
        return out @ wo

    def _L0_ffn_ref(x, W_q, scale, zero):
        import jax, jax.numpy as jnp
        import numpy as np
        OUT_FEATURES = 512
        IN_FEATURES = 512
        GROUP_SIZE = 64
        PACKED_NUMEL = OUT_FEATURES * IN_FEATURES // 2
        N_GROUPS = OUT_FEATURES * IN_FEATURES // GROUP_SIZE
        dtype = x.dtype
        wq_flat = W_q.reshape(-1)
        high = wq_flat >> 4 & 15
        low = wq_flat & 15
        w_uint = jnp.concatenate([high, low]).astype(dtype)
        w_grouped = w_uint.reshape(-1, GROUP_SIZE)
        w_fp = ((w_grouped - zero.astype(dtype)) * scale.astype(dtype)).reshape(OUT_FEATURES, IN_FEATURES)
        return jnp.einsum('bsi,oi->bso', x, w_fp)

    def _L1_xattn_ref(hidden_states, encoder_hidden_states, wq, wk, wv, wo, ln_w):
        import jax, jax.numpy as jnp
        import numpy as np
        HIDDEN = 512
        N_HEADS = 32
        N_KV_HEADS = 8
        HEAD_DIM = HIDDEN // N_HEADS
        N_REP = N_HEADS // N_KV_HEADS
        EPS = 1e-05

        def _rmsnorm(x, w):
            xf = x.astype(jnp.float32)
            var = jnp.mean(xf * xf, axis=-1, keepdims=True)
            return (xf * jax.lax.rsqrt(var + EPS)).astype(x.dtype) * w
        B, Qlen, _ = hidden_states.shape
        _, Klen, _ = encoder_hidden_states.shape
        x = _rmsnorm(hidden_states, ln_w)
        q = jnp.einsum('bqd,hd->bqh', x, wq).reshape(B, Qlen, N_HEADS, HEAD_DIM)
        k = jnp.einsum('bkd,hd->bkh', encoder_hidden_states, wk).reshape(B, Klen, N_KV_HEADS, HEAD_DIM)
        v = jnp.einsum('bkd,hd->bkh', encoder_hidden_states, wv).reshape(B, Klen, N_KV_HEADS, HEAD_DIM)
        q = q.transpose(0, 2, 1, 3)
        k = k.transpose(0, 2, 1, 3)
        v = v.transpose(0, 2, 1, 3)
        k = jnp.repeat(k, N_REP, axis=1)
        v = jnp.repeat(v, N_REP, axis=1)
        scores = jnp.einsum('bhqd,bhkd->bhqk', q, k) / np.sqrt(HEAD_DIM).astype(np.float32)
        attn = jax.nn.softmax(scores.astype(jnp.float32), axis=-1).astype(q.dtype)
        out = jnp.einsum('bhqk,bhkd->bhqd', attn, v)
        out = out.transpose(0, 2, 1, 3).reshape(B, Qlen, HIDDEN)
        return jnp.einsum('bqh,dh->bqd', out, wo)

    def _L1_ffn_ref(x, base_W, gate_W, lora_A, lora_B):
        import jax, jax.numpy as jnp
        import numpy as np
        N_EXPERTS = 28
        TOP_K = 2
        RANK = 8
        LORA_ALPHA = 16
        SCALING = LORA_ALPHA / RANK
        TEMP = 1.0
        B, S, D_in = x.shape
        xf = x.reshape(B * S, D_in)
        base = xf @ base_W.T
        logits = xf @ gate_W.T
        top_vals, top_idx = jax.lax.top_k(logits, TOP_K)
        top_probs = jax.nn.softmax(top_vals / TEMP, axis=-1)
        N = xf.shape[0]
        gate_full = jnp.zeros((N, N_EXPERTS), dtype=xf.dtype).at[jnp.arange(N)[:, None], top_idx].add(top_probs)
        h = jnp.einsum('nd,erd->ner', xf, lora_A)
        h = h * (gate_full * SCALING)[:, :, None]
        lora_out = jnp.einsum('ner,eor->no', h, lora_B)
        out = base + lora_out
        return out.reshape(B, S, -1)

    def _L2_xattn_ref(text, features, Wq, bq, Wk, bk):
        import jax, jax.numpy as jnp
        import numpy as np
        TEXT_DIM = 512
        FEATURE_DIM = 512

        def _xavier_uniform(key, shape):
            fan_in, fan_out = (shape[1], shape[0])
            limit = float(np.sqrt(6.0 / (fan_in + fan_out)))
            return jax.random.uniform(key, shape, jnp.float32, -limit, limit)
        Q = jnp.einsum('btx,dx->btd', text, Wq) + bq
        K = jnp.einsum('bpx,dx->bpd', features, Wk) + bk
        scale = 1.0 / jnp.sqrt(jnp.asarray(K.shape[-1], K.dtype))
        scores = jnp.einsum('btd,bpd->btp', Q, K) * scale
        attn = jax.nn.softmax(scores, axis=-1)
        attended = jnp.einsum('btp,bpd->btd', attn, features)
        return attended

    def _L2_ffn_ref(x, w1, w2, w3):
        import jax, jax.numpy as jnp
        import numpy as np
        NF4_CODE = jnp.array([-1.0, -0.6961928009986877, -0.5250730514526367, -0.39491748809814453, -0.28444138169288635, -0.18477343022823334, -0.09105003625154495, 0.0, 0.07958029955625534, 0.16093020141124725, 0.24611230194568634, 0.33791524171829224, 0.44070982933044434, 0.5626170039176941, 0.7229568362236023, 1.0], dtype=jnp.float32)
        BLOCKSIZE = 64

        def nf4_quant_dequant(w):
            shape = w.shape
            flat = w.reshape(-1, BLOCKSIZE)
            absmax = jnp.max(jnp.abs(flat), axis=1, keepdims=True)
            normalized = flat / jnp.where(absmax == 0, 1.0, absmax)
            bounds = (NF4_CODE[:-1] + NF4_CODE[1:]) * 0.5
            idx = jnp.searchsorted(bounds, normalized)
            return (NF4_CODE[idx] * absmax).reshape(shape)
        dq1 = nf4_quant_dequant(w1)
        dq2 = nf4_quant_dequant(w2)
        dq3 = nf4_quant_dequant(w3)
        gate = jnp.einsum('bsd,hd->bsh', x, dq1)
        up = jnp.einsum('bsd,hd->bsh', x, dq2)
        h = jax.nn.silu(gate) * up
        return jnp.einsum('bsh,dh->bsd', h, dq3)

    def _L3_xattn_ref(hidden_states, cross_attention_states, attention_mask, q_proj_w, k_proj_w, v_proj_w, o_proj_w, q_norm_w, k_norm_w):
        import jax, jax.numpy as jnp
        import numpy as np
        NUM_HEADS = 32
        NUM_KV_HEADS = 8
        HEAD_DIM = 128
        HIDDEN = 512
        EPS = 1e-05

        def rmsnorm(x, w, eps=EPS):
            xf = x.astype(jnp.float32)
            var = jnp.mean(xf * xf, axis=-1, keepdims=True)
            return w * (xf * jax.lax.rsqrt(var + eps)).astype(x.dtype)
        B, Q, _ = hidden_states.shape
        KV = cross_attention_states.shape[1]
        n_rep = NUM_HEADS // NUM_KV_HEADS
        q = (hidden_states @ q_proj_w.T).reshape(B, Q, NUM_HEADS, HEAD_DIM).transpose(0, 2, 1, 3)
        k = (cross_attention_states @ k_proj_w.T).reshape(B, KV, NUM_KV_HEADS, HEAD_DIM).transpose(0, 2, 1, 3)
        v = (cross_attention_states @ v_proj_w.T).reshape(B, KV, NUM_KV_HEADS, HEAD_DIM).transpose(0, 2, 1, 3)
        q = rmsnorm(q, q_norm_w)
        k = jnp.repeat(k, n_rep, axis=1)
        v = jnp.repeat(v, n_rep, axis=1)
        k = rmsnorm(k, k_norm_w)
        scale = 1.0 / np.sqrt(HEAD_DIM)
        scores = jnp.einsum('bhqd,bhkd->bhqk', q, k) * scale + attention_mask
        attn = jax.nn.softmax(scores.astype(jnp.float32), axis=-1).astype(q.dtype)
        out = jnp.einsum('bhqk,bhkd->bhqd', attn, v)
        out = out.transpose(0, 2, 1, 3).reshape(B, Q, NUM_HEADS * HEAD_DIM)
        return out @ o_proj_w.T

    def _L3_ffn_ref(x, W_res, W_pre, W_post, H_res_base, H_pre_base, H_post_base, gate, W_branch):
        import jax, jax.numpy as jnp
        import numpy as np
        N_STREAMS = 4
        DIM = 128
        SINKHORN_ITERS = 50
        SINKHORN_TAU = 0.1
        RMS_EPS = 1.1920929e-07

        def sinkhorn_log(logits, num_iters=SINKHORN_ITERS, tau=SINKHORN_TAU):
            Z = logits / tau
            u0 = jnp.zeros(Z.shape[:-1], Z.dtype)
            v0 = jnp.zeros_like(u0)

            def step(carry, _):
                u, v = carry
                u = -jax.nn.logsumexp(Z + v[..., None, :], axis=-1)
                v = -jax.nn.logsumexp(Z + u[..., :, None], axis=-2)
                return ((u, v), None)
            (u, v), _ = jax.lax.scan(step, (u0, v0), None, length=num_iters)
            return jnp.exp(Z + u[..., :, None] + v[..., None, :])
        B, T, nC = x.shape
        n = N_STREAMS
        C = nC // n
        x_norm = x * jax.lax.rsqrt(jnp.mean(x * x, axis=-1, keepdims=True) + RMS_EPS)
        H_res_logits = (x_norm @ W_res.T).reshape(B, T, n, n) + H_res_base
        H_pre_logits = x_norm @ W_pre.T + H_pre_base
        H_post_logits = x_norm @ W_post.T + H_post_base
        H_res = sinkhorn_log(H_res_logits)
        H_pre = jax.nn.softmax(H_pre_logits, axis=-1)
        H_post = jax.nn.softmax(H_post_logits, axis=-1)
        g = jax.nn.sigmoid(gate)[0]
        I = jnp.eye(n, dtype=H_res.dtype)
        H_res = (1.0 - g) * I + g * H_res
        x_streams = x.reshape(B, T, n, C)
        x_pre = jnp.einsum('btnc,btn->btc', x_streams, H_pre)
        y = x_pre @ W_branch
        x_mixed = jnp.einsum('btij,btjc->btic', H_res, x_streams)
        y_distributed = jnp.einsum('btc,btn->btnc', y, H_post)
        return (x_mixed + y_distributed).reshape(B, T, nC)
    x = x + jnp.tanh(g_xattn[0]) * _L0_xattn_ref(_layernorm(x, axis=-1), ctx_4096, L0_xattn_wq, L0_xattn_wk, L0_xattn_wv, L0_xattn_wo)
    x = x + jnp.tanh(g_ffn[0]) * _L0_ffn_ref(_layernorm(x, axis=-1), L0_ffn_W_q, L0_ffn_scale, L0_ffn_zero)
    x = x + jnp.tanh(g_xattn[1]) * _L1_xattn_ref(_layernorm(x, axis=-1), ctx_4096, L1_xattn_wq, L1_xattn_wk, L1_xattn_wv, L1_xattn_wo, L1_xattn_ln_w)
    x = x + jnp.tanh(g_ffn[1]) * _L1_ffn_ref(_layernorm(x, axis=-1), L1_ffn_base_W, L1_ffn_gate_W, L1_ffn_lora_A, L1_ffn_lora_B)
    x = x + jnp.tanh(g_xattn[2]) * _L2_xattn_ref(_layernorm(x, axis=-1), ctx_4096, L2_xattn_Wq, L2_xattn_bq, L2_xattn_Wk, L2_xattn_bk)
    x = x + jnp.tanh(g_ffn[2]) * _L2_ffn_ref(_layernorm(x, axis=-1), L2_ffn_w1, L2_ffn_w2, L2_ffn_w3)
    x = x + jnp.tanh(g_xattn[3]) * _L3_xattn_ref(_layernorm(x, axis=-1), ctx_4096, mask_1x1xSxS2_ff0, L3_xattn_q_proj_w, L3_xattn_k_proj_w, L3_xattn_v_proj_w, L3_xattn_o_proj_w, L3_xattn_q_norm_w, L3_xattn_k_norm_w)
    x = x + jnp.tanh(g_ffn[3]) * _L3_ffn_ref(_layernorm(x, axis=-1), L3_ffn_W_res, L3_ffn_W_pre, L3_ffn_W_post, L3_ffn_H_res_base, L3_ffn_H_pre_base, L3_ffn_H_post_base, L3_ffn_gate, L3_ffn_W_branch)
    return x

_drawn_inputs = setup_inputs


def setup_inputs(seed=0):
    import zlib

    import numpy as np

    out = dict(_drawn_inputs(seed))
    spreads = {'L1_xattn_ln_w': (1.0, 0.6),
     'L2_xattn_bq': (0.0, 2.0),
     'L2_xattn_bk': (0.0, 2.0),
     'L3_xattn_q_norm_w': (1.0, 0.6),
     'L3_xattn_k_norm_w': (1.0, 0.6),
     'L3_ffn_H_post_base': (0.0, 2.0)}
    factors = {'g_ffn': 7.892,
     'L0_xattn_wq': 3.273,
     'L0_xattn_wk': 3.285,
     'L1_xattn_wq': 8.0,
     'L1_xattn_wk': 8.0,
     'L1_xattn_wv': 3.354,
     'L1_xattn_wo': 3.408,
     'L1_ffn_gate_W': 8.0,
     'L1_ffn_lora_A': 8.0,
     'L1_ffn_lora_B': 8.0,
     'L2_ffn_w1': 5.72,
     'L2_ffn_w2': 5.597,
     'L2_ffn_w3': 5.613,
     'L3_ffn_W_pre': 30.538,
     'L3_ffn_W_post': 8.0,
     'L3_ffn_H_pre_base': 5.947,
     'L3_ffn_W_branch': 3.227,
     'L3_ffn_W_res': 5.008}
    for name, (base, spread) in spreads.items():
        noise = np.random.default_rng([zlib.crc32(name.encode()), seed]).standard_normal(out[name].shape)
        drawn = base * np.exp(spread * noise) if base else spread * noise
        out[name] = jnp.asarray(drawn.astype(out[name].dtype))
    for name, factor in factors.items():
        out[name] = (out[name] * factor).astype(out[name].dtype)
    return out
```

```python
import concourse.bass as bass
from concourse import mybir
from contextlib import ExitStack
import numpy as np

F32 = mybir.dt.float32
F32R = mybir.dt.float32r
U8 = mybir.dt.uint8
ALU = mybir.AluOpType
ACT = mybir.ActivationFunctionType
AX = mybir.AxisListType

P = 128
B, S, D = 4, 256, 512
SK = 64
T = B * S // P
C = D // P
NG, HG, DH = 8, 4, 128
HS = HG // 2
WQ = HG * DH
WG = WQ + 2 * DH
NH1, DH1, NKV1 = 32, 16, 8
HC1 = P // DH1
NE, RANK = 28, 8
ER = NE * RANK
EH = ER // 2
LORA_SCALE = 2.0
HF = 1376
NF = -(-HF // P)
QB = 64
NB3 = D * HF // P // QB
NBU = NF * D // QB // NG
NBT = 3 * NBU
NFW = NF * D
NS = 4
NL = NS * NS + 2 * NS
SK_LINEAR = 24
EPS = 1e-5
EPS_RMS = 1.1920929e-07
BIG_INDEX = 1024.0
HALF_MAX = 1.7e38

CODE = [np.float32(v) for v in (
    -1.0, -0.6961928009986877, -0.5250730514526367, -0.39491748809814453, -0.28444138169288635,
    -0.18477343022823334, -0.09105003625154495, 0.0, 0.07958029955625534, 0.16093020141124725,
    0.24611230194568634, 0.33791524171829224, 0.44070982933044434, 0.5626170039176941,
    0.7229568362236023, 1.0)]
STEPS = []
for _i in list(range(7, 15)) + list(range(6, -1, -1)):
    _bound = float(np.float32((CODE[_i] + CODE[_i + 1]) * np.float32(0.5)))
    _rise = float(np.float32(CODE[_i + 1] - CODE[_i]))
    STEPS.append((ALU.is_gt, _bound, _rise) if _i >= 7 else (ALU.is_le, _bound, -_rise))


def build(nc, x_d, ctxT_d, ctxB_d, gx_d, gf_d, wl_d, ol_d, w4_d, sc4_d, ze4_d, l1wqv_d, l1kr_d, l1o_d,
          lnw_d, l1f_d, lb_d, l2k_d, l2q_d, b2_d, nf_d, qkn_d, mask_d, iota_d, w24_d, bases_d, gate_d, wbr_d, out_d):
    scratch = nc.dram_tensor("dequantised", [P, 3, NFW], F32, kind="Internal").ap()
    ctx = ExitStack()
    with ctx:
        def sb(name, shape, dt=F32):
            return ctx.enter_context(nc.sbuf_tensor(name, shape, dt))

        def sem(name):
            return ctx.enter_context(nc.semaphore(name))

        X = sb("X", [P, T, D])
        HN = sb("HN", [P, 2, D])
        HTh = sb("HTh", [P, C, T * P], F32R)
        HTl = sb("HTl", [P, C, T * P], F32R)
        CT = sb("CT", [P, C, B * SK])
        CTh = sb("CTh", [P, C, B * SK], F32R)
        CTl = sb("CTl", [P, C, B * SK], F32R)
        ident = sb("ident", [P, P])
        ones = sb("ones", [P, P])
        gates = sb("gates", [P, 2, 4])
        tg = sb("tg", [P, 2, 4])
        st = sb("st", [P, T, 6])
        mv = sb("mv", [P, T, 2])
        veps = sb("veps", [P, 2, T])
        rstd = sb("rstd", [P, T])
        rms = sb("rms", [P, T])
        half = sb("half", [P, T])
        sm = sb("sm", [P, 4, 32])
        qkn = sb("qkn", [P, 2])
        qkw = sb("qkw", [P, 1])
        lnw = sb("lnw", [P, D])
        WR = sb("WR", [P, C * WG])
        Wh = sb("Wh", [P, C * WG], F32R)
        Wl = sb("Wl", [P, C * WG], F32R)
        OR = sb("OR", [P, 4 * D])
        Oh = sb("Oh", [P, 4 * D], F32R)
        Ol = sb("Ol", [P, 4 * D], F32R)
        qT = sb("qT", [P, 2, HG * S])
        s_sb = sb("s_sb", [P, 2, 2 * D])
        PT = sb("PT", [P, 2 * D])
        OTh = sb("OTh", [P, HG * S], F32R)
        OTl = sb("OTl", [P, HG * S], F32R)
        v_sb = sb("v_sb", [P, B, DH])
        kT = sb("kT", [P, B * SK])
        kn = sb("kn", [P, 2, DH])
        AR = sb("AR", [P, 10240])
        PS = ctx.enter_context(nc.psum_tensor("PS", [P, 8, 512], F32))

        def bank(i, n=1):
            return PS[:, i, :] if n == 1 else PS[:, i:i + n, :].rearrange("p a b -> p (a b)")

        block = ctx.enter_context(nc.Block())

        x_in, consts_in, ctx_in = sem("x_in"), sem("consts_in"), sem("ctx_in")
        pool_consts, gates_ready, ctx_hi, ctx_split = sem("pool_consts"), sem("gates_ready"), sem("ctx_hi"), sem("ctx_split")
        stats, rstd_ready, hn_ready = sem("stats"), sem("rstd_ready"), sem("hn_ready")
        hn_turned, hi_ready, lo_ready = sem("hn_turned"), sem("hi_ready"), sem("lo_ready")
        out_stored = sem("out_stored")

        class Sems:

            def __init__(self, stage, names):
                self.all = {n: sem(f"{stage}_{n}") for n in names.split()}

            def __getitem__(self, n):
                return self.all[n]

        ATT = ("w_in o_in w_hi o_hi w_split o_split kv_mm kn_ready v_ready kt_mm kt_ready q_mm qT_ready s_mm s_read "
               "shifted exps probs t_mm pt_ready pv_mm ohi olo wo_mm acc ksq krs qrs_in qrs "
               "kn_in mask_in nf_in nf_mask nf_added nf_out nf_stored nf_free nf_norm")
        A = Sems("att", ATT)
        F0 = Sems("f0", "w_in packed w_hi split mm acc")
        A1 = Sems("a1", "w_in kr_in o_in w_hi o_hi w_split o_split kr_mm kr_out v_out q_mm qT_ready s_mm "
                        "shifted exps probs t_mm pt_ready pv_mm ohi olo wo_mm acc")
        F1 = Sems("f1", "w_in b_in w_hi split lg_mm lg_ready gap egap h_ready t_mm ht_ready mm acc")
        A2 = Sems("a2", "k_in q_in b_in k_mm kt_ready m_mm mhi mlo s_mm shifted exps probs t_mm "
                        "pt_ready mm acc")
        F2 = Sems("f2", "in0 in1 t_mm whi wlo g_mm u_mm silu act ahi alo mm acc")
        F3 = Sems("f3", "w_in w_hi wlo lg_mm to_act from_act pre preT_mm preT y_mm done")

        def mm3(out, ah, al, bh, bl, first, last_):
            nc.tensor.matmul(out, ah, bh, start=first, stop=False)
            nc.tensor.matmul(out, ah, bl, start=False, stop=False)
            return nc.tensor.matmul(out, al, bh, start=False, stop=last_)

        def hn_of(n, t):
            if n == 7:
                return AR[:, t * D:(t + 1) * D]
            return HN[:, t % 2, :]

        def dve_norm(dve, n):
            if n == 0:
                dve.wait_ge(x_in, 16)
            dve.drain()
            for t in range(T):
                nc.vector.bn_stats(st[:, t, :], X[:, t, :])
            dve.drain()
            for t in range(T):
                i = nc.vector.bn_aggr(mv[:, t, :], st[:, t, :])
            i.then_inc(stats, 1)
            dve.wait_ge(rstd_ready, n + 1)
            if n == 2:
                nc.vector.tensor_tensor(rstd[:], rstd[:], rms[:], ALU.mult)
                dve.wait_ge(consts_in, CONSTS)
                dve.drain()

            def low(t):
                dve.wait_ge(hi_ready, T * n + t + 1)
                cols = slice(t * P, (t + 1) * P)
                nc.vector.tensor_tensor(HTl[:, :, cols], bank(t % 2).rearrange("p (c k) -> p c k", c=C),
                                        HTh[:, :, cols].bitcast(F32), ALU.subtract).then_inc(lo_ready, 1)

            for t in range(T):
                if t >= 2 and n != 7:
                    dve.wait_ge(hn_turned, T * n + t - 1)
                i = nc.vector.tensor_scalar(hn_of(n, t), X[:, t, :], mv[:, t, 0:1], rstd[:, t:t + 1],
                                            ALU.subtract, ALU.mult)
                if n == 2:
                    dve.drain()
                    i = nc.vector.tensor_tensor(hn_of(n, t), hn_of(n, t), lnw[:], ALU.mult)
                i.then_inc(hn_ready, 1)
                if t:
                    low(t - 1)
            low(T - 1)

        def pool_norm(pool, n):
            pool.wait_ge(stats, n + 1)
            nc.gpsimd.tensor_scalar(veps[:, 0, :], mv[:, :, 1], EPS, None, ALU.add)
            pool.drain()
            i = nc.gpsimd.tensor_tensor(rstd[:], veps[:, 0, :], half[:], ALU.pow)
            if n in (2, 7):
                pool.drain()
                nc.gpsimd.tensor_tensor(veps[:, 1, :], mv[:, :, 1], rstd[:], ALU.mult)
                pool.drain()
                nc.gpsimd.tensor_tensor(veps[:, 1, :], veps[:, 1, :], rstd[:], ALU.mult)
                pool.drain()
                nc.gpsimd.tensor_scalar(veps[:, 1, :], veps[:, 1, :], EPS if n == 2 else EPS_RMS, None, ALU.add)
                pool.drain()
                i = nc.gpsimd.tensor_tensor(rms[:], veps[:, 1, :], half[:], ALU.pow)
            i.then_inc(rstd_ready, 1)

        def pe_norm(pe, n):
            if n == 0:
                pe.wait_ge(pool_consts, 1)
            for t in range(T):
                pe.wait_ge(hn_ready, T * n + t + 1)
                if t >= 2:
                    pe.wait_ge(lo_ready, T * n + t - 1)
                for c in range(C):
                    i = nc.tensor.transpose(bank(t % 2)[:, c * P:(c + 1) * P], hn_of(n, t)[:, c * P:(c + 1) * P],
                                            ident[:])
                i.then_inc(hn_turned, 1)
            pe.wait_ge(lo_ready, T * n + T)

        def act_norm(act, n):
            for t in range(T):
                act.wait_ge(hn_turned, T * n + t + 1)
                nc.scalar.copy(HTh[:, :, t * P:(t + 1) * P], bank(t % 2).rearrange("p (c k) -> p c k", c=C))\
                    .then_inc(hi_ready, 1)

        def w3d(t_, lo, hi_):
            return t_[:].rearrange("p (c n) -> p c n", c=C)[:, :, lo:hi_]

        def sp_attention(sp, a, l0):
            g0 = 0 if l0 else NG

            def load_w(g):
                sp.dma_start(WR[:], wl_d[g]).then_inc(a["w_in"], 16)

            def load_o(g):
                sp.dma_start(OR[:], ol_d[g]).then_inc(a["o_in"], 16)
            nf = l0
            nf_in = AR[:, 0:NBT * QB]
            if not l0:
                sp.wait_ge(F2["t_mm"], 3 * NF)
            load_w(g0)
            load_o(g0)

            def store(g):
                sp.wait_ge(a["nf_out"], g + 2)
                n = NBU * QB
                sp.dma_start(scratch[:, :, bass.ds(g * n, n)],
                             AR[:, NBT * QB:2 * NBT * QB].rearrange("p (w n) -> p w n", w=3))\
                    .then_inc(a["nf_stored"], 16)
                sp.wait_ge(a["nf_stored"], g * 16 + 16)
                sp.sem_inc(a["nf_free"], 1)
            if not l0:
                sp.dma_start(mask_sb, mask_d).then_inc(a["mask_in"], 16)
            if nf:
                sp.dma_start(nf_in, nf_d[0]).then_inc(a["nf_in"], 16)
                sp.sem_inc(a["nf_free"], 1)
            with sp.Fori(g0 + 1, g0 + NG) as g:
                sp.wait_ge(a["w_split"], g)
                load_w(g)
                sp.wait_ge(a["o_split"], g)
                load_o(g)
                if nf:
                    sp.wait_ge(a["nf_norm"], g)
                    sp.dma_start(nf_in, nf_d[g]).then_inc(a["nf_in"], 16)
                    store(g - 1)
            if nf:
                store(NG - 1)

        def pool_low(hi, lo, raw):
            return nc.gpsimd.tensor_tensor(lo, raw, hi.bitcast(F32), ALU.subtract)

        def pool_attention(pool, a, l0):
            g0 = 0 if l0 else NG
            if l0:
                pool.drain().then_inc(a["nf_added"], 1)
                pool.drain().then_inc(a["nf_out"], 1)
            pool.wait_ge(a["w_hi"], g0 + 1)
            pool_low(Wh[:], Wl[:], WR[:]).then_inc(a["w_split"], 1)
            if not l0:
                pool_norm(pool, 6)

            def steps(g, ids):
                N = NBT * QB
                for i in ids:
                    pool.wait_ge(a["nf_mask"], g * len(STEPS) + i + 1)
                    if i == 1:
                        pool.wait_ge(a["nf_free"], g + 1)
                    acc_ = AR[:, N:2 * N] if i > 1 else AR[:, 2 * N:3 * N]
                    nc.gpsimd.tensor_tensor(AR[:, N:2 * N], acc_, AR[:, (2 + i % 2) * N:(3 + i % 2) * N], ALU.add)\
                        .then_inc(a["nf_added"], 1)
                    pool.drain()

            def nf_scale(g):
                nf_acc = AR[:, NBT * QB:2 * NBT * QB].rearrange("p (n q) -> p n q", q=QB)
                nc.gpsimd.tensor_tensor(nf_acc, nf_acc, absmax[:].unsqueeze(2).to_broadcast([P, NBT, QB]),
                                        ALU.mult).then_inc(a["nf_out"], 1)

            def turn(g, more):
                if not l0:
                    pool.wait_ge(a["ksq"], g - (NG - 1))
                    ks = sm[:, 0, 0:2]
                    nc.gpsimd.tensor_tensor(ks, ks, tiny[:, 0:2], ALU.add)
                    pool.drain()
                    nc.gpsimd.tensor_tensor(sm[:, 0, 2:4], ks, half[:, 0:2], ALU.pow).then_inc(a["krs"], 1)
                pool.wait_ge(a["o_hi"], g + 1)
                pool_low(Oh[:], Ol[:], OR[:]).then_inc(a["o_split"], 1)
                if not l0:
                    for b in range(B):
                        pool.wait_ge(a["qrs_in"], g * B + (b + 1 - NG * B))
                        qs = sm[:, 0, 8:16]
                        nc.gpsimd.tensor_tensor(qs, qs, tiny[:, 8:16], ALU.add)
                        pool.drain()
                        nc.gpsimd.tensor_tensor(sm[:, 0, 16:24], qs, half[:], ALU.pow).then_inc(a["qrs"], 1)
                else:
                    steps(g, range(1, 5))
                if more:
                    pool.wait_ge(a["w_hi"], g + 2)
                    pool_low(Wh[:], Wl[:], WR[:]).then_inc(a["w_split"], 1)
                if l0:
                    steps(g, range(5, len(STEPS)))
                    nf_scale(g)
            with pool.Fori(g0, g0 + NG - 1) as g:
                turn(g, True)
            turn(g0 + NG - 1, False)

        tiny = sb("tiny", [P, 16])
        hm = sb("hm", [P, HC1])
        b2 = sb("b2", [P, 2 * C])
        iot = sb("iot", [P, NE])
        bases = sb("bases", [P, NL])
        gate = sb("gate", [P, 1])
        absmax = sb("absmax", [P, NBT])
        rabs = sb("rabs", [P, NBT])

        mask_sb = AR[:, 2 * HG * S:2 * HG * S + 2 * SK]
        def qrs_store():
            return sm[:, 0, 16:24]

        def pe_attention(pe, a, l0):
            g0 = 0 if l0 else NG

            def turn(g):
                u0 = g * B

                def project_kv():
                    pe.wait_ge(a["w_split"], g + 1)
                    for j in range(2):
                        for c in range(C):
                            rows = slice(j * P, (j + 1) * P)
                            i = mm3(bank(4)[:, j * 256:(j + 1) * 256], CTh[:, c, rows], CTl[:, c, rows],
                                    w3d(Wh, WQ, WG)[:, c], w3d(Wl, WQ, WG)[:, c], c == 0, c == C - 1)
                    i.then_inc(a["kv_mm"], 1)

                def turn_k():
                    pe.wait_ge(a["kn_ready"], g + 1)
                    pe.wait_ge(a["acc"], u0 * 2 + 1)
                    for j in range(2):
                        i = nc.tensor.transpose(bank(7)[:, j * P:(j + 1) * P], kn[:, j, :], ident[:])
                    i.then_inc(a["kt_mm"], 1)

                def project_q(b):
                    if b:
                        pe.wait_ge(a["qT_ready"], (u0 + b) * 2)
                    for pr in range(HS):
                        for hh in range(2):
                            h = 2 * pr + hh
                            for c in range(C):
                                tok = slice(b * S, (b + 1) * S)
                                i = mm3(bank(pr)[:, hh * S:(hh + 1) * S], w3d(Wh, h * DH, (h + 1) * DH)[:, c],
                                        w3d(Wl, h * DH, (h + 1) * DH)[:, c], HTh[:, c, tok], HTl[:, c, tok],
                                        c == 0, c == C - 1)
                        i.then_inc(a["q_mm"], 1)

                def scores(b):
                    pe.wait_ge(a["qT_ready"], (u0 + b) * 2 + 2)
                    if b == 0:
                        pe.wait_ge(a["kt_ready"], g + 1)
                    pe.wait_ge(a["s_read"], u0 + (b + 1))
                    if not l0:
                        for tt in range(2):
                            for h in range(HG):
                                nc.tensor.matmul(bank(3)[:, tt * HG + h:tt * HG + h + 1],
                                                 qsq(b)[:, h * S + tt * P:h * S + tt * P + P], ones[:, 0:1],
                                                 start=True, stop=True)
                    for tt in range(2):
                        for h in range(HG):
                            col = (tt * HG + h) * SK
                            i = nc.tensor.matmul(bank(2)[:, col:col + SK],
                                                 qT[:, b % 2, h * S + tt * P:h * S + tt * P + P],
                                                 kT[:, b * SK:(b + 1) * SK], start=True, stop=True)
                    i.then_inc(a["s_mm"], 1)

                def turn_p(b):
                    pe.wait_ge(a["probs"], u0 + (b + 1))
                    if b == 0:
                        pe.wait_ge(a["v_ready"], g + 1)
                    for pr in range(HS):
                        for tt in range(2):
                            i = nc.tensor.transpose(
                                bank(4)[:, (pr * 2 + tt) * P:(pr * 2 + tt + 1) * P],
                                s_sb[:, b % 2, tt * 256 + pr * P:tt * 256 + (pr + 1) * P], ident[:])
                    i.then_inc(a["t_mm"], 1)

                def weigh(b):
                    pe.wait_ge(a["pt_ready"], u0 + (b + 1))
                    pe.wait_ge(a["acc"], (u0 + b) * 2 + 1)
                    for h in range(HG):
                        half_ = slice(SK * (h % 2), SK * (h % 2 + 1))
                        i = nc.tensor.matmul(bank(5 + h % 2)[:, (h // 2) * S:(h // 2 + 1) * S],
                                             v_sb[half_, b, :], PT[half_, (h // 2) * S:(h // 2 + 1) * S],
                                             start=True, stop=True)
                    i.then_inc(a["pv_mm"], 1)

                def project_o(b):
                    pe.wait_ge(a["olo"], u0 + (b + 1))
                    if b == 0:
                        pe.wait_ge(a["o_split"], g + 1)
                    for tt in range(2):
                        for h in range(HG):
                            tok = slice(h * S + tt * P, h * S + tt * P + P)
                            i = mm3(bank(7 if tt == 0 else 5), OTh[:, tok], OTl[:, tok],
                                    Oh[:, h * D:(h + 1) * D], Ol[:, h * D:(h + 1) * D], h == 0, h == HG - 1)
                        i.then_inc(a["wo_mm"], 1)
                project_kv()
                project_q(0)
                turn_k()
                project_q(1)
                scores(0)
                project_q(2)
                turn_p(0)
                scores(1)
                weigh(0)
                project_q(3)
                project_o(0)
                for b in (1, 2):
                    turn_p(b)
                    scores(b + 1)
                    weigh(b)
                    project_o(b)
                turn_p(3)
                weigh(3)
                project_o(3)
            with pe.Fori(g0, g0 + NG) as g:
                turn(g)

        def qsq(b):
            return AR[:, (b % 2) * HG * S:(b % 2 + 1) * HG * S]

        def act_attention(act, a, l0):
            g0 = 0 if l0 else NG

            def turn(g, more):
                u0 = g * B
                act.wait_ge(a["kv_mm"], g + 1)
                kv = bank(4).rearrange("p (j n) -> p j n", j=2)
                nc.scalar.copy(kn[:], kv[:, :, 0:DH]).then_inc(a["kn_ready" if l0 else "kn_in"], 1)
                for par in range(2):
                    for hf in range(2):
                        i = nc.scalar.copy(v_sb[SK * hf:SK * (hf + 1), par::2, :],
                                           kv[SK * par:SK * (par + 1), :, DH:2 * DH])
                i.then_inc(a["v_ready"], 1)

                def queries(b):
                    for pr in range(HS):
                        act.wait_ge(a["q_mm"], (u0 + b) * 2 + pr + 1)
                        cols = slice(pr * 2 * S, (pr + 1) * 2 * S)
                        if not l0:
                            nc.scalar.square(qsq(b)[:, cols], bank(pr))
                        nc.scalar.copy(qT[:, b % 2, cols], bank(pr)).then_inc(a["qT_ready"], 1)

                def keys():
                    act.wait_ge(a["kt_mm"], g + 1)
                    if l0:
                        nc.scalar.copy(kT[:], bank(7)[:, 0:B * SK]).then_inc(a["kt_ready"], 1)
                    else:
                        nc.scalar.activation(kT[:], bank(7)[:, 0:B * SK], ACT.Copy, scale=qkw[:, 0:1])\
                            .then_inc(a["kt_ready"], 1)

                def exps(b):
                    act.wait_ge(a["shifted"], u0 + (b + 1))
                    s = s_sb[:, b % 2, 0:512]
                    nc.scalar.activation(s, s, ACT.Exp, scale=float(DH) ** -0.5 if l0 else 1.0).then_inc(a["exps"], 1)

                def probs_t(b):
                    act.wait_ge(a["t_mm"], u0 + (b + 1))
                    nc.scalar.copy(PT[:, 0:512], bank(4)).then_inc(a["pt_ready"], 1)

                def heads(b):
                    act.wait_ge(a["pv_mm"], u0 + (b + 1))
                    for par in range(2):
                        i = nc.scalar.copy(OTh[:].rearrange("p (r q s) -> p q r s", q=2, s=S)[:, par],
                                           bank(5 + par).rearrange("p (r s) -> p r s", s=S))
                    i.then_inc(a["ohi"], 1)
                queries(0)
                keys()
                act.wait_ge(a["o_in"], g * 16 + 16)
                nc.scalar.copy(Oh[:], OR[:]).then_inc(a["o_hi"], 1)
                queries(1)
                exps(0)
                queries(2)
                probs_t(0)
                exps(1)
                heads(0)
                queries(3)
                for b in (1, 2):
                    probs_t(b)
                    exps(b + 1)
                    heads(b)
                    if b == 1 and more:
                        act.wait_ge(a["w_in"], g * 16 + 32)
                        act.wait_ge(a["q_mm"], g * 8 + 8)
                        nc.scalar.copy(Wh[:], WR[:]).then_inc(a["w_hi"], 1)
                probs_t(3)
                heads(3)
            act.wait_ge(a["w_in"], g0 * 16 + 16)
            if not l0:
                act.wait_ge(F2["mm"], T * NF)
            nc.scalar.copy(Wh[:], WR[:]).then_inc(a["w_hi"], 1)
            if not l0:
                act_norm(act, 6)
            with act.Fori(g0, g0 + NG - 1) as g:
                turn(g, True)
            turn(g0 + NG - 1, False)

        def softmax_shift(dve, out, src, n, w, stat):
            m = stat[:, 0:n]
            nc.vector.tensor_reduce(m, src.rearrange("p (n w) -> p n w", w=w), AX.X, ALU.max)
            dve.drain()
            return nc.vector.tensor_tensor(out.rearrange("p (n w) -> p n w", w=w),
                                           src.rearrange("p (n w) -> p n w", w=w),
                                           m.unsqueeze(2).to_broadcast([P, n, w]), ALU.subtract)

        def softmax_norm(dve, buf, n, w, stat):
            v = buf.rearrange("p (n w) -> p n w", w=w)
            nc.vector.reduce_sum(stat[:, 0:n], v, AX.X)
            dve.drain()
            nc.vector.reciprocal(stat[:, 0:n], stat[:, 0:n])
            dve.drain()
            return nc.vector.tensor_tensor(v, v, stat[:, 0:n].unsqueeze(2).to_broadcast([P, n, w]), ALU.mult)

        def dve_attention(dve, a, l0):
            g0 = 0 if l0 else NG
            li = 0 if l0 else 3
            if not l0:
                dve.wait_ge(a["mask_in"], 16)
                nc.vector.tensor_tensor(qkw[:], qkn[:, 0:1], qkn[:, 1:2], ALU.mult)
                dve.drain()
            if l0:
                dve.drain().then_inc(a["acc"], 1)
                dve.drain().then_inc(a["s_read"], 1)
            N = NBT * QB
            nf_in, nf_acc = AR[:, 0:N], AR[:, N:2 * N]

            def turn(g):
                u0 = g * B
                if not l0:
                    dve.wait_ge(a["kn_in"], g - (NG - 1))
                    for j in range(2):
                        nc.vector.tensor_tensor(s_sb[:, 1, 512 + j * P:512 + (j + 1) * P], kn[:, j, :],
                                                kn[:, j, :], ALU.mult)
                    dve.drain()
                    nc.vector.reduce_sum(sm[:, 0, 4:6], s_sb[:, 1, 512:768].rearrange("p (j n) -> p j n", j=2), AX.X)
                    dve.drain()
                    nc.vector.tensor_scalar(sm[:, 0, 0:2], sm[:, 0, 4:6], 1.0 / DH, None, ALU.mult)\
                        .then_inc(a["ksq"], 1)
                    dve.wait_ge(a["krs"], g - (NG - 1))
                    for j in range(2):
                        i = nc.vector.tensor_scalar(kn[:, j, :], kn[:, j, :], sm[:, 0, 2 + j:3 + j], None, ALU.mult)
                    i.then_inc(a["kn_ready"], 1)
                else:
                    dve.wait_ge(a["nf_out"], g + 1)
                    dve.wait_ge(a["nf_in"], g * 16 + 16)
                    blocks = nf_in.rearrange("p (n q) -> p n q", q=QB)
                    nc.vector.tensor_reduce(absmax[:], blocks, AX.X, ALU.max, apply_absolute_value=True)
                    dve.drain()
                    nc.vector.scalar_tensor_tensor(rabs[:], absmax[:], 0.0, absmax[:], ALU.is_equal, ALU.add)
                    dve.drain()
                    nc.vector.reciprocal(rabs[:], rabs[:])
                    dve.drain()
                    nc.vector.tensor_tensor(blocks, blocks, rabs[:].unsqueeze(2).to_broadcast([P, NBT, QB]), ALU.mult)
                    dve.drain()

                def masks(ids):
                    if not l0:
                        return
                    for i in ids:
                        dve.wait_ge(a["nf_added"], g * (len(STEPS) - 1) + (1 if i < 2 else max(i - 1, 2)))
                        op, bound, rise = STEPS[i]
                        i_ = nc.vector.tensor_scalar(AR[:, (2 + i % 2) * N:(3 + i % 2) * N], nf_in, bound, rise,
                                                     op, ALU.mult)
                        i_.then_inc(a["nf_mask"], 1)
                    if ids[-1] == len(STEPS) - 1:
                        dve.drain().then_inc(a["nf_norm"], 1)

                def shift(b):
                    dve.wait_ge(a["s_mm"], u0 + (b + 1))
                    s = s_sb[:, b % 2, 0:512]
                    src = bank(2)
                    if not l0:
                        nc.vector.tensor_copy(sm[:, 0, 8:16], bank(3)[:, 0:8]).then_inc(a["qrs_in"], 1)
                        dve.wait_ge(a["qrs"], u0 + (b + 1 - NG * B))
                        nc.vector.tensor_tensor(s.rearrange("p (n w) -> p n w", w=SK),
                                                src.rearrange("p (n w) -> p n w", w=SK),
                                                qrs_store().unsqueeze(2).to_broadcast([P, 8, SK]), ALU.mult)\
                            .then_inc(a["s_read"], 1)
                        dve.drain()
                        s4 = s.rearrange("p (t h k) -> p t h k", t=2, h=HG)
                        nc.vector.tensor_tensor(s4, s4, mask_sb.rearrange("p (t k) -> p t k", t=2).unsqueeze(2)
                                                .to_broadcast([P, 2, HG, SK]), ALU.add)
                        dve.drain()
                        softmax_shift(dve, s, s, 8, SK, sm[:, 1, :]).then_inc(a["shifted"], 1)
                    else:
                        softmax_shift(dve, s, src, 8, SK, sm[:, 1, :]).then_inc(a["shifted"], 1)
                        dve.drain().then_inc(a["s_read"], 1)

                def norm(b):
                    dve.wait_ge(a["exps"], u0 + (b + 1))
                    softmax_norm(dve, s_sb[:, b % 2, 0:512], 8, SK, sm[:, 1, :]).then_inc(a["probs"], 1)

                def low(b):
                    dve.wait_ge(a["ohi"], u0 + (b + 1))
                    for par in range(2):
                        v = [o[:].rearrange("p (r q s) -> p q r s", q=2, s=S)[:, par] for o in (OTh, OTl)]
                        i = nc.vector.tensor_tensor(v[1], bank(5 + par).rearrange("p (r s) -> p r s", s=S),
                                                    v[0].bitcast(F32), ALU.subtract)
                    i.then_inc(a["olo"], 1)

                def add(b):
                    for tt in range(2):
                        dve.wait_ge(a["wo_mm"], (u0 + b) * 2 + tt + 1)
                        xt = X[:, 2 * b + tt, :]
                        nc.vector.scalar_tensor_tensor(xt, bank(7 if tt == 0 else 5), tg[:, 0, li:li + 1], xt,
                                                       ALU.mult, ALU.add).then_inc(a["acc"], 1)
                shift(0)
                norm(0)
                masks(range(0, 3))
                shift(1)
                norm(1)
                low(0)
                masks(range(3, 5))
                add(0)
                shift(2)
                norm(2)
                masks(range(5, 7))
                low(1)
                add(1)
                masks(range(7, 9))
                shift(3)
                norm(3)
                low(2)
                masks(range(9, 11))
                add(2)
                masks(range(11, 13))
                low(3)
                masks(range(13, 15))
                add(3)
                dve.drain()
            with dve.Fori(g0, g0 + NG) as g:
                turn(g)

        def pe_f0(pe):
            pe.wait_ge(F0["split"], 1)
            for t in range(T):
                if t >= 4:
                    pe.wait_ge(F0["acc"], t - 3)
                for c in range(C):
                    tok = slice(t * P, (t + 1) * P)
                    i = mm3(bank(2 + t % 4), HTh[:, c, tok], HTl[:, c, tok], Oh[:, c * D:(c + 1) * D],
                            Ol[:, c * D:(c + 1) * D], c == 0, c == C - 1)
                i.then_inc(F0["mm"], 1)

        def dve_f0_dequant(dve):
            dve.wait_ge(F0["w_in"], 16 * 5)
            w8 = AR[:, 4096:4352].bitcast(U8)
            nib = AR[:, 4352:4864].bitcast(U8)
            n3 = nib.rearrange("p (c o) -> p c o", c=C)
            w3 = w8.rearrange("p (c o) -> p c o", c=C)
            nc.vector.tensor_scalar(n3[:, :, 0:256], w3, 4, None, ALU.logical_shift_right)
            nc.vector.tensor_scalar(n3[:, :, 256:512], w3, 15, None, ALU.bitwise_and)
            dve.drain()
            nc.vector.tensor_tensor(WR[:, 0:2048], nib, Ze, ALU.subtract)
            dve.drain()
            nc.vector.tensor_tensor(OR[:], WR[:, 0:2048], Sc, ALU.mult).then_inc(F0["packed"], 1)
        Ze = AR[:, 0:2048]
        Sc = AR[:, 2048:4096]

        def sp_f0(sp):
            sp.wait_ge(A["nf_norm"], NG)
            sp.dma_start(AR[:, 4096:4352].bitcast(mybir.dt.int32), w4_d).then_inc(F0["w_in"], 16)
            for k, (dst, src) in enumerate(((Ze, ze4_d), (Sc, sc4_d))):
                for hf in range(2):
                    d = dst[64 * hf:64 * hf + 64, :]
                    sp.dma_start(d, src[hf:hf + 1, :].to_broadcast([64, 2048])).then_inc(F0["w_in"], 16)

        def dve_sum(dve, s, stage, kind, banks):
            for t in range(T):
                dve.wait_ge(s["mm"], t + 1)
                nc.vector.scalar_tensor_tensor(X[:, t, :], bank(banks[t % len(banks)]), tg[:, kind, stage:stage + 1],
                                               X[:, t, :], ALU.mult, ALU.add).then_inc(s["acc"], 1)

        Kbd = AR[:, 0:C * B * HC1 * SK]
        Vbd = AR[:, C * B * HC1 * SK:C * B * HC1 * SK + B * NKV1 * 2 * DH1]
        NU = B * C

        def sp_a1(sp):
            sp.wait_ge(F0["split"], 1)
            sp.dma_start(OR[:], l1kr_d).then_inc(A1["kr_in"], 16)
            sp.dma_start(WR[:, 0:2560], l1wqv_d).then_inc(A1["w_in"], 16)
            sp.wait_ge(A1["kr_mm"], 1)
            sp.dma_start(OR[:], l1o_d).then_inc(A1["o_in"], 16)

        def pool_a1(pool):
            pool.memset(Vbd, 0.0).then_inc(A1["v_out"], 1)
            pool_norm(pool, 2)
            pool.wait_ge(A1["w_hi"], 1)
            pool_low(Wh[:, 0:2048], Wl[:, 0:2048], WR[:, 0:2048]).then_inc(A1["w_split"], 1)
            pool.wait_ge(A1["o_hi"], 1)
            pool_low(Oh[:], Ol[:], OR[:]).then_inc(A1["o_split"], 1)

        def pe_a1(pe):
            pe.wait_ge(A1["kr_in"], 16)
            pe.wait_ge(F0["acc"], T)
            for hc in range(C):
                for c in range(C):
                    nc.tensor.matmul(bank(2 + hc // 2)[:, (hc % 2) * 256:(hc % 2 + 1) * 256],
                                     OR[:, c * D + hc * P:c * D + (hc + 1) * P], CT[:, c, :],
                                     start=c == 0, stop=c == C - 1)
            pe.wait_ge(A1["w_in"], 16)
            for j in range(2):
                for c in range(C):
                    i = nc.tensor.matmul(bank(4)[:, j * P:(j + 1) * P], CT[:, c, j * P:(j + 1) * P],
                                         WR[:, 2048 + c * P:2048 + (c + 1) * P], start=c == 0, stop=c == C - 1)
            i.then_inc(A1["kr_mm"], 1)
            pe_norm(pe, 2)
            pe.wait_ge(A1["w_split"], 1)

            def project_q(b):
                if b:
                    pe.wait_ge(A1["qT_ready"], 2 * b)
                for pr in range(2):
                    for hh in range(2):
                        hc = 2 * pr + hh
                        for c in range(C):
                            w = slice(c * D + hc * P, c * D + (hc + 1) * P)
                            tok = slice(b * S, (b + 1) * S)
                            i = mm3(bank(pr)[:, hh * S:(hh + 1) * S], Wh[:, w], Wl[:, w], HTh[:, c, tok],
                                    HTl[:, c, tok], c == 0, c == C - 1)
                    i.then_inc(A1["q_mm"], 1)

            def scores(u):
                b, hc = divmod(u, C)
                if u == 0:
                    pe.wait_ge(A1["kr_out"], 1)
                if hc == 0:
                    pe.wait_ge(A1["qT_ready"], 2 * b + 2)
                if u:
                    pe.wait_ge(A1["shifted"], u)
                for tt in range(2):
                    i = nc.tensor.matmul(bank(2 + tt), qT[:, b % 2, hc * S + tt * P:hc * S + tt * P + P],
                                         Kbd[:, u_kbd(hc, b)], start=True, stop=True)
                i.then_inc(A1["s_mm"], 1)

            def u_kbd(hc, b):
                at = (hc * B + b) * HC1 * SK
                return slice(at, at + HC1 * SK)

            def weigh(u):
                b, hc = divmod(u, C)
                pe.wait_ge(A1["probs"], u + 1)
                for pr in range(4):
                    for tt in range(2):
                        i = nc.tensor.transpose(bank(4, 2)[:, (pr * 2 + tt) * P:(pr * 2 + tt + 1) * P],
                                                s_sb[:, u % 2, tt * 512 + pr * P:tt * 512 + (pr + 1) * P], ident[:])
                i.then_inc(A1["t_mm"], 1)
                pe.wait_ge(A1["pt_ready"], u + 1)
                if u:
                    pe.wait_ge(A1["olo"], u)
                if u == 0:
                    pe.wait_ge(A1["v_out"], 2)
                for pr in range(4):
                    at = (b * NKV1 + 2 * hc + pr // 2) * 2 * DH1
                    i = nc.tensor.matmul(bank(6)[32 * pr:32 * pr + 32, 0:S], Vbd[:, at:at + 2 * DH1],
                                         PT[:, pr * S:(pr + 1) * S], start=True, stop=True)
                i.then_inc(A1["pv_mm"], 1)

            project_q(0)
            scores(0)
            for u in range(NU):
                b = u // C
                if u % C == 1 and b < B - 1:
                    project_q(b + 1)
                if u + 1 < NU:
                    scores(u + 1)
                weigh(u)
                if u % C == C - 1:
                    pe.wait_ge(A1["olo"], u + 1)
                    if b == 0:
                        pe.wait_ge(A1["o_split"], 1)
                    for tt in range(2):
                        if 2 * b + tt:
                            pe.wait_ge(A1["acc"], 2 * b + tt)
                        for hc in range(C):
                            tok = slice(hc * S + tt * P, hc * S + tt * P + P)
                            i = mm3(bank(7), OTh[:, tok], OTl[:, tok], Oh[:, hc * D:(hc + 1) * D],
                                    Ol[:, hc * D:(hc + 1) * D], hc == 0, hc == C - 1)
                        i.then_inc(A1["wo_mm"], 1)

        def act_a1(act):
            act.wait_ge(A1["kr_mm"], 1)
            K5 = Kbd.rearrange("p (c b h k) -> p c b h k", c=C, b=B, h=HC1)
            for hc in range(C):
                src = bank(2 + hc // 2)[:, (hc % 2) * 256:(hc % 2 + 1) * 256].rearrange("p (b k) -> p b k", b=B)
                for h in range(HC1):
                    i = nc.scalar.activation(K5[:, hc, :, h, :], src, ACT.Copy, scale=hm[:, h:h + 1])
            i.then_inc(A1["kr_out"], 1)
            act.wait_ge(A1["v_out"], 1)
            V5 = Vbd.rearrange("p (b v q d) -> p b v q d", b=B, v=NKV1, q=2)
            vv = bank(4)[:, 0:256].rearrange("p (j v d) -> p j v d", j=2, v=NKV1)
            for par in range(2):
                for hf in range(2):
                    i = nc.scalar.copy(V5[SK * hf:SK * (hf + 1), par::2, :, hf, :], vv[SK * par:SK * (par + 1)])
            i.then_inc(A1["v_out"], 1)
            nc.scalar.copy(Wh[:, 0:2048], WR[:, 0:2048]).then_inc(A1["w_hi"], 1)
            act.wait_ge(A1["o_in"], 16)
            nc.scalar.copy(Oh[:], OR[:]).then_inc(A1["o_hi"], 1)
            act_norm(act, 2)

            def queries(b):
                for pr in range(2):
                    act.wait_ge(A1["q_mm"], 2 * b + pr + 1)
                    nc.scalar.copy(qT[:, b % 2, pr * 512:(pr + 1) * 512], bank(pr)).then_inc(A1["qT_ready"], 1)

            def exps(u):
                act.wait_ge(A1["shifted"], u + 1)
                nc.scalar.activation(s_sb[:, u % 2, :], s_sb[:, u % 2, :], ACT.Exp, scale=float(DH1) ** -0.5)\
                    .then_inc(A1["exps"], 1)

            queries(0)
            exps(0)
            for u in range(NU):
                if u % C == 1 and u // C < B - 1:
                    queries(u // C + 1)
                act.wait_ge(A1["t_mm"], u + 1)
                nc.scalar.copy(PT[:], bank(4, 2)).then_inc(A1["pt_ready"], 1)
                if u + 1 < NU:
                    exps(u + 1)
                act.wait_ge(A1["pv_mm"], u + 1)
                hc = u % C
                nc.scalar.copy(OTh[:, hc * S:(hc + 1) * S], bank(6)[:, 0:S]).then_inc(A1["ohi"], 1)

        def dve_a1(dve):
            dve_norm(dve, 2)

            def shift(u):
                dve.wait_ge(A1["s_mm"], u + 1)
                softmax_shift(dve, s_sb[:, u % 2, :], bank(2, 2), 16, SK, sm[:, 1, :]).then_inc(A1["shifted"], 1)

            shift(0)
            for u in range(NU):
                dve.wait_ge(A1["exps"], u + 1)
                softmax_norm(dve, s_sb[:, u % 2, :], 16, SK, sm[:, 2, :]).then_inc(A1["probs"], 1)
                if u + 1 < NU:
                    shift(u + 1)
                dve.wait_ge(A1["ohi"], u + 1)
                b, hc = divmod(u, C)
                cols = slice(hc * S, (hc + 1) * S)
                nc.vector.tensor_tensor(OTl[:, cols], bank(6)[:, 0:S], OTh[:, cols].bitcast(F32), ALU.subtract)\
                    .then_inc(A1["olo"], 1)
                if hc == C - 1:
                    for tt in range(2):
                        dve.wait_ge(A1["wo_mm"], 2 * b + tt + 1)
                        xt = X[:, 2 * b + tt, :]
                        nc.vector.scalar_tensor_tensor(xt, bank(7), tg[:, 0, 1:2], xt, ALU.mult, ALU.add)\
                            .then_inc(A1["acc"], 1)

        NWF = D + NE + ER
        G = AR[:, 0:T * (NE + ER)]
        TK = AR[:, 2048:2048 + 8 * T * NE]

        def tk(i):
            return TK[:, i * T * NE:(i + 1) * T * NE]

        def sp_f1(sp):
            sp.wait_ge(A1["w_split"], 1)
            sp.wait_ge(A1["kr_mm"], 1)
            sp.dma_start(WR[:, 0:C * NWF], l1f_d).then_inc(F1["w_in"], 16)
            sp.wait_ge(A1["o_split"], 1)
            sp.dma_start(OR[0:EH, 0:2 * D], lb_d).then_inc(F1["b_in"], 16)

        def pool_f1(pool):
            pool.wait_ge(F1["w_hi"], 1)
            pool_low(Wh[:, 0:C * NWF], Wl[:, 0:C * NWF], WR[:, 0:C * NWF]).then_inc(F1["split"], 1)
            pool_norm(pool, 3)

        def wf(t_, c, lo, hi_):
            return t_[:, c * NWF + lo:c * NWF + hi_]

        def pe_f1(pe):
            pe_norm(pe, 3)
            pe.wait_ge(F1["split"], 1)
            for t in range(T):
                if t >= 2:
                    pe.wait_ge(F1["lg_ready"], t - 1)
                for c in range(C):
                    tok = slice(t * P, (t + 1) * P)
                    i = mm3(bank(6 + t % 2)[:, 0:NE + ER], HTh[:, c, tok], HTl[:, c, tok],
                            wf(Wh, c, D, NWF), wf(Wl, c, D, NWF), c == 0, c == C - 1)
                i.then_inc(F1["lg_mm"], 1)

            def base(t):
                if t >= 4:
                    pe.wait_ge(F1["acc"], t - 3)
                for c in range(C):
                    tok = slice(t * P, (t + 1) * P)
                    mm3(bank(2 + t % 4), HTh[:, c, tok], HTl[:, c, tok], wf(Wh, c, 0, D), wf(Wl, c, 0, D),
                        c == 0, False)
            for t in range(3):
                base(t)
            pe.wait_ge(F1["h_ready"], 1)
            pe.wait_ge(F1["b_in"], 16)
            for t in range(T):
                if t == 0:
                    pe.wait_ge(F1["lg_ready"], T)
                for e in range(2):
                    at = t * (NE + ER) + NE + e * EH
                    i = nc.tensor.transpose(bank(6 + t % 2)[0:EH, e * P:(e + 1) * P], G[:, at:at + EH], ident[:])
                i.then_inc(F1["t_mm"], 1)
                if t + 3 < T:
                    base(t + 3)
                pe.wait_ge(F1["ht_ready"], t + 1)
                for e in range(2):
                    at = (t % 2) * 256 + e * P
                    i = nc.tensor.matmul(bank(2 + t % 4), PT[0:EH, at:at + P], OR[0:EH, e * D:(e + 1) * D],
                                         start=False, stop=e == 1)
                i.then_inc(F1["mm"], 1)

        def act_f1(act):
            act.wait_ge(F1["w_in"], 16)
            act.wait_ge(A1["wo_mm"], T)
            nc.scalar.copy(Wh[:, 0:C * NWF], WR[:, 0:C * NWF]).then_inc(F1["w_hi"], 1)
            act_norm(act, 3)
            for t in range(T):
                act.wait_ge(F1["lg_mm"], t + 1)
                nc.scalar.copy(G[:, t * (NE + ER):(t + 1) * (NE + ER)], bank(6 + t % 2)[:, 0:NE + ER])\
                    .then_inc(F1["lg_ready"], 1)
            act.wait_ge(F1["gap"], 1)
            nc.scalar.activation(sm[:, 0, 16:24], sm[:, 0, 16:24], ACT.Exp).then_inc(F1["egap"], 1)
            for t in range(T):
                act.wait_ge(F1["t_mm"], t + 1)
                nc.scalar.copy(PT[0:EH, (t % 2) * 256:(t % 2 + 1) * 256], bank(6 + t % 2)[0:EH, 0:256])\
                    .then_inc(F1["ht_ready"], 1)

        def dve_f1(dve):
            dve_norm(dve, 3)
            dve.wait_ge(F1["lg_ready"], T)
            G3 = G.rearrange("p (t n) -> p t n", t=T)

            def v3(i):
                return tk(i).rearrange("p (t n) -> p t n", t=T)
            L = G3[:, :, 0:NE]
            iob = iot[:].unsqueeze(1).to_broadcast([P, T, NE])

            def col(k):
                return sm[:, 0, k * T:(k + 1) * T]

            def bc(k):
                return col(k).unsqueeze(2).to_broadcast([P, T, NE])

            def pick(src, top, at, one):
                nc.vector.tensor_reduce(col(top), src, AX.X, ALU.max)
                dve.drain()
                nc.vector.tensor_tensor(v3(5), src, bc(top), ALU.is_equal)
                dve.drain()
                nc.vector.tensor_tensor(v3(5), v3(5), iob, ALU.mult)
                dve.drain()
                nc.vector.tensor_reduce(col(at), v3(5), AX.X, ALU.min)
                dve.drain()
                nc.vector.tensor_tensor(v3(one), iob, bc(at), ALU.is_equal)
                dve.drain()
            pick(L, 0, 1, 0)
            nc.vector.tensor_scalar(tk(2), tk(0), -2.0 * HALF_MAX, HALF_MAX, ALU.mult, ALU.add)
            dve.drain()
            nc.vector.tensor_tensor(v3(2), L, v3(2), ALU.min)
            dve.drain()
            pick(v3(2), 3, 1, 1)
            nc.vector.tensor_tensor(col(2), col(3), col(0), ALU.subtract).then_inc(F1["gap"], 1)
            dve.wait_ge(F1["egap"], 1)
            nc.vector.tensor_scalar(col(0), col(2), 1.0, None, ALU.add)
            dve.drain()
            nc.vector.reciprocal(col(0), col(0))
            dve.drain()
            nc.vector.tensor_scalar(col(0), col(0), LORA_SCALE, None, ALU.mult)
            dve.drain()
            nc.vector.tensor_tensor(col(2), col(2), col(0), ALU.mult)
            dve.drain()
            nc.vector.tensor_tensor(v3(0), v3(0), bc(0), ALU.mult)
            nc.vector.tensor_tensor(v3(1), v3(1), bc(2), ALU.mult)
            dve.drain()
            nc.vector.tensor_tensor(tk(0), tk(0), tk(1), ALU.add)
            dve.drain()
            for t in range(T):
                h = G3[:, t, NE:NE + ER].rearrange("p (e r) -> p e r", r=RANK)
                i = nc.vector.tensor_tensor(h, h, v3(0)[:, t, :].unsqueeze(2).to_broadcast([P, NE, RANK]), ALU.mult)
            i.then_inc(F1["h_ready"], 1)
            dve_sum(dve, F1, 1, 1, (2, 3, 4, 5))

        CB = AR[0:SK, 0:B * D]
        KT2 = AR[:, B * D:B * D + C * B * SK]
        BK = AR[0:1, 3072:3072 + B * SK]

        def sp_a2(sp):
            sp.wait_ge(F1["split"], 1)
            sp.dma_start(WR[:, 0:2048], l2k_d).then_inc(A2["k_in"], 16)
            sp.wait_ge(F1["mm"], T)
            sp.dma_start(CB, ctxB_d.rearrange("k b n -> k (b n)")).then_inc(A2["b_in"], 16)
            sp.dma_start(OR[:], l2q_d).then_inc(A2["q_in"], 16)

        def pe_a2(pe):
            pe.wait_ge(A2["k_in"], 16)
            pe.wait_ge(F1["acc"], T)
            for dc in range(C):
                for c in range(C):
                    i = nc.tensor.matmul(bank(2 + dc // 2)[:, (dc % 2) * 256:(dc % 2 + 1) * 256],
                                         WR[:, c * D + dc * P:c * D + (dc + 1) * P], CT[:, c, :],
                                         start=c == 0, stop=c == C - 1)
            i.then_inc(A2["k_mm"], 1)
            pe.wait_ge(A2["kt_ready"], 1)
            pe.wait_ge(A2["q_in"], 16)
            for ic in range(C):
                for dc in range(C):
                    nc.tensor.matmul(bank(4 + ic // 2)[:, (ic % 2) * 256:(ic % 2 + 1) * 256],
                                     OR[:, dc * D + ic * P:dc * D + (ic + 1) * P],
                                     KT2[:, dc * 256:(dc + 1) * 256], start=dc == 0, stop=dc == C - 1)
            for dc in range(C):
                i = nc.tensor.matmul(bank(6)[0:1, 0:256], b2[:, dc:dc + 1], KT2[:, dc * 256:(dc + 1) * 256],
                                     start=dc == 0, stop=dc == C - 1)
            i.then_inc(A2["m_mm"], 1)
            pe_norm(pe, 4)
            pe.wait_ge(A2["mlo"], 1)
            for t in range(T):
                tok = slice(t * P, (t + 1) * P)
                o = bank(7)[:, t * SK:(t + 1) * SK]
                b = t // 2
                nc.tensor.matmul(o, ones[0:1, :], BK[:, b * SK:(b + 1) * SK], start=True, stop=False)
                for c in range(C):
                    m = slice(c * 256 + b * SK, c * 256 + (b + 1) * SK)
                    i = mm3(o, HTh[:, c, tok], HTl[:, c, tok], OTh[:, m], OTl[:, m], False, c == C - 1)
            i.then_inc(A2["s_mm"], 1)
            pe.wait_ge(A2["probs"], 1)
            for t in range(T):
                i = nc.tensor.transpose(bank(2 + t // 4)[0:SK, (t % 4) * P:(t % 4 + 1) * P],
                                        s_sb[:, 0, t * SK:(t + 1) * SK], ident[:])
            i.then_inc(A2["t_mm"], 1)
            pe.wait_ge(A2["pt_ready"], 1)
            pe.wait_ge(A2["b_in"], 16)
            for t in range(T):
                if t >= 2:
                    pe.wait_ge(A2["acc"], t - 1)
                b = t // 2
                nc.tensor.matmul(bank(4 + t % 2), PT[0:SK, t * P:(t + 1) * P], CB[:, b * D:(b + 1) * D],
                                 start=True, stop=True).then_inc(A2["mm"], 1)

        def act_a2(act):
            act.wait_ge(A2["k_mm"], 1)
            act.wait_ge(F1["mm"], T)
            for dc in range(C):
                i = nc.scalar.activation(KT2[:, dc * 256:(dc + 1) * 256],
                                         bank(2 + dc // 2)[:, (dc % 2) * 256:(dc % 2 + 1) * 256], ACT.Identity,
                                         bias=b2[:, C + dc:C + dc + 1])
            i.then_inc(A2["kt_ready"], 1)
            act.wait_ge(A2["m_mm"], 1)
            nc.scalar.copy(BK, bank(6)[0:1, 0:256])
            nc.scalar.copy(OTh[:], bank(4, 2)).then_inc(A2["mhi"], 1)
            act_norm(act, 4)
            act.wait_ge(A2["shifted"], 1)
            nc.scalar.activation(s_sb[:, 0, 0:512], s_sb[:, 0, 0:512], ACT.Exp, scale=float(D) ** -0.5)\
                .then_inc(A2["exps"], 1)
            act.wait_ge(A2["t_mm"], 1)
            nc.scalar.copy(PT[0:SK, :], bank(2, 2)[0:SK, :]).then_inc(A2["pt_ready"], 1)

        def dve_a2(dve):
            dve.wait_ge(A2["mhi"], 1)
            nc.vector.tensor_tensor(OTl[:], bank(4, 2), OTh[:].bitcast(F32), ALU.subtract).then_inc(A2["mlo"], 1)
            dve_norm(dve, 4)
            dve.wait_ge(A2["s_mm"], 1)
            softmax_shift(dve, s_sb[:, 0, 0:512], bank(7), T, SK, sm[:, 1, :]).then_inc(A2["shifted"], 1)
            dve.wait_ge(A2["exps"], 1)
            softmax_norm(dve, s_sb[:, 0, 0:512], T, SK, sm[:, 2, :]).then_inc(A2["probs"], 1)
            dve_sum(dve, A2, 2, 0, (4, 5))

        HW = 3 * D

        def sp_f2(sp):
            def load(f, par):
                at = par * HW
                nc_sem = F2["in0"] if par == 0 else F2["in1"]
                for k in range(2):
                    sp.dma_start(WR[:, at + k * D:at + (k + 1) * D], scratch[:, k, bass.ds(f * D, D)])\
                        .then_inc(nc_sem, 16)
                w3v = WR[:, at + 2 * D:at + 3 * D].rearrange("p (r h) -> p r h", r=4)
                for r in range(4):
                    sp.dma_start(w3v[:, r, :], scratch[:, 2, bass.ds(f * P + r * HF, P)]).then_inc(nc_sem, 16)
            sp.wait_ge(A["nf_stored"], 16 * NG)
            sp.wait_ge(A2["k_mm"], 1)
            load(0, 0)
            load(1, 1)
            with sp.Fori(0, 4) as k:
                for par in range(2):
                    f = k * 2 + (par + 2)
                    sp.wait_ge(F2["t_mm"], f * 3 - 3)
                    load(f, par)
            sp.wait_ge(F2["t_mm"], 3 * (NF - 2))
            load(NF - 1, 0)

        def pe_f2(pe):
            def turn_w(f, par, first=False):
                pe.wait_ge(F2["in0"] if par == 0 else F2["in1"], f * 48 + (96 - 48 * par))
                for k in range(3):
                    if k == 0 and not first:
                        pe.wait_ge(F2["wlo"], f * 3)
                    if k == 2:
                        pe.wait_ge(F2["wlo"], f * 3 + 1)
                    for c in range(C):
                        at = par * HW + k * D + c * P
                        i = nc.tensor.transpose(bank(5 + k % 2)[:, c * P:(c + 1) * P], WR[:, at:at + P], ident[:])
                    i.then_inc(F2["t_mm"], 1)

            def gate_up(f, par, first=False):
                pe.wait_ge(F2["wlo"], f * 3 + 2)
                if not first:
                    pe.wait_ge(F2["act"], f)
                for k in range(2):
                    for th in range(2):
                        for c in range(C):
                            w = slice(par * HW + k * D + c * P, par * HW + k * D + (c + 1) * P)
                            tok = slice(th * 512, (th + 1) * 512)
                            i = mm3(bank(2 * k + th), Wh[:, w], Wl[:, w], HTh[:, c, tok], HTl[:, c, tok],
                                    c == 0, c == C - 1)
                    i.then_inc(F2["g_mm" if k == 0 else "u_mm"], 1)

            def down(f, par):
                pe.wait_ge(F2["alo"], f + 1)
                pe.wait_ge(F2["wlo"], f * 3 + 3)
                w = slice(par * HW + 2 * D, (par + 1) * HW)
                for t in range(T):
                    pe.wait_ge(F2["acc"], f * T + (t + 1))
                    tok = slice(par * 1024 + t * P, par * 1024 + (t + 1) * P)
                    mm3(bank(7 if t % 2 == 0 else 4), Oh[:, tok], Ol[:, tok], Wh[:, w], Wl[:, w], True, True)\
                        .then_inc(F2["mm"], 1)
            pe.wait_ge(A2["acc"], T)
            turn_w(0, 0, True)
            turn_w(1, 1)
            pe_norm(pe, 5)
            gate_up(0, 0, True)
            with pe.Fori(0, 4) as k:
                for par in range(2):
                    f = k * 2 + par
                    gate_up(f + 1, 1 - par)
                    down(f, par)
                    turn_w(f + 2, par)
            gate_up(NF - 2, 1)
            down(NF - 3, 0)
            turn_w(NF - 1, 0)
            gate_up(NF - 1, 0)
            down(NF - 2, 1)
            down(NF - 1, 0)

        def w_parts(par, k):
            v = [t_[:, par * HW + k * D:par * HW + (k + 1) * D] for t_ in (Wh, Wl)]
            if k < 2:
                return v
            return [x.rearrange("p (q r) -> p r q", r=4) for x in v]

        def w_bank(k):
            return bank(5 + k % 2) if k < 2 else bank(5).rearrange("p (r q) -> p r q", r=4)

        def act_f2(act):
            def high(f, par):
                for k in range(3):
                    act.wait_ge(F2["t_mm"], f * 3 + (k + 1))
                    nc.scalar.copy(w_parts(par, k)[0], w_bank(k)).then_inc(F2["whi"], 1)

            def silu(f, par):
                act.wait_ge(F2["g_mm"], f + 1)
                nc.scalar.activation(s_sb[:, 0, :], bank(0, 2), ACT.Silu).then_inc(F2["silu"], 1)
                act.wait_ge(F2["act"], f + 1)
                nc.scalar.copy(Oh[:, par * 1024:(par + 1) * 1024], s_sb[:, 1, :]).then_inc(F2["ahi"], 1)
            silu(0, 0)
            with act.Fori(0, 4) as k:
                for par in range(2):
                    f = k * 2 + par
                    silu(f + 1, 1 - par)
                    high(f + 2, par)
            silu(NF - 2, 1)
            high(NF - 1, 0)
            silu(NF - 1, 0)

        def act_f2_first(act):
            for f in range(2):
                for k in range(3):
                    act.wait_ge(F2["t_mm"], f * 3 + k + 1)
                    nc.scalar.copy(w_parts(f, k)[0], w_bank(k)).then_inc(F2["whi"], 1)

        def dve_f2(dve):
            def low(f, par):
                for k in range(3):
                    dve.wait_ge(F2["whi"], f * 3 + (k + 1))
                    hi, lo = w_parts(par, k)
                    nc.vector.tensor_tensor(lo, w_bank(k), hi.bitcast(F32), ALU.subtract).then_inc(F2["wlo"], 1)

            def product(f):
                dve.drain()
                dve.wait_ge(F2["silu"], f + 1)
                dve.wait_ge(F2["u_mm"], f + 1)
                nc.vector.tensor_tensor(s_sb[:, 1, :], bank(2, 2), s_sb[:, 0, :], ALU.mult).then_inc(F2["act"], 1)

            def low_act(f, par):
                dve.wait_ge(F2["ahi"], f + 1)
                cols = slice(par * 1024, (par + 1) * 1024)
                nc.vector.tensor_tensor(Ol[:, cols], s_sb[:, 1, :], Oh[:, cols].bitcast(F32), ALU.subtract)\
                    .then_inc(F2["alo"], 1)

            def add(f, ts):
                for t in ts:
                    dve.wait_ge(F2["mm"], f * T + (t + 1))
                    nc.vector.scalar_tensor_tensor(X[:, t, :], bank(7 if t % 2 == 0 else 4), tg[:, 1, 2:3],
                                                   X[:, t, :], ALU.mult, ALU.add).then_inc(F2["acc"], 1)
            low(0, 0)
            low(1, 1)
            dve.drain().then_inc(F2["acc"], 1)
            dve.drain().then_inc(F2["acc"], 1)
            dve_norm(dve, 5)
            product(0)
            low_act(0, 0)

            def step(f, par, more):
                if more:
                    product(f + 1)
                add(f, range(0, 4))
                if more:
                    low_act(f + 1, 1 - par)
                add(f, range(4, 8))
            with dve.Fori(0, 4) as k:
                for par in range(2):
                    f = k * 2 + par
                    step(f, par, True)
                    low(f + 2, par)
                dve.drain()
            step(NF - 3, 0, True)
            low(NF - 1, 0)
            step(NF - 2, 1, True)
            step(NF - 1, 0, False)

        def at3(lo, n):
            return AR[:, lo:lo + n]
        NM = NS * NS
        LG = at3(4096, T * NL)
        Z = at3(4352, T * NM)
        K3 = at3(4480, T * NM)
        TM = at3(4608, T * NM)
        PP = at3(4736, T * 2 * NS)
        RR = at3(4800, T * NS)
        CC = at3(4832, T * NS)
        MX = at3(4864, T * 2 * NS)
        SG = at3(4928, 4)
        XP = at3(5120, T * P)
        WB = at3(6144, P)

        def sp_f3(sp):
            sp.wait_ge(A["w_split"], 2 * NG)
            sp.wait_ge(A["acc"], 16 * NG + 1)
            sp.dma_start(WR[:, 0:C * NL], w24_d).then_inc(F3["w_in"], 16)
            sp.dma_start(WB, wbr_d).then_inc(F3["w_in"], 16)

        def pool_f3(pool):
            pool_norm(pool, 7)

        def pe_f3(pe):
            pe_norm(pe, 7)
            pe.wait_ge(F3["wlo"], 1)
            for t in range(T):
                tok = slice(t * P, (t + 1) * P)
                for c in range(C):
                    w = slice(c * NL, (c + 1) * NL)
                    i = mm3(bank(7)[:, t * NL:(t + 1) * NL], HTh[:, c, tok], HTl[:, c, tok], Wh[:, w], Wl[:, w],
                            c == 0, c == C - 1)
            i.then_inc(F3["lg_mm"], 1)
            pe.wait_ge(F3["pre"], 1)
            for t in range(T):
                i = nc.tensor.transpose(bank(2, 2)[:, t * P:(t + 1) * P], XP[:, t * P:(t + 1) * P], ident[:])
            i.then_inc(F3["preT_mm"], 1)
            pe.wait_ge(F3["preT"], 1)
            for t in range(T):
                i = nc.tensor.matmul(bank(4, 2)[:, t * P:(t + 1) * P], PT[:, t * P:(t + 1) * P], WB,
                                     start=True, stop=True)
            i.then_inc(F3["y_mm"], 1)

        def act_f3(act):
            act.wait_ge(F3["w_in"], 32)
            nc.scalar.copy(Wh[:, 0:C * NL], WR[:, 0:C * NL]).then_inc(F3["w_hi"], 1)
            act_norm(act, 7)
            asked = [0]

            def run(out, in_, f, **kw):
                asked[0] += 1
                act.wait_ge(F3["to_act"], asked[0])
                nc.scalar.activation(out, in_, f, **kw).then_inc(F3["from_act"], 1)
            run(PP, PP, ACT.Exp)
            run(SG[:, 0:1], gate[:], ACT.Exp, scale=-1.0)
            for _ in range(2):
                run(K3, Z, ACT.Exp)
                run(MX[:, 0:T * NS], MX[:, 0:T * NS], ACT.Ln)
            run(K3, Z, ACT.Exp)
            act.wait_ge(F3["preT_mm"], 1)
            nc.scalar.copy(PT[:], bank(2, 2)).then_inc(F3["preT"], 1)
            run(AR[:, 4800:4864], AR[:, 4800:4864], ACT.Ln)
            run(K3, Z, ACT.Exp)

        def dve_f3(dve):
            dve.wait_ge(F3["w_hi"], 1)
            nc.vector.tensor_tensor(Wl[:, 0:C * NL], WR[:, 0:C * NL], Wh[:, 0:C * NL].bitcast(F32), ALU.subtract)\
                .then_inc(F3["wlo"], 1)
            dve_norm(dve, 7)
            dve.wait_ge(F3["lg_mm"], 1)
            asked = [0]

            def ask(i):
                asked[0] += 1
                i.then_inc(F3["to_act"], 1)

            def answered():
                dve.wait_ge(F3["from_act"], asked[0])
            LG3 = LG.rearrange("p (t n) -> p t n", t=T)
            nc.vector.tensor_tensor(LG3, bank(7)[:, 0:T * NL].rearrange("p (t n) -> p t n", t=T),
                                    rms[:].unsqueeze(2).to_broadcast([P, T, NL]), ALU.mult)
            dve.drain()
            nc.vector.tensor_tensor(LG3, LG3, bases[:].unsqueeze(1).to_broadcast([P, T, NL]), ALU.add)
            dve.drain()
            Z4 = Z.rearrange("p (t i j) -> p t i j", t=T, i=NS)
            K4 = K3.rearrange("p (t i j) -> p t i j", t=T, i=NS)
            T4 = TM.rearrange("p (t i j) -> p t i j", t=T, i=NS)
            nc.vector.tensor_scalar(Z.rearrange("p (t n) -> p t n", t=T), LG3[:, :, 0:NM], 10.0, None, ALU.mult)
            nc.vector.tensor_copy(PP.rearrange("p (t n) -> p t n", t=T), LG3[:, :, NM:NL])
            dve.drain()
            ask(softmax_shift(dve, PP, PP, 2 * T, NS, MX))
            dve.drain()

            def view(x, rows):
                return x if rows else x.rearrange("p t i j -> p t j i")

            def spread(v, rows):
                v = v.rearrange("p (t n) -> p t n", t=T)
                return (v.unsqueeze(3) if rows else v.unsqueeze(2)).to_broadcast([P, T, NS, NS])
            asked[0] += 1
            nc.vector.tensor_copy(SG[:, 1:2], gate[:]).then_inc(F3["to_act"], 1)
            for rows in (True, False):
                M = MX[:, 0:T * NS]
                nc.vector.tensor_reduce(M, view(Z4, rows), AX.X, ALU.max)
                dve.drain()
                ask(nc.vector.tensor_tensor(Z4, Z4, spread(M, rows), ALU.subtract))
                answered()
                ask(nc.vector.tensor_reduce(M, view(K4, rows), AX.X, ALU.add))
                answered()
                i = nc.vector.tensor_tensor(Z4, Z4, spread(M, rows), ALU.subtract)
                dve.drain()
            ask(nc.vector.memset(CC, 1.0))
            softmax_norm(dve, PP, 2 * T, NS, MX)
            dve.drain()
            P3 = PP.rearrange("p (t n) -> p t n", t=T)
            for n in range(NS):
                for t in range(T):
                    h = hn_of(7, t)[:, n * P:(n + 1) * P]
                    xp = XP[:, t * P:(t + 1) * P]
                    if n == 0:
                        i = nc.vector.tensor_scalar(xp, h, P3[:, t, n:n + 1], None, ALU.mult)
                    else:
                        i = nc.vector.scalar_tensor_tensor(xp, h, P3[:, t, n:n + 1], xp, ALU.mult, ALU.add)
                dve.drain()
            dve.drain().then_inc(F3["pre"], 1)
            answered()

            def balance():
                for rows, given, got in ((True, CC, RR), (False, RR, CC)):
                    nc.vector.tensor_tensor(T4, K4, spread(given, not rows), ALU.mult)
                    dve.drain()
                    nc.vector.tensor_reduce(got, view(T4, rows), AX.X, ALU.add)
                    dve.drain()
                    nc.vector.reciprocal(got, got)
                    dve.drain()
            with dve.Fori(0, SK_LINEAR) as _:
                balance()
            ask(dve.drain())
            answered()
            nc.vector.tensor_tensor(Z4, Z4, spread(RR, True), ALU.add)
            dve.drain()
            ask(nc.vector.tensor_tensor(Z4, Z4, spread(CC, False), ALU.add))
            answered()
            dve.drain()
            nc.vector.memset(CC, 1.0)
            dve.drain()
            with dve.Fori(0, SK_LINEAR + 1) as _:
                balance()
            nc.vector.tensor_tensor(K4, K4, spread(RR, True), ALU.mult)
            nc.vector.tensor_scalar(SG[:, 0:1], SG[:, 0:1], 1.0, None, ALU.add)
            dve.drain()
            nc.vector.tensor_tensor(K4, K4, spread(CC, False), ALU.mult)
            nc.vector.reciprocal(SG[:, 0:1], SG[:, 0:1])
            dve.drain()
            nc.vector.tensor_tensor(SG[:, 1:2], SG[:, 0:1], tg[:, 1, 3:4], ALU.mult)
            dve.drain()
            nc.vector.tensor_tensor(SG[:, 2:3], tg[:, 1, 3:4], SG[:, 1:2], ALU.subtract)
            nc.vector.tensor_scalar(K3, K3, SG[:, 1:2], None, ALU.mult)
            nc.vector.tensor_scalar(PP, PP, tg[:, 1, 3:4], None, ALU.mult)
            dve.drain()
            diag = K3.rearrange("p (t n) -> p t n", t=T)[:, :, 0:NM:NS + 1]
            nc.vector.tensor_scalar(diag, diag, SG[:, 2:3], None, ALU.add)
            dve.wait_ge(F3["y_mm"], 1)
            dve.drain()
            H3 = K3.rearrange("p (t n) -> p t n", t=T)
            for t in range(T):
                for j in range(NS + 1):
                    for i_ in range(NS):
                        xt = X[:, t, i_ * P:(i_ + 1) * P]
                        src = bank(4, 2)[:, t * P:(t + 1) * P] if j == NS else hn_of(7, t)[:, j * P:(j + 1) * P]
                        w = P3[:, t, NS + i_:NS + i_ + 1] if j == NS else H3[:, t, i_ * NS + j:i_ * NS + j + 1]
                        i = nc.vector.scalar_tensor_tensor(xt, src, w, xt, ALU.mult, ALU.add)
                    dve.drain()
                dve.drain().then_inc(F3["done"], 1)

        CONSTS = 16 * 8

        @block.sync
        def _(sp):
            sp.dma_start(X[:], x_d.rearrange("(t p) n -> p t n", p=P)).then_inc(x_in, 16)
            sp.dma_start(CT[:], ctxT_d).then_inc(ctx_in, 16)
            sp.dma_start(gates[:, 0, :], gx_d.to_broadcast([P, 4])).then_inc(consts_in, 16)
            sp.dma_start(gates[:, 1, :], gf_d.to_broadcast([P, 4])).then_inc(consts_in, 16)
            sp.dma_start(lnw[:], lnw_d.to_broadcast([P, D])).then_inc(consts_in, 16)
            sp.dma_start(qkn[:], qkn_d).then_inc(consts_in, 16)
            sp.dma_start(b2[:], b2_d).then_inc(consts_in, 16)
            sp.dma_start(iot[:], iota_d.to_broadcast([P, NE])).then_inc(consts_in, 16)
            sp.dma_start(bases[:], bases_d.to_broadcast([P, NL])).then_inc(consts_in, 16)
            sp.dma_start(gate[:], gate_d.to_broadcast([P, 1])).then_inc(consts_in, 16)
            sp_attention(sp, A, True)
            sp_f0(sp)
            sp_a1(sp)
            sp_f1(sp)
            sp_a2(sp)
            sp_f2(sp)
            sp_attention(sp, A, False)
            sp_f3(sp)
            sp.wait_ge(F3["done"], T)
            for t in range(T):
                sp.dma_start(out_d[t * P:(t + 1) * P, :], X[:, t, :]).then_inc(out_stored, 16)
            sp.wait_ge(out_stored, 16 * T)

        @block.gpsimd
        def _(pool):
            nc.gpsimd.memset(ident[:], 0.0)
            nc.gpsimd.memset(ones[:], 1.0)
            nc.gpsimd.memset(half[:], -0.5)
            nc.gpsimd.memset(tiny[:, 0:8], EPS)
            nc.gpsimd.memset(tiny[:, 8:16], EPS * DH)
            nc.gpsimd.memset(hm[:], 1.0)
            pool.drain()
            nc.gpsimd.affine_select(out=ident[:], in_=ident[:], compare_op=ALU.not_equal, fill=1.0, base=0,
                                    pattern=[[-1, P]], channel_multiplier=1)
            nc.gpsimd.affine_select(out=hm[:], in_=hm[:], compare_op=ALU.is_ge, fill=0.0, base=0,
                                    pattern=[[-DH1, HC1]], channel_multiplier=1)
            pool.drain()
            nc.gpsimd.affine_select(out=hm[:], in_=hm[:], compare_op=ALU.is_ge, fill=0.0, base=DH1 - 1,
                                    pattern=[[DH1, HC1]], channel_multiplier=-1)
            pool.drain().then_inc(pool_consts, 1)
            pool.wait_ge(ctx_hi, 1)
            pool_low(CTh[:], CTl[:], CT[:]).then_inc(ctx_split, 1)
            pool_norm(pool, 0)
            pool_attention(pool, A, True)
            pool_norm(pool, 1)
            pool.wait_ge(F0["w_hi"], 1)
            pool_low(Oh[:], Ol[:], OR[:]).then_inc(F0["split"], 1)
            pool_a1(pool)
            pool_f1(pool)
            pool_norm(pool, 4)
            pool_norm(pool, 5)
            pool_attention(pool, A, False)
            pool_f3(pool)

        @block.scalar
        def _(act):
            act.wait_ge(consts_in, CONSTS)
            nc.scalar.activation(tg[:], gates[:], ACT.Tanh).then_inc(gates_ready, 1)
            act.wait_ge(ctx_in, 16)
            nc.scalar.copy(CTh[:], CT[:]).then_inc(ctx_hi, 1)
            act_norm(act, 0)
            act_attention(act, A, True)
            act_norm(act, 1)
            act.wait_ge(F0["packed"], 1)
            nc.scalar.copy(Oh[:], OR[:]).then_inc(F0["w_hi"], 1)
            act_a1(act)
            act_f1(act)
            act_a2(act)
            act_f2_first(act)
            act_norm(act, 5)
            act_f2(act)
            act_attention(act, A, False)
            act_f3(act)

        @block.tensor
        def _(pe):
            pe_norm(pe, 0)
            pe.wait_ge(ctx_split, 1)
            pe_attention(pe, A, True)
            pe_norm(pe, 1)
            pe_f0(pe)
            pe_a1(pe)
            pe_f1(pe)
            pe_a2(pe)
            pe_f2(pe)
            pe_norm(pe, 6)
            pe_attention(pe, A, False)
            pe_f3(pe)

        @block.vector
        def _(dve):
            dve_norm(dve, 0)
            dve.wait_ge(gates_ready, 1)
            dve_attention(dve, A, True)
            dve_norm(dve, 1)
            dve_f0_dequant(dve)
            dve_sum(dve, F0, 0, 1, (2, 3, 4, 5))
            dve_a1(dve)
            dve_f1(dve)
            dve_a2(dve)
            dve_f2(dve)
            dve_norm(dve, 6)
            dve_attention(dve, A, False)
            dve_f3(dve)


def lay_out(i):
    f = {k: np.asarray(v) for k, v in i.items()}

    def chunks(w):
        return w.reshape(C, P, -1).transpose(1, 0, 2)

    def group(wq, wk, wv):
        g = [np.concatenate([wq[:, k * WQ:(k + 1) * WQ], wk[:, k * DH:(k + 1) * DH], wv[:, k * DH:(k + 1) * DH]], 1)
             for k in range(NG)]
        return np.stack([chunks(w).reshape(P, -1) for w in g])

    def rows(wo):
        return wo.reshape(NG, HG, DH, D).transpose(0, 2, 1, 3).reshape(NG, P, -1)

    ctxf = f['ctx_4096'].reshape(B * SK, D)
    w1, w2 = (np.concatenate([f[f'L2_ffn_{k}'], np.zeros((NF * P - HF, D), np.float32)])
              .reshape(NF, P, D).transpose(1, 0, 2).reshape(P, NG, NBU * QB) for k in ('w1', 'w2'))
    w3 = np.concatenate([f['L2_ffn_w3'].reshape(P, NB3 * QB), np.zeros((P, NFW - NB3 * QB), np.float32)], 1)\
        .reshape(P, NG, NBU * QB)
    kr = f['L1_xattn_wk'].reshape(NKV1, DH1, D)
    kr = np.stack([np.concatenate([kr[2 * c + h // 4] for h in range(HC1)]) for c in range(C)])
    packed = f['L0_ffn_W_q'].reshape(D // 2, D).T

    def groups(z):
        return z.reshape(D, C, 2).transpose(2, 1, 0).reshape(2, -1)
    out = {
        'x': f['x'].reshape(B * S, D),
        'ctxT': chunks(ctxf.T),
        'ctxB': f['ctx_4096'].transpose(1, 0, 2),
        'gx': f['g_xattn'].reshape(1, 4), 'gf': f['g_ffn'].reshape(1, 4),
        'wl': np.concatenate([group(f['L0_xattn_wq'], f['L0_xattn_wk'], f['L0_xattn_wv']),
                        group(f['L3_xattn_q_proj_w'].T, f['L3_xattn_k_proj_w'].T, f['L3_xattn_v_proj_w'].T)]),
        'ol': np.concatenate([rows(f['L0_xattn_wo']), rows(f['L3_xattn_o_proj_w'].T)]),
        'w4': np.ascontiguousarray(chunks(packed).reshape(P, -1)).view(np.int32),
        'sc4': groups(f['L0_ffn_scale']), 'ze4': groups(f['L0_ffn_zero']),
        'l1wqv': np.concatenate([chunks(f['L1_xattn_wq'].T).reshape(P, -1), chunks(f['L1_xattn_wv'].T).reshape(P, -1)], 1),
        'l1kr': chunks(kr.reshape(C * P, D).T).reshape(P, -1),
        'l1o': chunks(f['L1_xattn_wo'].T).reshape(P, -1),
        'lnw': f['L1_xattn_ln_w'].reshape(1, D),
        'l1f': chunks(np.concatenate([f['L1_ffn_base_W'], f['L1_ffn_gate_W'], f['L1_ffn_lora_A'].reshape(ER, D)]).T)
        .reshape(P, -1),
        'lb': f['L1_ffn_lora_B'].transpose(0, 2, 1).reshape(2, EH, D).transpose(1, 0, 2).reshape(EH, -1),
        'l2k': chunks(f['L2_xattn_Wk'].T).reshape(P, -1), 'l2q': chunks(f['L2_xattn_Wq']).reshape(P, -1),
        'b2': np.stack([f['L2_xattn_bq'].reshape(C, P).T, f['L2_xattn_bk'].reshape(C, P).T], 1).reshape(P, -1),
        'nf': np.stack([w1, w2, w3], 2).transpose(1, 0, 2, 3).reshape(NG, P, NBT * QB),
        'qkn': np.stack([f['L3_xattn_q_norm_w'], f['L3_xattn_k_norm_w']], 1),
        'mask': f['mask_1x1xSxS2_ff0'].reshape(2, P, SK).transpose(1, 0, 2).reshape(P, -1),
        'iota': (np.arange(NE, dtype=np.float32) - BIG_INDEX).reshape(1, NE).astype(np.float32),
        'w24': chunks(np.concatenate([f['L3_ffn_W_res'], f['L3_ffn_W_pre'], f['L3_ffn_W_post']]).T).reshape(P, -1),
        'bases': np.concatenate([f['L3_ffn_H_res_base'].reshape(-1), f['L3_ffn_H_pre_base'],
                                 f['L3_ffn_H_post_base']]).reshape(1, NL),
        'gate': f['L3_ffn_gate'].reshape(1, 1),
        'wbr': f['L3_ffn_W_branch'],
    }
    return {k: np.ascontiguousarray(v) for k, v in out.items()}


def kernel(**inputs):
    import concourse.bacc as _bacc
    from concourse import mybir as _mybir
    from concourse.bass_utils import run_bass_kernel_spmd as _run

    nc = _bacc.Bacc("TRN2", target_bir_lowering=False, num_devices=1)
    arrays, args = {}, []
    for name, a in lay_out(inputs).items():
        arrays[f"in_{name}"] = a
        args.append(nc.dram_tensor(f"in_{name}", a.shape, _mybir.dt.from_np(a.dtype), kind="ExternalInput").ap())
    out = nc.dram_tensor("out", (B * S, D), _mybir.dt.float32, kind="ExternalOutput").ap()
    build(nc, *args, out)
    r = _run(nc, [arrays], core_ids=[0])
    return r.results[0]["out"].reshape(B, S, D)
```

```python
import concourse.bass as bass
from concourse import mybir
from contextlib import ExitStack
import numpy as np

F32 = mybir.dt.float32
F32R = mybir.dt.float32r
U8 = mybir.dt.uint8
BF16 = mybir.dt.bfloat16
ALU = mybir.AluOpType
ACT = mybir.ActivationFunctionType
AX = mybir.AxisListType

P = 128
B, S, D = 4, 256, 512
SK = 64
T = B * S // P
C = D // P
NG, HG, DH = 8, 4, 128
HS = HG // 2
WQ = HG * DH
WG = WQ + 2 * DH
NH1, DH1, NKV1 = 32, 16, 8
HC1 = P // DH1
NE, RANK = 28, 8
ER = NE * RANK
EH = ER // 2
LORA_SCALE = 2.0
HF = 1376
NF = -(-HF // P)
QB = 64
NB3 = D * HF // P // QB
NBU = NF * D // QB // NG
NBT = 3 * NBU
NFW = NF * D
NS = 4
NL = NS * NS + 2 * NS
SK_LINEAR = 24
EPS = 1e-5
EPS_RMS = 1.1920929e-07
BIG_INDEX = 1024.0
HALF_MAX = 1.7e38

CODE = [np.float32(v) for v in (
    -1.0, -0.6961928009986877, -0.5250730514526367, -0.39491748809814453, -0.28444138169288635,
    -0.18477343022823334, -0.09105003625154495, 0.0, 0.07958029955625534, 0.16093020141124725,
    0.24611230194568634, 0.33791524171829224, 0.44070982933044434, 0.5626170039176941,
    0.7229568362236023, 1.0)]
_BOUNDS = [float(np.float32((lo + hi) * np.float32(0.5))) for lo, hi in zip(CODE, CODE[1:])]
UP = [(_BOUNDS[i], float(np.float32(CODE[i + 1] - CODE[i]))) for i in range(7, 15)]
DOWN = [(_BOUNDS[i], float(np.float32(CODE[i] - CODE[i + 1]))) for i in range(6, -1, -1)]
FAR = 2.0 ** 100


def build(nc, x_d, ctxT_d, ctxB_d, gx_d, gf_d, wl_d, ol_d, w4_d, sc4_d, ze4_d, l1wqv_d, l1kr_d, l1o_d,
          lnw_d, l1f_d, lb_d, l2k_d, l2q_d, b2_d, nf_d, qkn_d, mask_d, iota_d, w24_d, bases_d, gate_d, wbr_d, out_d):
    scratch = nc.dram_tensor("dequantised", [P, 3, NFW], F32, kind="Internal").ap()
    ctx = ExitStack()
    with ctx:
        def sb(name, shape, dt=F32):
            return ctx.enter_context(nc.sbuf_tensor(name, shape, dt))

        def sem(name):
            return ctx.enter_context(nc.semaphore(name))

        X = sb("X", [P, T, D])
        HN = sb("HN", [P, 2, D])
        HTh = sb("HTh", [P, C, T * P], F32R)
        HTl = sb("HTl", [P, C, T * P], F32R)
        CT = sb("CT", [P, C, B * SK])
        CTh = sb("CTh", [P, C, B * SK], F32R)
        CTl = sb("CTl", [P, C, B * SK], F32R)
        ident = sb("ident", [P, P])
        ones = sb("ones", [P, P])
        gates = sb("gates", [P, 2, 4])
        tg = sb("tg", [P, 2, 4])
        st = sb("st", [P, T, 6])
        mv = sb("mv", [P, T, 2])
        veps = sb("veps", [P, 2, T])
        rstd = sb("rstd", [P, T])
        rms = sb("rms", [P, T])
        half = sb("half", [P, T])
        sm = sb("sm", [P, 4, 32])
        qkn = sb("qkn", [P, 2])
        qkw = sb("qkw", [P, 1])
        lnw = sb("lnw", [P, D])
        WR = sb("WR", [P, C * WG])
        Wh = sb("Wh", [P, C * WG], F32R)
        Wl = sb("Wl", [P, C * WG], F32R)
        OR = sb("OR", [P, 4 * D])
        Oh = sb("Oh", [P, 4 * D], F32R)
        Ol = sb("Ol", [P, 4 * D], F32R)
        qT = sb("qT", [P, 2, HG * S])
        s_sb = sb("s_sb", [P, 2, 2 * D])
        PT = sb("PT", [P, 2 * D])
        OTh = sb("OTh", [P, HG * S], F32R)
        OTl = sb("OTl", [P, HG * S], F32R)
        v_sb = sb("v_sb", [P, B, DH])
        kT = sb("kT", [P, B * SK])
        kvs = sb("kvs", [P, 2, 2 * DH])
        AR = sb("AR", [P, 5 * NBT * QB + NBT * QB // 2])
        PS = ctx.enter_context(nc.psum_tensor("PS", [P, 8, 512], F32))

        def bank(i, n=1):
            return PS[:, i, :] if n == 1 else PS[:, i:i + n, :].rearrange("p a b -> p (a b)")

        block = ctx.enter_context(nc.Block())

        x_in, consts_in, ctx_in = sem("x_in"), sem("consts_in"), sem("ctx_in")
        pool_consts, gates_ready, ctx_hi, ctx_split = sem("pool_consts"), sem("gates_ready"), sem("ctx_hi"), sem("ctx_split")
        stats, rstd_ready, hn_ready = sem("stats"), sem("rstd_ready"), sem("hn_ready")
        hn_turned, hi_ready, lo_ready = sem("hn_turned"), sem("hi_ready"), sem("lo_ready")
        out_stored = sem("out_stored")

        class Sems:

            def __init__(self, stage, names):
                self.all = {n: sem(f"{stage}_{n}") for n in names.split()}

            def __getitem__(self, n):
                return self.all[n]

        ATT = ("w_in o_in w_hi o_hi w_split o_split kv_mm kn_ready v_ready kt_mm kt_ready q_mm qT_ready s_mm s_read "
               "shifted exps probs t_mm pt_ready pv_mm ohi olo wo_mm acc ksq krs qrs_in qrs "
               "kn_in mask_in nf_in nf_v nf_mask nf_added nf_rise nf_summed nf_out nf_stored nf_free nf_norm")
        A = Sems("att", ATT)
        F0 = Sems("f0", "w_in packed w_hi split mm acc")
        A1 = Sems("a1", "w_in kr_in o_in w_hi o_hi w_split o_split kr_mm kr_out v_out q_mm qT_ready s_mm "
                        "shifted exps probs t_mm pt_ready pv_mm ohi olo wo_mm acc")
        F1 = Sems("f1", "w_in b_in w_hi split lg_mm lg_ready gap egap h_ready t_mm ht_ready mm acc")
        A2 = Sems("a2", "k_in q_in b_in k_mm kt_ready m_mm mhi mlo s_mm shifted exps probs t_mm "
                        "pt_ready mm acc")
        F2 = Sems("f2", "in0 in1 t_mm whi wlo g_mm u_mm silu act ahi alo mm acc")
        F3 = Sems("f3", "w_in w_hi wlo lg_mm to_act from_act pre preT_mm preT y_mm done")

        def mm3(out, ah, al, bh, bl, first, last_):
            nc.tensor.matmul(out, ah, bh, start=first, stop=False)
            nc.tensor.matmul(out, ah, bl, start=False, stop=False)
            return nc.tensor.matmul(out, al, bh, start=False, stop=last_)

        def hn_of(n, t):
            if n == 7:
                return AR[:, t * D:(t + 1) * D]
            return HN[:, t % 2, :]

        def dve_norm(dve, n):
            if n == 0:
                dve.wait_ge(x_in, 16)
            dve.drain()
            for t in range(T):
                nc.vector.bn_stats(st[:, t, :], X[:, t, :])
            dve.drain()
            for t in range(T):
                i = nc.vector.bn_aggr(mv[:, t, :], st[:, t, :])
            i.then_inc(stats, 1)
            dve.wait_ge(rstd_ready, n + 1)
            if n == 2:
                nc.vector.tensor_tensor(rstd[:], rstd[:], rms[:], ALU.mult)
                dve.wait_ge(consts_in, CONSTS)
                dve.drain()

            def low(t):
                dve.wait_ge(hi_ready, T * n + t + 1)
                cols = slice(t * P, (t + 1) * P)
                nc.vector.tensor_tensor(HTl[:, :, cols], bank(t % 2).rearrange("p (c k) -> p c k", c=C),
                                        HTh[:, :, cols].bitcast(F32), ALU.subtract).then_inc(lo_ready, 1)

            for t in range(T):
                if t >= 2 and n != 7:
                    dve.wait_ge(hn_turned, T * n + t - 1)
                i = nc.vector.tensor_scalar(hn_of(n, t), X[:, t, :], mv[:, t, 0:1], rstd[:, t:t + 1],
                                            ALU.subtract, ALU.mult)
                if n == 2:
                    dve.drain()
                    i = nc.vector.tensor_tensor(hn_of(n, t), hn_of(n, t), lnw[:], ALU.mult)
                i.then_inc(hn_ready, 1)
                if t:
                    low(t - 1)
            low(T - 1)

        def pool_norm(pool, n):
            pool.wait_ge(stats, n + 1)
            nc.gpsimd.tensor_scalar(veps[:, 0, :], mv[:, :, 1], EPS, None, ALU.add)
            pool.drain()
            i = nc.gpsimd.tensor_tensor(rstd[:], veps[:, 0, :], half[:], ALU.pow)
            if n in (2, 7):
                pool.drain()
                nc.gpsimd.tensor_tensor(veps[:, 1, :], mv[:, :, 1], rstd[:], ALU.mult)
                pool.drain()
                nc.gpsimd.tensor_tensor(veps[:, 1, :], veps[:, 1, :], rstd[:], ALU.mult)
                pool.drain()
                nc.gpsimd.tensor_scalar(veps[:, 1, :], veps[:, 1, :], EPS if n == 2 else EPS_RMS, None, ALU.add)
                pool.drain()
                i = nc.gpsimd.tensor_tensor(rms[:], veps[:, 1, :], half[:], ALU.pow)
            i.then_inc(rstd_ready, 1)

        def pe_norm(pe, n):
            if n == 0:
                pe.wait_ge(pool_consts, 1)
            for t in range(T):
                pe.wait_ge(hn_ready, T * n + t + 1)
                if t >= 2:
                    pe.wait_ge(lo_ready, T * n + t - 1)
                for c in range(C):
                    i = nc.tensor.transpose(bank(t % 2)[:, c * P:(c + 1) * P], hn_of(n, t)[:, c * P:(c + 1) * P],
                                            ident[:])
                i.then_inc(hn_turned, 1)
            pe.wait_ge(lo_ready, T * n + T)

        def act_norm(act, n):
            for t in range(T):
                act.wait_ge(hn_turned, T * n + t + 1)
                nc.scalar.copy(HTh[:, :, t * P:(t + 1) * P], bank(t % 2).rearrange("p (c k) -> p c k", c=C))\
                    .then_inc(hi_ready, 1)

        def w3d(t_, lo, hi_):
            return t_[:].rearrange("p (c n) -> p c n", c=C)[:, :, lo:hi_]

        W_PIECES = ((WQ, WG), (0, 2 * DH), (2 * DH, WQ))
        N_NF = NBT * QB
        nf_in, nf_below, nf_m0, nf_m1, nf_above = (AR[:, k * N_NF:(k + 1) * N_NF] for k in range(5))
        nf_far = AR[:, 5 * N_NF:5 * N_NF + N_NF // 2].bitcast(BF16)
        NUP, NDOWN = len(UP), len(DOWN)

        def sp_attention(sp, a, l0):
            g0 = 0 if l0 else NG

            def load_w(g):
                sp.dma_start(WR[:], wl_d[g]).then_inc(a["w_in"], 16)

            def load_o(g):
                sp.dma_start(OR[:], ol_d[g]).then_inc(a["o_in"], 16)

            def load_nf(g):
                sp.dma_start(nf_in, nf_d[g]).then_inc(a["nf_in"], 16)

            def store(g):
                sp.wait_ge(a["nf_out"], g + 2)
                n = NBU * QB
                sp.dma_start(scratch[:, :, bass.ds(g * n, n)], nf_below.rearrange("p (w n) -> p w n", w=3))\
                    .then_inc(a["nf_stored"], 16)
                sp.wait_ge(a["nf_stored"], g * 16 + 16)
                sp.sem_inc(a["nf_free"], 1)
            if not l0:
                sp.wait_ge(F2["t_mm"], 3 * NF)
            load_w(g0)
            load_o(g0)
            if l0:
                load_nf(0)
                sp.sem_inc(a["nf_free"], 1)
            else:
                sp.dma_start(mask_sb, mask_d).then_inc(a["mask_in"], 16)
            sp.wait_ge(a["w_split"], 3 * g0 + 3)
            load_w(g0 + 1)

            def turn(g, more):
                sp.wait_ge(a["o_split"], g)
                load_o(g)
                if more:
                    sp.wait_ge(a["w_split"], g * 3 + 3)
                    load_w(g + 1)
                if l0:
                    sp.wait_ge(a["nf_norm"], g)
                    load_nf(g)
                    store(g - 1)
            with sp.Fori(g0 + 1, g0 + NG - 1) as g:
                turn(g, True)
            turn(g0 + NG - 1, False)
            if l0:
                store(NG - 1)

        def pool_low(hi, lo, raw):
            return nc.gpsimd.tensor_tensor(lo, raw, hi.bitcast(F32), ALU.subtract)

        def pool_attention(pool, a, l0):
            g0 = 0 if l0 else NG

            def split_w(g):
                for k, (lo, hi_) in enumerate(W_PIECES):
                    pool.wait_ge(a["w_hi"], g * 3 + (k + 1))
                    pool_low(w3d(Wh, lo, hi_), w3d(Wl, lo, hi_), w3d(WR, lo, hi_)).then_inc(a["w_split"], 1)

            def split_o(g):
                pool.wait_ge(a["o_hi"], g + 1)
                pool_low(Oh[:], Ol[:], OR[:]).then_inc(a["o_split"], 1)

            def key_scale(g):
                pool.wait_ge(a["ksq"], g - (NG - 1))
                ks = sm[:, 0, 0:2]
                nc.gpsimd.tensor_tensor(ks, ks, tiny[:, 0:2], ALU.add)
                pool.drain()
                nc.gpsimd.tensor_tensor(sm[:, 0, 2:4], ks, half[:, 0:2], ALU.pow).then_inc(a["krs"], 1)

            def query_scale(g, b):
                pool.wait_ge(a["qrs_in"], g * B + (b + 1 - NG * B))
                qs = sm[:, 0, 8:16]
                nc.gpsimd.tensor_tensor(qs, qs, tiny[:, 8:16], ALU.add)
                pool.drain()
                nc.gpsimd.tensor_tensor(sm[:, 0, 16:24], qs, half[:], ALU.pow).then_inc(a["qrs"], 1)

            def add_below(g, ks):
                for k in ks:
                    pool.wait_ge(a["nf_mask"], g * NDOWN + (k + 1))
                    if k == 1:
                        pool.wait_ge(a["nf_free"], g + 1)
                    nc.gpsimd.tensor_tensor(nf_below, nf_below if k > 1 else nf_m0, nf_m1 if k % 2 else nf_m0,
                                            ALU.add).then_inc(a["nf_added"], 1)
                    pool.drain()

            def nf_finish(g):
                pool.wait_ge(a["nf_summed"], g * NUP + (NUP + 1))
                nc.gpsimd.tensor_tensor(nf_below, nf_below, nf_above, ALU.add)
                pool.drain()
                v = nf_below.rearrange("p (n q) -> p n q", q=QB)
                nc.gpsimd.tensor_tensor(v, v, absmax[:].unsqueeze(2).to_broadcast([P, NBT, QB]),
                                        ALU.mult).then_inc(a["nf_out"], 1)
            if l0:
                pool.drain().then_inc(a["nf_added"], 1)
                pool.drain().then_inc(a["nf_out"], 1)
            split_w(g0)
            if not l0:
                pool_norm(pool, 6)
                key_scale(g0)
            split_o(g0)
            if not l0:
                query_scale(g0, 0)
                query_scale(g0, 1)

            def turn(g, more):
                if not l0:
                    query_scale(g, 2)
                if more:
                    split_w(g + 1)
                if not l0:
                    query_scale(g, 3)
                    if more:
                        key_scale(g + 1)
                        query_scale(g, 4)
                        query_scale(g, 5)
                else:
                    add_below(g, range(1, NDOWN))
                    nf_finish(g)
                if more:
                    split_o(g + 1)
            with pool.Fori(g0, g0 + NG - 1) as g:
                turn(g, True)
            turn(g0 + NG - 1, False)

        tiny = sb("tiny", [P, 16])
        hm = sb("hm", [P, HC1])
        b2 = sb("b2", [P, 2 * C])
        iot = sb("iot", [P, NE])
        bases = sb("bases", [P, NL])
        gate = sb("gate", [P, 1])
        absmax = sb("absmax", [P, NBT])
        absnew = sb("absnew", [P, NBT])
        rabs = sb("rabs", [P, NBT])
        nf_bias = sb("nf_bias", [P, NUP])

        mask_sb = AR[:, 2 * HG * S:2 * HG * S + 2 * SK]

        def pe_attention(pe, a, l0):
            g0 = 0 if l0 else NG

            def project_kv(g):
                pe.wait_ge(a["w_split"], g * 3 + 1)
                for j in range(2):
                    for c in range(C):
                        rows = slice(j * P, (j + 1) * P)
                        i = mm3(bank(4)[:, j * 256:(j + 1) * 256], CTh[:, c, rows], CTl[:, c, rows],
                                w3d(Wh, WQ, WG)[:, c], w3d(Wl, WQ, WG)[:, c], c == 0, c == C - 1)
                i.then_inc(a["kv_mm"], 1)

            def turn_k(g):
                if l0:
                    pe.wait_ge(a["kn_in"], g + 1)
                else:
                    pe.wait_ge(a["kn_ready"], g - (NG - 1))
                pe.wait_ge(a["acc"], g * 2 * B - 3 if not (l0 and isinstance(g, int)) else 1)
                for j in range(2):
                    i = nc.tensor.transpose(bank(7)[:, j * P:(j + 1) * P], kvs[:, j, 0:DH], ident[:])
                i.then_inc(a["kt_mm"], 1)

            def project_q(g, b, first=False):
                u = g * B + b
                for pr in range(HS):
                    if b % B == 0:
                        pe.wait_ge(a["w_split"], (g + b // B) * 3 + (2 + pr))
                    if not first:
                        pe.wait_ge(a["qT_ready"], g * 2 * B + (2 * b - 1 + pr))
                    if not l0 and pr == 1 and not first:
                        pe.wait_ge(a["qrs_in"], g * B + (b - NG * B))
                    for hh in range(2):
                        h = 2 * pr + hh
                        for c in range(C):
                            tok = slice((b % B) * S, (b % B + 1) * S)
                            i = mm3(bank(pr)[:, hh * S:(hh + 1) * S], w3d(Wh, h * DH, (h + 1) * DH)[:, c],
                                    w3d(Wl, h * DH, (h + 1) * DH)[:, c], HTh[:, c, tok], HTl[:, c, tok],
                                    c == 0, c == C - 1)
                    i.then_inc(a["q_mm"], 1)

            def scores(g, b):
                pe.wait_ge(a["qT_ready"], g * 2 * B + (2 * b + 2))
                if b % B == 0:
                    pe.wait_ge(a["kt_ready"], g + (b // B + 1))
                pe.wait_ge(a["s_read"], g * B + (b + 1))
                if not l0:
                    for tt in range(2):
                        for h in range(HG):
                            nc.tensor.matmul(bank(1)[:, tt * HG + h:tt * HG + h + 1],
                                             qsq(b)[:, h * S + tt * P:h * S + tt * P + P], ones[:, 0:1],
                                             start=True, stop=True)
                for tt in range(2):
                    for h in range(HG):
                        col = (tt * HG + h) * SK
                        i = nc.tensor.matmul(bank(2)[:, col:col + SK],
                                             qT[:, b % 2, h * S + tt * P:h * S + tt * P + P],
                                             kT[:, (b % B) * SK:(b % B + 1) * SK], start=True, stop=True)
                i.then_inc(a["s_mm"], 1)

            def turn_p(g, b):
                pe.wait_ge(a["probs"], g * B + (b + 1))
                if more_[0] and b == 2:
                    pe.wait_ge(a["kn_in"], g + 2)
                for pr in range(HS):
                    for tt in range(2):
                        i = nc.tensor.transpose(
                            bank(4)[:, (pr * 2 + tt) * P:(pr * 2 + tt + 1) * P],
                            s_sb[:, b % 2, tt * 256 + pr * P:tt * 256 + (pr + 1) * P], ident[:])
                i.then_inc(a["t_mm"], 1)

            def weigh(g, b):
                pe.wait_ge(a["pt_ready"], g * B + (b + 1))
                if b % B == 0:
                    pe.wait_ge(a["v_ready"], g + (b // B + 1))
                for h in range(HG):
                    half_ = slice(SK * (h % 2), SK * (h % 2 + 1))
                    i = nc.tensor.matmul(bank(5 + h % 2)[:, (h // 2) * S:(h // 2 + 1) * S],
                                         v_sb[half_, b % B, :], PT[half_, (h // 2) * S:(h // 2 + 1) * S],
                                         start=True, stop=True)
                i.then_inc(a["pv_mm"], 1)

            def project_o(g, b):
                pe.wait_ge(a["olo"], g * B + (b + 1))
                if b % B == 0:
                    pe.wait_ge(a["o_split"], g + 1)
                for tt in range(2):
                    pe.wait_ge(a["acc"], g * 2 * B + (2 * b + tt + 1))
                    for h in range(HG):
                        tok = slice(h * S + tt * P, h * S + tt * P + P)
                        i = mm3(bank(7 if tt == 0 else 3), OTh[:, tok], OTl[:, tok],
                                Oh[:, h * D:(h + 1) * D], Ol[:, h * D:(h + 1) * D], h == 0, h == HG - 1)
                    i.then_inc(a["wo_mm"], 1)
            more_ = [True]
            project_kv(g0)
            project_q(g0, 0, True)
            turn_k(g0)
            scores(g0, 0)
            project_q(g0, 1)
            scores(g0, 1)
            project_q(g0, 2)
            turn_p(g0, 0)
            weigh(g0, 0)

            def turn(g, more):
                more_[0] = more
                scores(g, 2)
                project_q(g, 3)
                turn_p(g, 1)
                project_o(g, 0)
                weigh(g, 1)
                scores(g, 3)
                if more:
                    project_kv(g + 1)
                    project_q(g, 4)
                turn_p(g, 2)
                project_o(g, 1)
                weigh(g, 2)
                if more:
                    turn_k(g + 1)
                    scores(g, 4)
                    project_q(g, 5)
                turn_p(g, 3)
                project_o(g, 2)
                weigh(g, 3)
                if more:
                    scores(g, 5)
                    project_q(g, 6)
                    turn_p(g, 4)
                project_o(g, 3)
                if more:
                    weigh(g, 4)
            with pe.Fori(g0, g0 + NG - 1) as g:
                turn(g, True)
            turn(g0 + NG - 1, False)

        def qsq(b):
            return AR[:, (b % 2) * HG * S:(b % 2 + 1) * HG * S]

        def act_attention(act, a, l0):
            g0 = 0 if l0 else NG

            def high_w(g):
                act.wait_ge(a["w_in"], g * 16 + 16)
                for lo, hi_ in W_PIECES:
                    nc.scalar.copy(w3d(Wh, lo, hi_), w3d(WR, lo, hi_)).then_inc(a["w_hi"], 1)

            def high_o(g):
                act.wait_ge(a["o_in"], g * 16 + 16)
                nc.scalar.copy(Oh[:], OR[:]).then_inc(a["o_hi"], 1)

            def keys_values(g):
                act.wait_ge(a["kv_mm"], g + 1)
                nc.scalar.copy(kvs[:], bank(4).rearrange("p (j n) -> p j n", j=2)).then_inc(a["kn_in"], 1)

            def keys(g):
                act.wait_ge(a["kt_mm"], g + 1)
                nc.scalar.activation(kT[:], bank(7)[:, 0:B * SK], ACT.Copy, scale=1.0 if l0 else qkw[:, 0:1])\
                    .then_inc(a["kt_ready"], 1)

            def values(g):
                for par in range(2):
                    for hf in range(2):
                        i = nc.scalar.copy(v_sb[SK * hf:SK * (hf + 1), par::2, :],
                                           kvs[SK * par:SK * (par + 1), :, DH:2 * DH])
                i.then_inc(a["v_ready"], 1)

            def queries(g, b):
                for pr in range(HS):
                    act.wait_ge(a["q_mm"], g * 2 * B + (2 * b + pr + 1))
                    cols = slice(pr * 2 * S, (pr + 1) * 2 * S)
                    if not l0:
                        nc.scalar.square(qsq(b)[:, cols], bank(pr))
                    nc.scalar.copy(qT[:, b % 2, cols], bank(pr)).then_inc(a["qT_ready"], 1)

            def exps(g, b):
                act.wait_ge(a["shifted"], g * B + (b + 1))
                s = s_sb[:, b % 2, 0:512]
                nc.scalar.activation(s, s, ACT.Exp, scale=float(DH) ** -0.5 if l0 else 1.0).then_inc(a["exps"], 1)

            def probs_t(g, b):
                act.wait_ge(a["t_mm"], g * B + (b + 1))
                nc.scalar.copy(PT[:, 0:512], bank(4)).then_inc(a["pt_ready"], 1)

            def heads(g, b):
                act.wait_ge(a["pv_mm"], g * B + (b + 1))
                for par in range(2):
                    i = nc.scalar.copy(OTh[:].rearrange("p (r q s) -> p q r s", q=2, s=S)[:, par],
                                       bank(5 + par).rearrange("p (r s) -> p r s", s=S))
                i.then_inc(a["ohi"], 1)

            def far_above(g, k):
                if l0:
                    if k == 1:
                        act.wait_ge(a["nf_v"], g + 1)
                    act.wait_ge(a["nf_summed"], g * NUP + (k + 1))
                    nc.scalar.activation(nf_far, nf_in, ACT.Relu, scale=FAR, bias=nf_bias[:, k:k + 1])\
                        .then_inc(a["nf_rise"], 1)
            if not l0:
                act.wait_ge(F2["mm"], T * NF)
            high_w(g0)
            if not l0:
                act_norm(act, 6)
            keys_values(g0)
            queries(g0, 0)
            keys(g0)
            values(g0)
            high_o(g0)
            queries(g0, 1)
            exps(g0, 0)
            queries(g0, 2)
            probs_t(g0, 0)
            exps(g0, 1)
            heads(g0, 0)

            def turn(g, more):
                queries(g, 3)
                far_above(g, 1)
                if more:
                    high_w(g + 1)
                probs_t(g, 1)
                exps(g, 2)
                far_above(g, 2)
                heads(g, 1)
                far_above(g, 3)
                if more:
                    keys_values(g + 1)
                    queries(g, 4)
                probs_t(g, 2)
                exps(g, 3)
                far_above(g, 4)
                heads(g, 2)
                if more:
                    keys(g + 1)
                far_above(g, 5)
                if more:
                    queries(g, 5)
                probs_t(g, 3)
                if more:
                    exps(g, 4)
                far_above(g, 6)
                heads(g, 3)
                if more:
                    values(g + 1)
                far_above(g, 7)
                if more:
                    queries(g, 6)
                    probs_t(g, 4)
                    exps(g, 5)
                    act.wait_ge(a["wo_mm"], g * 2 * B + 2 * B)
                    high_o(g + 1)
                    heads(g, 4)
            with act.Fori(g0, g0 + NG - 1) as g:
                turn(g, True)
            turn(g0 + NG - 1, False)

        def softmax_shift(dve, out, src, n, w, stat):
            m = stat[:, 0:n]
            nc.vector.tensor_reduce(m, src.rearrange("p (n w) -> p n w", w=w), AX.X, ALU.max)
            dve.drain()
            return nc.vector.tensor_tensor(out.rearrange("p (n w) -> p n w", w=w),
                                           src.rearrange("p (n w) -> p n w", w=w),
                                           m.unsqueeze(2).to_broadcast([P, n, w]), ALU.subtract)

        def softmax_norm(dve, buf, n, w, stat):
            v = buf.rearrange("p (n w) -> p n w", w=w)
            nc.vector.reduce_sum(stat[:, 0:n], v, AX.X)
            dve.drain()
            nc.vector.reciprocal(stat[:, 0:n], stat[:, 0:n])
            dve.drain()
            return nc.vector.tensor_tensor(v, v, stat[:, 0:n].unsqueeze(2).to_broadcast([P, n, w]), ALU.mult)

        def dve_attention(dve, a, l0):
            g0 = 0 if l0 else NG
            li = 0 if l0 else 3

            def key_norm(g):
                dve.wait_ge(a["kn_in"], g + 1)
                for j in range(2):
                    nc.vector.tensor_tensor(s_sb[:, 1, 512 + j * P:512 + (j + 1) * P], kvs[:, j, 0:DH],
                                            kvs[:, j, 0:DH], ALU.mult)
                dve.drain()
                nc.vector.reduce_sum(sm[:, 0, 4:6], s_sb[:, 1, 512:768].rearrange("p (j n) -> p j n", j=2), AX.X)
                dve.drain()
                nc.vector.tensor_scalar(sm[:, 0, 0:2], sm[:, 0, 4:6], 1.0 / DH, None, ALU.mult)\
                    .then_inc(a["ksq"], 1)
                dve.wait_ge(a["krs"], g - (NG - 1))
                for j in range(2):
                    i = nc.vector.tensor_scalar(kvs[:, j, 0:DH], kvs[:, j, 0:DH], sm[:, 0, 2 + j:3 + j], None,
                                                ALU.mult)
                i.then_inc(a["kn_ready"], 1)

            def nf_start(g):
                dve.wait_ge(a["nf_in"], g * 16 + 16)
                blocks = nf_in.rearrange("p (n q) -> p n q", q=QB)
                nc.vector.tensor_reduce(absnew[:], blocks, AX.X, ALU.max, apply_absolute_value=True)
                dve.drain()
                nc.vector.scalar_tensor_tensor(rabs[:], absnew[:], 0.0, absnew[:], ALU.is_equal, ALU.add)
                dve.drain()
                nc.vector.reciprocal(rabs[:], rabs[:])
                dve.drain()
                nc.vector.tensor_tensor(blocks, blocks, rabs[:].unsqueeze(2).to_broadcast([P, NBT, QB]), ALU.mult)
                dve.drain().then_inc(a["nf_v"], 1)

            def up(g, k):
                if not l0:
                    return
                bound, rise = UP[k]
                if k == 0:
                    dve.wait_ge(a["nf_out"], g + 1)
                    nc.vector.tensor_copy(absmax[:], absnew[:])
                    nc.vector.tensor_scalar(nf_above, nf_in, bound, rise, ALU.is_gt, ALU.mult)\
                        .then_inc(a["nf_summed"], 1)
                else:
                    dve.drain()
                    dve.wait_ge(a["nf_rise"], g * (NUP - 1) + k)
                    nc.vector.scalar_tensor_tensor(nf_above, nf_far, rise, nf_above, ALU.min, ALU.add)\
                        .then_inc(a["nf_summed"], 1)

            def down(g, k):
                if l0:
                    dve.wait_ge(a["nf_added"], g * (NDOWN - 1) + (1 if k < 2 else max(k - 1, 2)))
                    bound, fall = DOWN[k]
                    nc.vector.tensor_scalar(nf_m1 if k % 2 else nf_m0, nf_in, bound, fall, ALU.is_le, ALU.mult)\
                        .then_inc(a["nf_mask"], 1)

            def shift(g, b):
                dve.wait_ge(a["s_mm"], g * B + (b + 1))
                s = s_sb[:, b % 2, 0:512]
                src = bank(2)
                if not l0:
                    nc.vector.tensor_copy(sm[:, 0, 8:16], bank(1)[:, 0:8]).then_inc(a["qrs_in"], 1)
                    dve.wait_ge(a["qrs"], g * B + (b + 1 - NG * B))
                    nc.vector.tensor_tensor(s.rearrange("p (n w) -> p n w", w=SK),
                                            src.rearrange("p (n w) -> p n w", w=SK),
                                            sm[:, 0, 16:24].unsqueeze(2).to_broadcast([P, 8, SK]), ALU.mult)\
                        .then_inc(a["s_read"], 1)
                    dve.drain()
                    s4 = s.rearrange("p (t h k) -> p t h k", t=2, h=HG)
                    nc.vector.tensor_tensor(s4, s4, mask_sb.rearrange("p (t k) -> p t k", t=2).unsqueeze(2)
                                            .to_broadcast([P, 2, HG, SK]), ALU.add)
                    dve.drain()
                    softmax_shift(dve, s, s, 8, SK, sm[:, 1, :]).then_inc(a["shifted"], 1)
                else:
                    softmax_shift(dve, s, src, 8, SK, sm[:, 1, :]).then_inc(a["shifted"], 1)
                    dve.drain().then_inc(a["s_read"], 1)

            def norm(g, b):
                dve.wait_ge(a["exps"], g * B + (b + 1))
                softmax_norm(dve, s_sb[:, b % 2, 0:512], 8, SK, sm[:, 2, :]).then_inc(a["probs"], 1)

            def low(g, b):
                dve.wait_ge(a["ohi"], g * B + (b + 1))
                for par in range(2):
                    v = [o[:].rearrange("p (r q s) -> p q r s", q=2, s=S)[:, par] for o in (OTh, OTl)]
                    i = nc.vector.tensor_tensor(v[1], bank(5 + par).rearrange("p (r s) -> p r s", s=S),
                                                v[0].bitcast(F32), ALU.subtract)
                i.then_inc(a["olo"], 1)

            def add(g, b):
                for tt in range(2):
                    dve.wait_ge(a["wo_mm"], g * 2 * B + (2 * b + tt + 1))
                    xt = X[:, 2 * b + tt, :]
                    nc.vector.scalar_tensor_tensor(xt, bank(7 if tt == 0 else 3), tg[:, 0, li:li + 1], xt,
                                                   ALU.mult, ALU.add).then_inc(a["acc"], 1)
            if l0:
                for _ in range(2):
                    dve.drain().then_inc(a["acc"], 1)
                dve.drain().then_inc(a["s_read"], 1)
                dve.drain().then_inc(a["nf_summed"], 1)
                nf_start(0)
            else:
                dve.wait_ge(a["mask_in"], 16)
                nc.vector.tensor_tensor(qkw[:], qkn[:, 0:1], qkn[:, 1:2], ALU.mult)
                dve.drain()
                key_norm(g0)
            shift(g0, 0)
            norm(g0, 0)
            shift(g0, 1)
            norm(g0, 1)
            low(g0, 0)

            def nf_done():
                if l0:
                    dve.drain().then_inc(a["nf_norm"], 1)

            def turn(g, more):
                shift(g, 2)
                up(g, 0)
                up(g, 1)
                down(g, 0)
                norm(g, 2)
                up(g, 2)
                down(g, 1)
                add(g, 0)
                low(g, 1)
                shift(g, 3)
                if more and not l0:
                    key_norm(g + 1)
                up(g, 3)
                down(g, 2)
                norm(g, 3)
                up(g, 4)
                down(g, 3)
                add(g, 1)
                low(g, 2)
                if more:
                    shift(g, 4)
                up(g, 5)
                down(g, 4)
                down(g, 5)
                if more:
                    norm(g, 4)
                up(g, 6)
                down(g, 6)
                add(g, 2)
                low(g, 3)
                if more:
                    shift(g, 5)
                up(g, 7)
                nf_done()
                if more:
                    norm(g, 5)
                add(g, 3)
                if more:
                    if l0:
                        nf_start(g + 1)
                    low(g, 4)
                dve.drain()
            with dve.Fori(g0, g0 + NG - 1) as g:
                turn(g, True)
            turn(g0 + NG - 1, False)

        def pe_f0(pe):
            pe.wait_ge(F0["split"], 1)
            for t in range(T):
                if t >= 4:
                    pe.wait_ge(F0["acc"], t - 3)
                for c in range(C):
                    tok = slice(t * P, (t + 1) * P)
                    i = mm3(bank(2 + t % 4), HTh[:, c, tok], HTl[:, c, tok], Oh[:, c * D:(c + 1) * D],
                            Ol[:, c * D:(c + 1) * D], c == 0, c == C - 1)
                i.then_inc(F0["mm"], 1)

        def dve_f0_dequant(dve):
            dve.wait_ge(F0["w_in"], 16 * 5)
            w8 = AR[:, 4096:4352].bitcast(U8)
            nib = AR[:, 4352:4864].bitcast(U8)
            n3 = nib.rearrange("p (c o) -> p c o", c=C)
            w3 = w8.rearrange("p (c o) -> p c o", c=C)
            nc.vector.tensor_scalar(n3[:, :, 0:256], w3, 4, None, ALU.logical_shift_right)
            nc.vector.tensor_scalar(n3[:, :, 256:512], w3, 15, None, ALU.bitwise_and)
            dve.drain()
            nc.vector.tensor_tensor(WR[:, 0:2048], nib, Ze, ALU.subtract)
            dve.drain()
            nc.vector.tensor_tensor(OR[:], WR[:, 0:2048], Sc, ALU.mult).then_inc(F0["packed"], 1)
        Ze = AR[:, 0:2048]
        Sc = AR[:, 2048:4096]

        def sp_f0(sp):
            sp.wait_ge(A["nf_norm"], NG)
            sp.dma_start(AR[:, 4096:4352].bitcast(mybir.dt.int32), w4_d).then_inc(F0["w_in"], 16)
            for k, (dst, src) in enumerate(((Ze, ze4_d), (Sc, sc4_d))):
                for hf in range(2):
                    d = dst[64 * hf:64 * hf + 64, :]
                    sp.dma_start(d, src[hf:hf + 1, :].to_broadcast([64, 2048])).then_inc(F0["w_in"], 16)

        def dve_sum(dve, s, stage, kind, banks):
            for t in range(T):
                dve.wait_ge(s["mm"], t + 1)
                nc.vector.scalar_tensor_tensor(X[:, t, :], bank(banks[t % len(banks)]), tg[:, kind, stage:stage + 1],
                                               X[:, t, :], ALU.mult, ALU.add).then_inc(s["acc"], 1)

        Kbd = AR[:, 0:C * B * HC1 * SK]
        Vbd = AR[:, C * B * HC1 * SK:C * B * HC1 * SK + B * NKV1 * 2 * DH1]
        NU = B * C

        def sp_a1(sp):
            sp.wait_ge(F0["split"], 1)
            sp.dma_start(OR[:], l1kr_d).then_inc(A1["kr_in"], 16)
            sp.dma_start(WR[:, 0:2560], l1wqv_d).then_inc(A1["w_in"], 16)
            sp.wait_ge(A1["kr_mm"], 1)
            sp.dma_start(OR[:], l1o_d).then_inc(A1["o_in"], 16)

        def pool_a1(pool):
            pool.memset(Vbd, 0.0).then_inc(A1["v_out"], 1)
            pool_norm(pool, 2)
            pool.wait_ge(A1["w_hi"], 1)
            pool_low(Wh[:, 0:2048], Wl[:, 0:2048], WR[:, 0:2048]).then_inc(A1["w_split"], 1)
            pool.wait_ge(A1["o_hi"], 1)
            pool_low(Oh[:], Ol[:], OR[:]).then_inc(A1["o_split"], 1)

        def pe_a1(pe):
            pe.wait_ge(A1["kr_in"], 16)
            pe.wait_ge(F0["acc"], T)
            for hc in range(C):
                for c in range(C):
                    nc.tensor.matmul(bank(2 + hc // 2)[:, (hc % 2) * 256:(hc % 2 + 1) * 256],
                                     OR[:, c * D + hc * P:c * D + (hc + 1) * P], CT[:, c, :],
                                     start=c == 0, stop=c == C - 1)
            pe.wait_ge(A1["w_in"], 16)
            for j in range(2):
                for c in range(C):
                    i = nc.tensor.matmul(bank(4)[:, j * P:(j + 1) * P], CT[:, c, j * P:(j + 1) * P],
                                         WR[:, 2048 + c * P:2048 + (c + 1) * P], start=c == 0, stop=c == C - 1)
            i.then_inc(A1["kr_mm"], 1)
            pe_norm(pe, 2)
            pe.wait_ge(A1["w_split"], 1)

            def project_q(b):
                if b:
                    pe.wait_ge(A1["qT_ready"], 2 * b)
                for pr in range(2):
                    for hh in range(2):
                        hc = 2 * pr + hh
                        for c in range(C):
                            w = slice(c * D + hc * P, c * D + (hc + 1) * P)
                            tok = slice(b * S, (b + 1) * S)
                            i = mm3(bank(pr)[:, hh * S:(hh + 1) * S], Wh[:, w], Wl[:, w], HTh[:, c, tok],
                                    HTl[:, c, tok], c == 0, c == C - 1)
                    i.then_inc(A1["q_mm"], 1)

            def scores(u):
                b, hc = divmod(u, C)
                if u == 0:
                    pe.wait_ge(A1["kr_out"], 1)
                if hc == 0:
                    pe.wait_ge(A1["qT_ready"], 2 * b + 2)
                if u:
                    pe.wait_ge(A1["shifted"], u)
                for tt in range(2):
                    i = nc.tensor.matmul(bank(2 + tt), qT[:, b % 2, hc * S + tt * P:hc * S + tt * P + P],
                                         Kbd[:, u_kbd(hc, b)], start=True, stop=True)
                i.then_inc(A1["s_mm"], 1)

            def u_kbd(hc, b):
                at = (hc * B + b) * HC1 * SK
                return slice(at, at + HC1 * SK)

            def weigh(u):
                b, hc = divmod(u, C)
                pe.wait_ge(A1["probs"], u + 1)
                for pr in range(4):
                    for tt in range(2):
                        i = nc.tensor.transpose(bank(4, 2)[:, (pr * 2 + tt) * P:(pr * 2 + tt + 1) * P],
                                                s_sb[:, u % 2, tt * 512 + pr * P:tt * 512 + (pr + 1) * P], ident[:])
                i.then_inc(A1["t_mm"], 1)
                pe.wait_ge(A1["pt_ready"], u + 1)
                if u:
                    pe.wait_ge(A1["olo"], u)
                if u == 0:
                    pe.wait_ge(A1["v_out"], 2)
                for pr in range(4):
                    at = (b * NKV1 + 2 * hc + pr // 2) * 2 * DH1
                    i = nc.tensor.matmul(bank(6)[32 * pr:32 * pr + 32, 0:S], Vbd[:, at:at + 2 * DH1],
                                         PT[:, pr * S:(pr + 1) * S], start=True, stop=True)
                i.then_inc(A1["pv_mm"], 1)

            project_q(0)
            scores(0)
            for u in range(NU):
                b = u // C
                if u % C == 1 and b < B - 1:
                    project_q(b + 1)
                if u + 1 < NU:
                    scores(u + 1)
                weigh(u)
                if u % C == C - 1:
                    pe.wait_ge(A1["olo"], u + 1)
                    if b == 0:
                        pe.wait_ge(A1["o_split"], 1)
                    for tt in range(2):
                        if 2 * b + tt:
                            pe.wait_ge(A1["acc"], 2 * b + tt)
                        for hc in range(C):
                            tok = slice(hc * S + tt * P, hc * S + tt * P + P)
                            i = mm3(bank(7), OTh[:, tok], OTl[:, tok], Oh[:, hc * D:(hc + 1) * D],
                                    Ol[:, hc * D:(hc + 1) * D], hc == 0, hc == C - 1)
                        i.then_inc(A1["wo_mm"], 1)

        def act_a1(act):
            act.wait_ge(A1["kr_mm"], 1)
            K5 = Kbd.rearrange("p (c b h k) -> p c b h k", c=C, b=B, h=HC1)
            for hc in range(C):
                src = bank(2 + hc // 2)[:, (hc % 2) * 256:(hc % 2 + 1) * 256].rearrange("p (b k) -> p b k", b=B)
                for h in range(HC1):
                    i = nc.scalar.activation(K5[:, hc, :, h, :], src, ACT.Copy, scale=hm[:, h:h + 1])
            i.then_inc(A1["kr_out"], 1)
            act.wait_ge(A1["v_out"], 1)
            V5 = Vbd.rearrange("p (b v q d) -> p b v q d", b=B, v=NKV1, q=2)
            vv = bank(4)[:, 0:256].rearrange("p (j v d) -> p j v d", j=2, v=NKV1)
            for par in range(2):
                for hf in range(2):
                    i = nc.scalar.copy(V5[SK * hf:SK * (hf + 1), par::2, :, hf, :], vv[SK * par:SK * (par + 1)])
            i.then_inc(A1["v_out"], 1)
            nc.scalar.copy(Wh[:, 0:2048], WR[:, 0:2048]).then_inc(A1["w_hi"], 1)
            act.wait_ge(A1["o_in"], 16)
            nc.scalar.copy(Oh[:], OR[:]).then_inc(A1["o_hi"], 1)
            act_norm(act, 2)

            def queries(b):
                for pr in range(2):
                    act.wait_ge(A1["q_mm"], 2 * b + pr + 1)
                    nc.scalar.copy(qT[:, b % 2, pr * 512:(pr + 1) * 512], bank(pr)).then_inc(A1["qT_ready"], 1)

            def exps(u):
                act.wait_ge(A1["shifted"], u + 1)
                nc.scalar.activation(s_sb[:, u % 2, :], s_sb[:, u % 2, :], ACT.Exp, scale=float(DH1) ** -0.5)\
                    .then_inc(A1["exps"], 1)

            queries(0)
            exps(0)
            for u in range(NU):
                if u % C == 1 and u // C < B - 1:
                    queries(u // C + 1)
                act.wait_ge(A1["t_mm"], u + 1)
                nc.scalar.copy(PT[:], bank(4, 2)).then_inc(A1["pt_ready"], 1)
                if u + 1 < NU:
                    exps(u + 1)
                act.wait_ge(A1["pv_mm"], u + 1)
                hc = u % C
                nc.scalar.copy(OTh[:, hc * S:(hc + 1) * S], bank(6)[:, 0:S]).then_inc(A1["ohi"], 1)

        def dve_a1(dve):
            dve_norm(dve, 2)

            def shift(u):
                dve.wait_ge(A1["s_mm"], u + 1)
                softmax_shift(dve, s_sb[:, u % 2, :], bank(2, 2), 16, SK, sm[:, 1, :]).then_inc(A1["shifted"], 1)

            shift(0)
            for u in range(NU):
                dve.wait_ge(A1["exps"], u + 1)
                softmax_norm(dve, s_sb[:, u % 2, :], 16, SK, sm[:, 2, :]).then_inc(A1["probs"], 1)
                if u + 1 < NU:
                    shift(u + 1)
                dve.wait_ge(A1["ohi"], u + 1)
                b, hc = divmod(u, C)
                cols = slice(hc * S, (hc + 1) * S)
                nc.vector.tensor_tensor(OTl[:, cols], bank(6)[:, 0:S], OTh[:, cols].bitcast(F32), ALU.subtract)\
                    .then_inc(A1["olo"], 1)
                if hc == C - 1:
                    for tt in range(2):
                        dve.wait_ge(A1["wo_mm"], 2 * b + tt + 1)
                        xt = X[:, 2 * b + tt, :]
                        nc.vector.scalar_tensor_tensor(xt, bank(7), tg[:, 0, 1:2], xt, ALU.mult, ALU.add)\
                            .then_inc(A1["acc"], 1)

        NWF = D + NE + ER
        G = AR[:, 0:T * (NE + ER)]
        TK = AR[:, 2048:2048 + 8 * T * NE]

        def tk(i):
            return TK[:, i * T * NE:(i + 1) * T * NE]

        def sp_f1(sp):
            sp.wait_ge(A1["w_split"], 1)
            sp.wait_ge(A1["kr_mm"], 1)
            sp.dma_start(WR[:, 0:C * NWF], l1f_d).then_inc(F1["w_in"], 16)
            sp.wait_ge(A1["o_split"], 1)
            sp.dma_start(OR[0:EH, 0:2 * D], lb_d).then_inc(F1["b_in"], 16)

        def pool_f1(pool):
            pool.wait_ge(F1["w_hi"], 1)
            pool_low(Wh[:, 0:C * NWF], Wl[:, 0:C * NWF], WR[:, 0:C * NWF]).then_inc(F1["split"], 1)
            pool_norm(pool, 3)

        def wf(t_, c, lo, hi_):
            return t_[:, c * NWF + lo:c * NWF + hi_]

        def pe_f1(pe):
            pe_norm(pe, 3)
            pe.wait_ge(F1["split"], 1)
            for t in range(T):
                if t >= 2:
                    pe.wait_ge(F1["lg_ready"], t - 1)
                for c in range(C):
                    tok = slice(t * P, (t + 1) * P)
                    i = mm3(bank(6 + t % 2)[:, 0:NE + ER], HTh[:, c, tok], HTl[:, c, tok],
                            wf(Wh, c, D, NWF), wf(Wl, c, D, NWF), c == 0, c == C - 1)
                i.then_inc(F1["lg_mm"], 1)

            def base(t):
                if t >= 4:
                    pe.wait_ge(F1["acc"], t - 3)
                for c in range(C):
                    tok = slice(t * P, (t + 1) * P)
                    mm3(bank(2 + t % 4), HTh[:, c, tok], HTl[:, c, tok], wf(Wh, c, 0, D), wf(Wl, c, 0, D),
                        c == 0, False)
            for t in range(3):
                base(t)
            pe.wait_ge(F1["h_ready"], 1)
            pe.wait_ge(F1["b_in"], 16)
            for t in range(T):
                if t == 0:
                    pe.wait_ge(F1["lg_ready"], T)
                for e in range(2):
                    at = t * (NE + ER) + NE + e * EH
                    i = nc.tensor.transpose(bank(6 + t % 2)[0:EH, e * P:(e + 1) * P], G[:, at:at + EH], ident[:])
                i.then_inc(F1["t_mm"], 1)
                if t + 3 < T:
                    base(t + 3)
                pe.wait_ge(F1["ht_ready"], t + 1)
                for e in range(2):
                    at = (t % 2) * 256 + e * P
                    i = nc.tensor.matmul(bank(2 + t % 4), PT[0:EH, at:at + P], OR[0:EH, e * D:(e + 1) * D],
                                         start=False, stop=e == 1)
                i.then_inc(F1["mm"], 1)

        def act_f1(act):
            act.wait_ge(F1["w_in"], 16)
            act.wait_ge(A1["wo_mm"], T)
            nc.scalar.copy(Wh[:, 0:C * NWF], WR[:, 0:C * NWF]).then_inc(F1["w_hi"], 1)
            act_norm(act, 3)
            for t in range(T):
                act.wait_ge(F1["lg_mm"], t + 1)
                nc.scalar.copy(G[:, t * (NE + ER):(t + 1) * (NE + ER)], bank(6 + t % 2)[:, 0:NE + ER])\
                    .then_inc(F1["lg_ready"], 1)
            act.wait_ge(F1["gap"], 1)
            nc.scalar.activation(sm[:, 0, 16:24], sm[:, 0, 16:24], ACT.Exp).then_inc(F1["egap"], 1)
            for t in range(T):
                act.wait_ge(F1["t_mm"], t + 1)
                nc.scalar.copy(PT[0:EH, (t % 2) * 256:(t % 2 + 1) * 256], bank(6 + t % 2)[0:EH, 0:256])\
                    .then_inc(F1["ht_ready"], 1)

        def dve_f1(dve):
            dve_norm(dve, 3)
            dve.wait_ge(F1["lg_ready"], T)
            G3 = G.rearrange("p (t n) -> p t n", t=T)

            def v3(i):
                return tk(i).rearrange("p (t n) -> p t n", t=T)
            L = G3[:, :, 0:NE]
            iob = iot[:].unsqueeze(1).to_broadcast([P, T, NE])

            def col(k):
                return sm[:, 0, k * T:(k + 1) * T]

            def bc(k):
                return col(k).unsqueeze(2).to_broadcast([P, T, NE])

            def pick(src, top, at, one):
                nc.vector.tensor_reduce(col(top), src, AX.X, ALU.max)
                dve.drain()
                nc.vector.tensor_tensor(v3(5), src, bc(top), ALU.is_equal)
                dve.drain()
                nc.vector.tensor_tensor(v3(5), v3(5), iob, ALU.mult)
                dve.drain()
                nc.vector.tensor_reduce(col(at), v3(5), AX.X, ALU.min)
                dve.drain()
                nc.vector.tensor_tensor(v3(one), iob, bc(at), ALU.is_equal)
                dve.drain()
            pick(L, 0, 1, 0)
            nc.vector.tensor_scalar(tk(2), tk(0), -2.0 * HALF_MAX, HALF_MAX, ALU.mult, ALU.add)
            dve.drain()
            nc.vector.tensor_tensor(v3(2), L, v3(2), ALU.min)
            dve.drain()
            pick(v3(2), 3, 1, 1)
            nc.vector.tensor_tensor(col(2), col(3), col(0), ALU.subtract).then_inc(F1["gap"], 1)
            dve.wait_ge(F1["egap"], 1)
            nc.vector.tensor_scalar(col(0), col(2), 1.0, None, ALU.add)
            dve.drain()
            nc.vector.reciprocal(col(0), col(0))
            dve.drain()
            nc.vector.tensor_scalar(col(0), col(0), LORA_SCALE, None, ALU.mult)
            dve.drain()
            nc.vector.tensor_tensor(col(2), col(2), col(0), ALU.mult)
            dve.drain()
            nc.vector.tensor_tensor(v3(0), v3(0), bc(0), ALU.mult)
            nc.vector.tensor_tensor(v3(1), v3(1), bc(2), ALU.mult)
            dve.drain()
            nc.vector.tensor_tensor(tk(0), tk(0), tk(1), ALU.add)
            dve.drain()
            for t in range(T):
                h = G3[:, t, NE:NE + ER].rearrange("p (e r) -> p e r", r=RANK)
                i = nc.vector.tensor_tensor(h, h, v3(0)[:, t, :].unsqueeze(2).to_broadcast([P, NE, RANK]), ALU.mult)
            i.then_inc(F1["h_ready"], 1)
            dve_sum(dve, F1, 1, 1, (2, 3, 4, 5))

        CB = AR[0:SK, 0:B * D]
        KT2 = AR[:, B * D:B * D + C * B * SK]
        BK = AR[0:1, 3072:3072 + B * SK]

        def sp_a2(sp):
            sp.wait_ge(F1["split"], 1)
            sp.dma_start(WR[:, 0:2048], l2k_d).then_inc(A2["k_in"], 16)
            sp.wait_ge(F1["mm"], T)
            sp.dma_start(CB, ctxB_d.rearrange("k b n -> k (b n)")).then_inc(A2["b_in"], 16)
            sp.dma_start(OR[:], l2q_d).then_inc(A2["q_in"], 16)

        def pe_a2(pe):
            pe.wait_ge(A2["k_in"], 16)
            pe.wait_ge(F1["acc"], T)
            for dc in range(C):
                for c in range(C):
                    i = nc.tensor.matmul(bank(2 + dc // 2)[:, (dc % 2) * 256:(dc % 2 + 1) * 256],
                                         WR[:, c * D + dc * P:c * D + (dc + 1) * P], CT[:, c, :],
                                         start=c == 0, stop=c == C - 1)
            i.then_inc(A2["k_mm"], 1)
            pe.wait_ge(A2["kt_ready"], 1)
            pe.wait_ge(A2["q_in"], 16)
            for ic in range(C):
                for dc in range(C):
                    nc.tensor.matmul(bank(4 + ic // 2)[:, (ic % 2) * 256:(ic % 2 + 1) * 256],
                                     OR[:, dc * D + ic * P:dc * D + (ic + 1) * P],
                                     KT2[:, dc * 256:(dc + 1) * 256], start=dc == 0, stop=dc == C - 1)
            for dc in range(C):
                i = nc.tensor.matmul(bank(6)[0:1, 0:256], b2[:, dc:dc + 1], KT2[:, dc * 256:(dc + 1) * 256],
                                     start=dc == 0, stop=dc == C - 1)
            i.then_inc(A2["m_mm"], 1)
            pe_norm(pe, 4)
            pe.wait_ge(A2["mlo"], 1)
            for t in range(T):
                tok = slice(t * P, (t + 1) * P)
                o = bank(7)[:, t * SK:(t + 1) * SK]
                b = t // 2
                nc.tensor.matmul(o, ones[0:1, :], BK[:, b * SK:(b + 1) * SK], start=True, stop=False)
                for c in range(C):
                    m = slice(c * 256 + b * SK, c * 256 + (b + 1) * SK)
                    i = mm3(o, HTh[:, c, tok], HTl[:, c, tok], OTh[:, m], OTl[:, m], False, c == C - 1)
            i.then_inc(A2["s_mm"], 1)
            pe.wait_ge(A2["probs"], 1)
            for t in range(T):
                i = nc.tensor.transpose(bank(2 + t // 4)[0:SK, (t % 4) * P:(t % 4 + 1) * P],
                                        s_sb[:, 0, t * SK:(t + 1) * SK], ident[:])
            i.then_inc(A2["t_mm"], 1)
            pe.wait_ge(A2["pt_ready"], 1)
            pe.wait_ge(A2["b_in"], 16)
            for t in range(T):
                if t >= 2:
                    pe.wait_ge(A2["acc"], t - 1)
                b = t // 2
                nc.tensor.matmul(bank(4 + t % 2), PT[0:SK, t * P:(t + 1) * P], CB[:, b * D:(b + 1) * D],
                                 start=True, stop=True).then_inc(A2["mm"], 1)

        def act_a2(act):
            act.wait_ge(A2["k_mm"], 1)
            act.wait_ge(F1["mm"], T)
            for dc in range(C):
                i = nc.scalar.activation(KT2[:, dc * 256:(dc + 1) * 256],
                                         bank(2 + dc // 2)[:, (dc % 2) * 256:(dc % 2 + 1) * 256], ACT.Identity,
                                         bias=b2[:, C + dc:C + dc + 1])
            i.then_inc(A2["kt_ready"], 1)
            act.wait_ge(A2["m_mm"], 1)
            nc.scalar.copy(BK, bank(6)[0:1, 0:256])
            nc.scalar.copy(OTh[:], bank(4, 2)).then_inc(A2["mhi"], 1)
            act_norm(act, 4)
            act.wait_ge(A2["shifted"], 1)
            nc.scalar.activation(s_sb[:, 0, 0:512], s_sb[:, 0, 0:512], ACT.Exp, scale=float(D) ** -0.5)\
                .then_inc(A2["exps"], 1)
            act.wait_ge(A2["t_mm"], 1)
            nc.scalar.copy(PT[0:SK, :], bank(2, 2)[0:SK, :]).then_inc(A2["pt_ready"], 1)

        def dve_a2(dve):
            dve.wait_ge(A2["mhi"], 1)
            nc.vector.tensor_tensor(OTl[:], bank(4, 2), OTh[:].bitcast(F32), ALU.subtract).then_inc(A2["mlo"], 1)
            dve_norm(dve, 4)
            dve.wait_ge(A2["s_mm"], 1)
            softmax_shift(dve, s_sb[:, 0, 0:512], bank(7), T, SK, sm[:, 1, :]).then_inc(A2["shifted"], 1)
            dve.wait_ge(A2["exps"], 1)
            softmax_norm(dve, s_sb[:, 0, 0:512], T, SK, sm[:, 2, :]).then_inc(A2["probs"], 1)
            dve_sum(dve, A2, 2, 0, (4, 5))

        HW = 3 * D

        def sp_f2(sp):
            def load(f, par):
                at = par * HW
                nc_sem = F2["in0"] if par == 0 else F2["in1"]
                for k in range(2):
                    sp.dma_start(WR[:, at + k * D:at + (k + 1) * D], scratch[:, k, bass.ds(f * D, D)])\
                        .then_inc(nc_sem, 16)
                w3v = WR[:, at + 2 * D:at + 3 * D].rearrange("p (r h) -> p r h", r=4)
                for r in range(4):
                    sp.dma_start(w3v[:, r, :], scratch[:, 2, bass.ds(f * P + r * HF, P)]).then_inc(nc_sem, 16)
            sp.wait_ge(A["nf_stored"], 16 * NG)
            sp.wait_ge(A2["k_mm"], 1)
            load(0, 0)
            load(1, 1)
            with sp.Fori(0, 4) as k:
                for par in range(2):
                    f = k * 2 + (par + 2)
                    sp.wait_ge(F2["t_mm"], f * 3 - 3)
                    load(f, par)
            sp.wait_ge(F2["t_mm"], 3 * (NF - 2))
            load(NF - 1, 0)

        def pe_f2(pe):
            def turn_w(f, par, first=False):
                pe.wait_ge(F2["in0"] if par == 0 else F2["in1"], f * 48 + (96 - 48 * par))
                for k in range(3):
                    if k == 0 and not first:
                        pe.wait_ge(F2["wlo"], f * 3)
                    if k == 2:
                        pe.wait_ge(F2["wlo"], f * 3 + 1)
                    for c in range(C):
                        at = par * HW + k * D + c * P
                        i = nc.tensor.transpose(bank(5 + k % 2)[:, c * P:(c + 1) * P], WR[:, at:at + P], ident[:])
                    i.then_inc(F2["t_mm"], 1)

            def gate_up(f, par, first=False):
                pe.wait_ge(F2["wlo"], f * 3 + 2)
                if not first:
                    pe.wait_ge(F2["act"], f)
                for k in range(2):
                    for th in range(2):
                        for c in range(C):
                            w = slice(par * HW + k * D + c * P, par * HW + k * D + (c + 1) * P)
                            tok = slice(th * 512, (th + 1) * 512)
                            i = mm3(bank(2 * k + th), Wh[:, w], Wl[:, w], HTh[:, c, tok], HTl[:, c, tok],
                                    c == 0, c == C - 1)
                    i.then_inc(F2["g_mm" if k == 0 else "u_mm"], 1)

            def down(f, par):
                pe.wait_ge(F2["alo"], f + 1)
                pe.wait_ge(F2["wlo"], f * 3 + 3)
                w = slice(par * HW + 2 * D, (par + 1) * HW)
                for t in range(T):
                    pe.wait_ge(F2["acc"], f * T + (t + 1))
                    tok = slice(par * 1024 + t * P, par * 1024 + (t + 1) * P)
                    mm3(bank(7 if t % 2 == 0 else 4), Oh[:, tok], Ol[:, tok], Wh[:, w], Wl[:, w], True, True)\
                        .then_inc(F2["mm"], 1)
            pe.wait_ge(A2["acc"], T)
            turn_w(0, 0, True)
            turn_w(1, 1)
            pe_norm(pe, 5)
            gate_up(0, 0, True)
            with pe.Fori(0, 4) as k:
                for par in range(2):
                    f = k * 2 + par
                    gate_up(f + 1, 1 - par)
                    down(f, par)
                    turn_w(f + 2, par)
            gate_up(NF - 2, 1)
            down(NF - 3, 0)
            turn_w(NF - 1, 0)
            gate_up(NF - 1, 0)
            down(NF - 2, 1)
            down(NF - 1, 0)

        def w_parts(par, k):
            v = [t_[:, par * HW + k * D:par * HW + (k + 1) * D] for t_ in (Wh, Wl)]
            if k < 2:
                return v
            return [x.rearrange("p (q r) -> p r q", r=4) for x in v]

        def w_bank(k):
            return bank(5 + k % 2) if k < 2 else bank(5).rearrange("p (r q) -> p r q", r=4)

        def act_f2(act):
            def high(f, par):
                for k in range(3):
                    act.wait_ge(F2["t_mm"], f * 3 + (k + 1))
                    nc.scalar.copy(w_parts(par, k)[0], w_bank(k)).then_inc(F2["whi"], 1)

            def silu(f, par):
                act.wait_ge(F2["g_mm"], f + 1)
                nc.scalar.activation(s_sb[:, 0, :], bank(0, 2), ACT.Silu).then_inc(F2["silu"], 1)
                act.wait_ge(F2["act"], f + 1)
                nc.scalar.copy(Oh[:, par * 1024:(par + 1) * 1024], s_sb[:, 1, :]).then_inc(F2["ahi"], 1)
            silu(0, 0)
            with act.Fori(0, 4) as k:
                for par in range(2):
                    f = k * 2 + par
                    silu(f + 1, 1 - par)
                    high(f + 2, par)
            silu(NF - 2, 1)
            high(NF - 1, 0)
            silu(NF - 1, 0)

        def act_f2_first(act):
            for f in range(2):
                for k in range(3):
                    act.wait_ge(F2["t_mm"], f * 3 + k + 1)
                    nc.scalar.copy(w_parts(f, k)[0], w_bank(k)).then_inc(F2["whi"], 1)

        def dve_f2(dve):
            def low(f, par):
                for k in range(3):
                    dve.wait_ge(F2["whi"], f * 3 + (k + 1))
                    hi, lo = w_parts(par, k)
                    nc.vector.tensor_tensor(lo, w_bank(k), hi.bitcast(F32), ALU.subtract).then_inc(F2["wlo"], 1)

            def product(f):
                dve.drain()
                dve.wait_ge(F2["silu"], f + 1)
                dve.wait_ge(F2["u_mm"], f + 1)
                nc.vector.tensor_tensor(s_sb[:, 1, :], bank(2, 2), s_sb[:, 0, :], ALU.mult).then_inc(F2["act"], 1)

            def low_act(f, par):
                dve.wait_ge(F2["ahi"], f + 1)
                cols = slice(par * 1024, (par + 1) * 1024)
                nc.vector.tensor_tensor(Ol[:, cols], s_sb[:, 1, :], Oh[:, cols].bitcast(F32), ALU.subtract)\
                    .then_inc(F2["alo"], 1)

            def add(f, ts):
                for t in ts:
                    dve.wait_ge(F2["mm"], f * T + (t + 1))
                    nc.vector.scalar_tensor_tensor(X[:, t, :], bank(7 if t % 2 == 0 else 4), tg[:, 1, 2:3],
                                                   X[:, t, :], ALU.mult, ALU.add).then_inc(F2["acc"], 1)
            low(0, 0)
            low(1, 1)
            dve.drain().then_inc(F2["acc"], 1)
            dve.drain().then_inc(F2["acc"], 1)
            dve_norm(dve, 5)
            product(0)
            low_act(0, 0)

            def step(f, par, more):
                if more:
                    product(f + 1)
                add(f, range(0, 4))
                if more:
                    low_act(f + 1, 1 - par)
                add(f, range(4, 8))
            with dve.Fori(0, 4) as k:
                for par in range(2):
                    f = k * 2 + par
                    step(f, par, True)
                    low(f + 2, par)
                dve.drain()
            step(NF - 3, 0, True)
            low(NF - 1, 0)
            step(NF - 2, 1, True)
            step(NF - 1, 0, False)

        def at3(lo, n):
            return AR[:, lo:lo + n]
        NM = NS * NS
        LG = at3(4096, T * NL)
        Z = at3(4352, T * NM)
        K3 = at3(4480, T * NM)
        TM = at3(4608, T * NM)
        PP = at3(4736, T * 2 * NS)
        RR = at3(4800, T * NS)
        CC = at3(4832, T * NS)
        MX = at3(4864, T * 2 * NS)
        SG = at3(4928, 4)
        XP = at3(5120, T * P)
        WB = at3(6144, P)

        def sp_f3(sp):
            sp.wait_ge(A["w_split"], 6 * NG)
            sp.wait_ge(A["acc"], 16 * NG + 2)
            sp.dma_start(WR[:, 0:C * NL], w24_d).then_inc(F3["w_in"], 16)
            sp.dma_start(WB, wbr_d).then_inc(F3["w_in"], 16)

        def pool_f3(pool):
            pool_norm(pool, 7)

        def pe_f3(pe):
            pe_norm(pe, 7)
            pe.wait_ge(F3["wlo"], 1)
            for t in range(T):
                tok = slice(t * P, (t + 1) * P)
                for c in range(C):
                    w = slice(c * NL, (c + 1) * NL)
                    i = mm3(bank(7)[:, t * NL:(t + 1) * NL], HTh[:, c, tok], HTl[:, c, tok], Wh[:, w], Wl[:, w],
                            c == 0, c == C - 1)
            i.then_inc(F3["lg_mm"], 1)
            pe.wait_ge(F3["pre"], 1)
            for t in range(T):
                i = nc.tensor.transpose(bank(2, 2)[:, t * P:(t + 1) * P], XP[:, t * P:(t + 1) * P], ident[:])
            i.then_inc(F3["preT_mm"], 1)
            pe.wait_ge(F3["preT"], 1)
            for t in range(T):
                i = nc.tensor.matmul(bank(4, 2)[:, t * P:(t + 1) * P], PT[:, t * P:(t + 1) * P], WB,
                                     start=True, stop=True)
            i.then_inc(F3["y_mm"], 1)

        def act_f3(act):
            act.wait_ge(F3["w_in"], 32)
            nc.scalar.copy(Wh[:, 0:C * NL], WR[:, 0:C * NL]).then_inc(F3["w_hi"], 1)
            act_norm(act, 7)
            asked = [0]

            def run(out, in_, f, **kw):
                asked[0] += 1
                act.wait_ge(F3["to_act"], asked[0])
                nc.scalar.activation(out, in_, f, **kw).then_inc(F3["from_act"], 1)
            run(PP, PP, ACT.Exp)
            run(SG[:, 0:1], gate[:], ACT.Exp, scale=-1.0)
            for _ in range(2):
                run(K3, Z, ACT.Exp)
                run(MX[:, 0:T * NS], MX[:, 0:T * NS], ACT.Ln)
            run(K3, Z, ACT.Exp)
            act.wait_ge(F3["preT_mm"], 1)
            nc.scalar.copy(PT[:], bank(2, 2)).then_inc(F3["preT"], 1)
            run(AR[:, 4800:4864], AR[:, 4800:4864], ACT.Ln)
            run(K3, Z, ACT.Exp)

        def dve_f3(dve):
            dve.wait_ge(F3["w_hi"], 1)
            nc.vector.tensor_tensor(Wl[:, 0:C * NL], WR[:, 0:C * NL], Wh[:, 0:C * NL].bitcast(F32), ALU.subtract)\
                .then_inc(F3["wlo"], 1)
            dve_norm(dve, 7)
            dve.wait_ge(F3["lg_mm"], 1)
            asked = [0]

            def ask(i):
                asked[0] += 1
                i.then_inc(F3["to_act"], 1)

            def answered():
                dve.wait_ge(F3["from_act"], asked[0])
            LG3 = LG.rearrange("p (t n) -> p t n", t=T)
            nc.vector.tensor_tensor(LG3, bank(7)[:, 0:T * NL].rearrange("p (t n) -> p t n", t=T),
                                    rms[:].unsqueeze(2).to_broadcast([P, T, NL]), ALU.mult)
            dve.drain()
            nc.vector.tensor_tensor(LG3, LG3, bases[:].unsqueeze(1).to_broadcast([P, T, NL]), ALU.add)
            dve.drain()
            Z4 = Z.rearrange("p (t i j) -> p t i j", t=T, i=NS)
            K4 = K3.rearrange("p (t i j) -> p t i j", t=T, i=NS)
            T4 = TM.rearrange("p (t i j) -> p t i j", t=T, i=NS)
            nc.vector.tensor_scalar(Z.rearrange("p (t n) -> p t n", t=T), LG3[:, :, 0:NM], 10.0, None, ALU.mult)
            nc.vector.tensor_copy(PP.rearrange("p (t n) -> p t n", t=T), LG3[:, :, NM:NL])
            dve.drain()
            ask(softmax_shift(dve, PP, PP, 2 * T, NS, MX))
            dve.drain()

            def view(x, rows):
                return x if rows else x.rearrange("p t i j -> p t j i")

            def spread(v, rows):
                v = v.rearrange("p (t n) -> p t n", t=T)
                return (v.unsqueeze(3) if rows else v.unsqueeze(2)).to_broadcast([P, T, NS, NS])
            asked[0] += 1
            nc.vector.tensor_copy(SG[:, 1:2], gate[:]).then_inc(F3["to_act"], 1)
            for rows in (True, False):
                M = MX[:, 0:T * NS]
                nc.vector.tensor_reduce(M, view(Z4, rows), AX.X, ALU.max)
                dve.drain()
                ask(nc.vector.tensor_tensor(Z4, Z4, spread(M, rows), ALU.subtract))
                answered()
                ask(nc.vector.tensor_reduce(M, view(K4, rows), AX.X, ALU.add))
                answered()
                i = nc.vector.tensor_tensor(Z4, Z4, spread(M, rows), ALU.subtract)
                dve.drain()
            ask(nc.vector.memset(CC, 1.0))
            softmax_norm(dve, PP, 2 * T, NS, MX)
            dve.drain()
            P3 = PP.rearrange("p (t n) -> p t n", t=T)
            for n in range(NS):
                for t in range(T):
                    h = hn_of(7, t)[:, n * P:(n + 1) * P]
                    xp = XP[:, t * P:(t + 1) * P]
                    if n == 0:
                        i = nc.vector.tensor_scalar(xp, h, P3[:, t, n:n + 1], None, ALU.mult)
                    else:
                        i = nc.vector.scalar_tensor_tensor(xp, h, P3[:, t, n:n + 1], xp, ALU.mult, ALU.add)
                dve.drain()
            dve.drain().then_inc(F3["pre"], 1)
            answered()

            def balance():
                for rows, given, got in ((True, CC, RR), (False, RR, CC)):
                    nc.vector.tensor_tensor(T4, K4, spread(given, not rows), ALU.mult)
                    dve.drain()
                    nc.vector.tensor_reduce(got, view(T4, rows), AX.X, ALU.add)
                    dve.drain()
                    nc.vector.reciprocal(got, got)
                    dve.drain()
            with dve.Fori(0, SK_LINEAR) as _:
                balance()
            ask(dve.drain())
            answered()
            nc.vector.tensor_tensor(Z4, Z4, spread(RR, True), ALU.add)
            dve.drain()
            ask(nc.vector.tensor_tensor(Z4, Z4, spread(CC, False), ALU.add))
            answered()
            dve.drain()
            nc.vector.memset(CC, 1.0)
            dve.drain()
            with dve.Fori(0, SK_LINEAR + 1) as _:
                balance()
            nc.vector.tensor_tensor(K4, K4, spread(RR, True), ALU.mult)
            nc.vector.tensor_scalar(SG[:, 0:1], SG[:, 0:1], 1.0, None, ALU.add)
            dve.drain()
            nc.vector.tensor_tensor(K4, K4, spread(CC, False), ALU.mult)
            nc.vector.reciprocal(SG[:, 0:1], SG[:, 0:1])
            dve.drain()
            nc.vector.tensor_tensor(SG[:, 1:2], SG[:, 0:1], tg[:, 1, 3:4], ALU.mult)
            dve.drain()
            nc.vector.tensor_tensor(SG[:, 2:3], tg[:, 1, 3:4], SG[:, 1:2], ALU.subtract)
            nc.vector.tensor_scalar(K3, K3, SG[:, 1:2], None, ALU.mult)
            nc.vector.tensor_scalar(PP, PP, tg[:, 1, 3:4], None, ALU.mult)
            dve.drain()
            diag = K3.rearrange("p (t n) -> p t n", t=T)[:, :, 0:NM:NS + 1]
            nc.vector.tensor_scalar(diag, diag, SG[:, 2:3], None, ALU.add)
            dve.wait_ge(F3["y_mm"], 1)
            dve.drain()
            H3 = K3.rearrange("p (t n) -> p t n", t=T)
            for t in range(T):
                for j in range(NS + 1):
                    for i_ in range(NS):
                        xt = X[:, t, i_ * P:(i_ + 1) * P]
                        src = bank(4, 2)[:, t * P:(t + 1) * P] if j == NS else hn_of(7, t)[:, j * P:(j + 1) * P]
                        w = P3[:, t, NS + i_:NS + i_ + 1] if j == NS else H3[:, t, i_ * NS + j:i_ * NS + j + 1]
                        i = nc.vector.scalar_tensor_tensor(xt, src, w, xt, ALU.mult, ALU.add)
                    dve.drain()
                dve.drain().then_inc(F3["done"], 1)

        CONSTS = 16 * 8

        @block.sync
        def _(sp):
            sp.dma_start(X[:], x_d.rearrange("(t p) n -> p t n", p=P)).then_inc(x_in, 16)
            sp.dma_start(CT[:], ctxT_d).then_inc(ctx_in, 16)
            sp.dma_start(gates[:, 0, :], gx_d.to_broadcast([P, 4])).then_inc(consts_in, 16)
            sp.dma_start(gates[:, 1, :], gf_d.to_broadcast([P, 4])).then_inc(consts_in, 16)
            sp.dma_start(lnw[:], lnw_d.to_broadcast([P, D])).then_inc(consts_in, 16)
            sp.dma_start(qkn[:], qkn_d).then_inc(consts_in, 16)
            sp.dma_start(b2[:], b2_d).then_inc(consts_in, 16)
            sp.dma_start(iot[:], iota_d.to_broadcast([P, NE])).then_inc(consts_in, 16)
            sp.dma_start(bases[:], bases_d.to_broadcast([P, NL])).then_inc(consts_in, 16)
            sp.dma_start(gate[:], gate_d.to_broadcast([P, 1])).then_inc(consts_in, 16)
            sp_attention(sp, A, True)
            sp_f0(sp)
            sp_a1(sp)
            sp_f1(sp)
            sp_a2(sp)
            sp_f2(sp)
            sp_attention(sp, A, False)
            sp_f3(sp)
            sp.wait_ge(F3["done"], T)
            for t in range(T):
                sp.dma_start(out_d[t * P:(t + 1) * P, :], X[:, t, :]).then_inc(out_stored, 16)
            sp.wait_ge(out_stored, 16 * T)

        @block.gpsimd
        def _(pool):
            nc.gpsimd.memset(ident[:], 0.0)
            nc.gpsimd.memset(ones[:], 1.0)
            nc.gpsimd.memset(half[:], -0.5)
            nc.gpsimd.memset(tiny[:, 0:8], EPS)
            nc.gpsimd.memset(tiny[:, 8:16], EPS * DH)
            nc.gpsimd.memset(hm[:], 1.0)
            for k in range(1, NUP):
                nc.gpsimd.memset(nf_bias[:, k:k + 1], -UP[k][0] * FAR)
            pool.drain()
            nc.gpsimd.affine_select(out=ident[:], in_=ident[:], compare_op=ALU.not_equal, fill=1.0, base=0,
                                    pattern=[[-1, P]], channel_multiplier=1)
            nc.gpsimd.affine_select(out=hm[:], in_=hm[:], compare_op=ALU.is_ge, fill=0.0, base=0,
                                    pattern=[[-DH1, HC1]], channel_multiplier=1)
            pool.drain()
            nc.gpsimd.affine_select(out=hm[:], in_=hm[:], compare_op=ALU.is_ge, fill=0.0, base=DH1 - 1,
                                    pattern=[[DH1, HC1]], channel_multiplier=-1)
            pool.drain().then_inc(pool_consts, 1)
            pool.wait_ge(ctx_hi, 1)
            pool_low(CTh[:], CTl[:], CT[:]).then_inc(ctx_split, 1)
            pool_norm(pool, 0)
            pool_attention(pool, A, True)
            pool_norm(pool, 1)
            pool.wait_ge(F0["w_hi"], 1)
            pool_low(Oh[:], Ol[:], OR[:]).then_inc(F0["split"], 1)
            pool_a1(pool)
            pool_f1(pool)
            pool_norm(pool, 4)
            pool_norm(pool, 5)
            pool_attention(pool, A, False)
            pool_f3(pool)

        @block.scalar
        def _(act):
            act.wait_ge(consts_in, CONSTS)
            nc.scalar.activation(tg[:], gates[:], ACT.Tanh).then_inc(gates_ready, 1)
            act.wait_ge(ctx_in, 16)
            nc.scalar.copy(CTh[:], CT[:]).then_inc(ctx_hi, 1)
            act_norm(act, 0)
            act_attention(act, A, True)
            act_norm(act, 1)
            act.wait_ge(F0["packed"], 1)
            nc.scalar.copy(Oh[:], OR[:]).then_inc(F0["w_hi"], 1)
            act_a1(act)
            act_f1(act)
            act_a2(act)
            act_f2_first(act)
            act_norm(act, 5)
            act_f2(act)
            act_attention(act, A, False)
            act_f3(act)

        @block.tensor
        def _(pe):
            pe_norm(pe, 0)
            pe.wait_ge(ctx_split, 1)
            pe_attention(pe, A, True)
            pe_norm(pe, 1)
            pe_f0(pe)
            pe_a1(pe)
            pe_f1(pe)
            pe_a2(pe)
            pe_f2(pe)
            pe_norm(pe, 6)
            pe_attention(pe, A, False)
            pe_f3(pe)

        @block.vector
        def _(dve):
            dve_norm(dve, 0)
            dve.wait_ge(gates_ready, 1)
            dve_attention(dve, A, True)
            dve_norm(dve, 1)
            dve_f0_dequant(dve)
            dve_sum(dve, F0, 0, 1, (2, 3, 4, 5))
            dve_a1(dve)
            dve_f1(dve)
            dve_a2(dve)
            dve_f2(dve)
            dve_norm(dve, 6)
            dve_attention(dve, A, False)
            dve_f3(dve)


def lay_out(i):
    f = {k: np.asarray(v) for k, v in i.items()}

    def chunks(w):
        return w.reshape(C, P, -1).transpose(1, 0, 2)

    def group(wq, wk, wv):
        g = [np.concatenate([wq[:, k * WQ:(k + 1) * WQ], wk[:, k * DH:(k + 1) * DH], wv[:, k * DH:(k + 1) * DH]], 1)
             for k in range(NG)]
        return np.stack([chunks(w).reshape(P, -1) for w in g])

    def rows(wo):
        return wo.reshape(NG, HG, DH, D).transpose(0, 2, 1, 3).reshape(NG, P, -1)

    ctxf = f['ctx_4096'].reshape(B * SK, D)
    w1, w2 = (np.concatenate([f[f'L2_ffn_{k}'], np.zeros((NF * P - HF, D), np.float32)])
              .reshape(NF, P, D).transpose(1, 0, 2).reshape(P, NG, NBU * QB) for k in ('w1', 'w2'))
    w3 = np.concatenate([f['L2_ffn_w3'].reshape(P, NB3 * QB), np.zeros((P, NFW - NB3 * QB), np.float32)], 1)\
        .reshape(P, NG, NBU * QB)
    kr = f['L1_xattn_wk'].reshape(NKV1, DH1, D)
    kr = np.stack([np.concatenate([kr[2 * c + h // 4] for h in range(HC1)]) for c in range(C)])
    packed = f['L0_ffn_W_q'].reshape(D // 2, D).T

    def groups(z):
        return z.reshape(D, C, 2).transpose(2, 1, 0).reshape(2, -1)
    out = {
        'x': f['x'].reshape(B * S, D),
        'ctxT': chunks(ctxf.T),
        'ctxB': f['ctx_4096'].transpose(1, 0, 2),
        'gx': f['g_xattn'].reshape(1, 4), 'gf': f['g_ffn'].reshape(1, 4),
        'wl': np.concatenate([group(f['L0_xattn_wq'], f['L0_xattn_wk'], f['L0_xattn_wv']),
                        group(f['L3_xattn_q_proj_w'].T, f['L3_xattn_k_proj_w'].T, f['L3_xattn_v_proj_w'].T)]),
        'ol': np.concatenate([rows(f['L0_xattn_wo']), rows(f['L3_xattn_o_proj_w'].T)]),
        'w4': np.ascontiguousarray(chunks(packed).reshape(P, -1)).view(np.int32),
        'sc4': groups(f['L0_ffn_scale']), 'ze4': groups(f['L0_ffn_zero']),
        'l1wqv': np.concatenate([chunks(f['L1_xattn_wq'].T).reshape(P, -1), chunks(f['L1_xattn_wv'].T).reshape(P, -1)], 1),
        'l1kr': chunks(kr.reshape(C * P, D).T).reshape(P, -1),
        'l1o': chunks(f['L1_xattn_wo'].T).reshape(P, -1),
        'lnw': f['L1_xattn_ln_w'].reshape(1, D),
        'l1f': chunks(np.concatenate([f['L1_ffn_base_W'], f['L1_ffn_gate_W'], f['L1_ffn_lora_A'].reshape(ER, D)]).T)
        .reshape(P, -1),
        'lb': f['L1_ffn_lora_B'].transpose(0, 2, 1).reshape(2, EH, D).transpose(1, 0, 2).reshape(EH, -1),
        'l2k': chunks(f['L2_xattn_Wk'].T).reshape(P, -1), 'l2q': chunks(f['L2_xattn_Wq']).reshape(P, -1),
        'b2': np.stack([f['L2_xattn_bq'].reshape(C, P).T, f['L2_xattn_bk'].reshape(C, P).T], 1).reshape(P, -1),
        'nf': np.stack([w1, w2, w3], 2).transpose(1, 0, 2, 3).reshape(NG, P, NBT * QB),
        'qkn': np.stack([f['L3_xattn_q_norm_w'], f['L3_xattn_k_norm_w']], 1),
        'mask': f['mask_1x1xSxS2_ff0'].reshape(2, P, SK).transpose(1, 0, 2).reshape(P, -1),
        'iota': (np.arange(NE, dtype=np.float32) - BIG_INDEX).reshape(1, NE).astype(np.float32),
        'w24': chunks(np.concatenate([f['L3_ffn_W_res'], f['L3_ffn_W_pre'], f['L3_ffn_W_post']]).T).reshape(P, -1),
        'bases': np.concatenate([f['L3_ffn_H_res_base'].reshape(-1), f['L3_ffn_H_pre_base'],
                                 f['L3_ffn_H_post_base']]).reshape(1, NL),
        'gate': f['L3_ffn_gate'].reshape(1, 1),
        'wbr': f['L3_ffn_W_branch'],
    }
    return {k: np.ascontiguousarray(v) for k, v in out.items()}


def kernel(**inputs):
    import concourse.bacc as _bacc
    from concourse import mybir as _mybir
    from concourse.bass_utils import run_bass_kernel_spmd as _run

    nc = _bacc.Bacc("TRN2", target_bir_lowering=False, num_devices=1)
    arrays, args = {}, []
    for name, a in lay_out(inputs).items():
        arrays[f"in_{name}"] = a
        args.append(nc.dram_tensor(f"in_{name}", a.shape, _mybir.dt.from_np(a.dtype), kind="ExternalInput").ap())
    out = nc.dram_tensor("out", (B * S, D), _mybir.dt.float32, kind="ExternalOutput").ap()
    build(nc, *args, out)
    r = _run(nc, [arrays], core_ids=[0])
    return r.results[0]["out"].reshape(B, S, D)
```

```python
import concourse.bass as bass
from concourse import mybir
from contextlib import ExitStack
import numpy as np

F32 = mybir.dt.float32
F32R = mybir.dt.float32r
U8 = mybir.dt.uint8
BF16 = mybir.dt.bfloat16
ALU = mybir.AluOpType
ACT = mybir.ActivationFunctionType
AX = mybir.AxisListType

P = 128
B, S, D = 4, 256, 512
SK = 64
T = B * S // P
C = D // P
NG, HG, DH = 8, 4, 128
HS = HG // 2
WQ = HG * DH
WG = WQ + 2 * DH
NH1, DH1, NKV1 = 32, 16, 8
HC1 = P // DH1
NE, RANK = 28, 8
ER = NE * RANK
EH = ER // 2
LORA_SCALE = 2.0
HF = 1376
NF = -(-HF // P)
QB = 64
NB3 = D * HF // P // QB
NBU = NF * D // QB // NG
NBT = 3 * NBU
NFW = NF * D
NS = 4
NL = NS * NS + 2 * NS
SK_UNROLL = 8
SK_LINEAR = 24
EPS = 1e-5
EPS_RMS = 1.1920929e-07
BIG_INDEX = 1024.0
HALF_MAX = 1.7e38

CODE = [np.float32(v) for v in (
    -1.0, -0.6961928009986877, -0.5250730514526367, -0.39491748809814453, -0.28444138169288635,
    -0.18477343022823334, -0.09105003625154495, 0.0, 0.07958029955625534, 0.16093020141124725,
    0.24611230194568634, 0.33791524171829224, 0.44070982933044434, 0.5626170039176941,
    0.7229568362236023, 1.0)]
_BOUNDS = [float(np.float32((lo + hi) * np.float32(0.5))) for lo, hi in zip(CODE, CODE[1:])]
UP = [(_BOUNDS[i], float(np.float32(CODE[i + 1] - CODE[i]))) for i in range(7, 15)]
DOWN = [(_BOUNDS[i], float(np.float32(CODE[i] - CODE[i + 1]))) for i in range(6, -1, -1)]
FAR = 2.0 ** 100


def build(nc, x_d, ctxT_d, ctxB_d, gx_d, gf_d, wl_d, ol_d, w4_d, sc4_d, ze4_d, l1wqv_d, l1kr_d, l1o_d,
          lnw_d, l1f_d, lb_d, l2k_d, l2q_d, b2_d, nf_d, qkn_d, mask_d, iota_d, w24_d, bases_d, gate_d, wbr_d, out_d):
    scratch = nc.dram_tensor("dequantised", [P, 3, NFW], F32, kind="Internal").ap()
    ctx = ExitStack()
    with ctx:
        def sb(name, shape, dt=F32):
            return ctx.enter_context(nc.sbuf_tensor(name, shape, dt))

        def sem(name):
            return ctx.enter_context(nc.semaphore(name))

        X = sb("X", [P, T, D])
        HN = sb("HN", [P, 2, D])
        HTh = sb("HTh", [P, C, T * P], F32R)
        HTl = sb("HTl", [P, C, T * P], F32R)
        CT = sb("CT", [P, C, B * SK])
        CTh = sb("CTh", [P, C, B * SK], F32R)
        CTl = sb("CTl", [P, C, B * SK], F32R)
        ident = sb("ident", [P, P])
        ones = sb("ones", [P, P])
        gates = sb("gates", [P, 2, 4])
        tg = sb("tg", [P, 2, 4])
        st = sb("st", [P, T, 6])
        mv = sb("mv", [P, T, 2])
        veps = sb("veps", [P, 2, T])
        rstd = sb("rstd", [P, T])
        rms = sb("rms", [P, T])
        half = sb("half", [P, T])
        sm = sb("sm", [P, 4, 32])
        qkn = sb("qkn", [P, 2])
        qkw = sb("qkw", [P, 1])
        lnw = sb("lnw", [P, D])
        WR = sb("WR", [P, C * WG])
        Wh = sb("Wh", [P, C * WG], F32R)
        Wl = sb("Wl", [P, C * WG], F32R)
        OR = sb("OR", [P, 4 * D])
        Oh = sb("Oh", [P, 4 * D], F32R)
        Ol = sb("Ol", [P, 4 * D], F32R)
        qT = sb("qT", [P, 2, HG * S])
        s_sb = sb("s_sb", [P, 2, 2 * D])
        PT = sb("PT", [P, 2 * D])
        OTh = sb("OTh", [P, HG * S], F32R)
        OTl = sb("OTl", [P, HG * S], F32R)
        v_sb = sb("v_sb", [P, B, DH])
        kT = sb("kT", [P, B * SK])
        kvs = sb("kvs", [P, 2, 2 * DH])
        AR = sb("AR", [P, 5 * NBT * QB + NBT * QB // 2])
        PS = ctx.enter_context(nc.psum_tensor("PS", [P, 8, 512], F32))

        def bank(i, n=1):
            return PS[:, i, :] if n == 1 else PS[:, i:i + n, :].rearrange("p a b -> p (a b)")

        block = ctx.enter_context(nc.Block())

        x_in, consts_in, ctx_in = sem("x_in"), sem("consts_in"), sem("ctx_in")
        pool_consts, gates_ready, ctx_hi, ctx_split = sem("pool_consts"), sem("gates_ready"), sem("ctx_hi"), sem("ctx_split")
        stats, rstd_ready, hn_ready = sem("stats"), sem("rstd_ready"), sem("hn_ready")
        hn_turned, hi_ready, lo_ready = sem("hn_turned"), sem("hi_ready"), sem("lo_ready")
        out_stored = sem("out_stored")

        class Sems:

            def __init__(self, stage, names):
                self.all = {n: sem(f"{stage}_{n}") for n in names.split()}

            def __getitem__(self, n):
                return self.all[n]

        ATT = ("w_in o_in w_hi o_hi w_split o_split kv_mm kn_ready v_ready kt_mm kt_ready q_mm qT_ready s_mm s_read "
               "shifted exps probs t_mm pt_ready pv_mm ohi olo wo_mm acc ksq krs qrs_in qrs "
               "kn_in mask_in nf_in nf_v nf_mask nf_added nf_rise nf_summed nf_out nf_stored nf_free nf_norm")
        A = Sems("att", ATT)
        F0 = Sems("f0", "w_in packed w_hi split mm acc")
        A1 = Sems("a1", "w_in kr_in o_in w_hi o_hi w_split o_split kr_mm kr_sb kr_out v_out q_mm qT_ready s_mm "
                        "shifted exps probs t_mm pt_ready pv_mm ohi olo wo_mm acc")
        F1 = Sems("f1", "w_in b_in w_hi split lg_mm lg_ready gap egap h_ready t_mm ht_ready mm acc")
        A2 = Sems("a2", "k_in q_in b_in k_mm kt_ready m_mm mhi mlo s_mm shifted exps probs t_mm "
                        "pt_ready mm acc")
        F2 = Sems("f2", "in0 in1 t_mm whi wlo g_mm u_mm silu act ahi alo mm acc")
        F3 = Sems("f3", "w_in w_hi wlo lg_mm to_act from_act pre preT_mm preT y_mm y_sb post posted mixed done done_pool")

        def mm3(out, ah, al, bh, bl, first, last_):
            nc.tensor.matmul(out, ah, bh, start=first, stop=False)
            nc.tensor.matmul(out, ah, bl, start=False, stop=False)
            return nc.tensor.matmul(out, al, bh, start=False, stop=last_)

        def hn_of(n, t):
            if n == 7:
                return AR[:, t * D:(t + 1) * D]
            return HN[:, t % 2, :]

        PAIRS = T // 2
        NORM_BANKS = {0: (5, 6), 1: (0, 1), 2: (5, 6), 3: (0, 1), 4: (0, 1), 5: (4, 7), 6: (5, 6), 7: (0, 1)}

        def norm_bank(n, t):
            return bank(NORM_BANKS[n][t % 2])

        def dve_stats(dve, p):
            dve.drain()
            for t in (2 * p, 2 * p + 1):
                nc.vector.bn_stats(st[:, t, :], X[:, t, :])
            dve.drain()
            for t in (2 * p, 2 * p + 1):
                i = nc.vector.bn_aggr(mv[:, t, :], st[:, t, :])
            i.then_inc(stats, 1)

        def dve_norm(dve, n, given=0):
            if n == 0:
                dve.wait_ge(x_in, 16)
            if n == 2:
                dve.wait_ge(consts_in, CONSTS)

            def stat(p):
                if p >= given:
                    dve_stats(dve, p)

            def low(t):
                dve.wait_ge(hi_ready, T * n + t + 1)
                cols = slice(t * P, (t + 1) * P)
                nc.vector.tensor_tensor(HTl[:, :, cols], norm_bank(n, t).rearrange("p (c k) -> p c k", c=C),
                                        HTh[:, :, cols].bitcast(F32), ALU.subtract).then_inc(lo_ready, 1)

            def scaled(t):
                if t >= 2 and n != 7:
                    dve.wait_ge(hn_turned, T * n + t - 1)
                i = nc.vector.tensor_scalar(hn_of(n, t), X[:, t, :], mv[:, t, 0:1], rstd[:, t:t + 1],
                                            ALU.subtract, ALU.mult)
                if n == 2:
                    dve.drain()
                    i = nc.vector.tensor_tensor(hn_of(n, t), hn_of(n, t), lnw[:], ALU.mult)
                i.then_inc(hn_ready, 1)
            stat(0)
            stat(1)
            for p in range(PAIRS):
                dve.wait_ge(rstd_ready, PAIRS * n + p + 1)
                if n == 2:
                    two = slice(2 * p, 2 * p + 2)
                    nc.vector.tensor_tensor(rstd[:, two], rstd[:, two], rms[:, two], ALU.mult)
                    dve.drain()
                for t in (2 * p, 2 * p + 1):
                    scaled(t)
                    if t >= 2:
                        low(t - 2)
                if p + 2 < PAIRS:
                    stat(p + 2)
            low(T - 2)
            low(T - 1)

        def pool_norm(pool, n, halfway=None):
            for p in range(PAIRS):
                if p == 2 and halfway is not None:
                    halfway()
                two = slice(2 * p, 2 * p + 2)
                pool.wait_ge(stats, PAIRS * n + p + 1)
                nc.gpsimd.tensor_scalar(veps[:, 0, two], mv[:, two, 1], EPS, None, ALU.add)
                pool.drain()
                i = nc.gpsimd.tensor_tensor(rstd[:, two], veps[:, 0, two], half[:, two], ALU.pow)
                if n in (2, 7):
                    pool.drain()
                    nc.gpsimd.tensor_tensor(veps[:, 1, two], mv[:, two, 1], rstd[:, two], ALU.mult)
                    pool.drain()
                    nc.gpsimd.tensor_tensor(veps[:, 1, two], veps[:, 1, two], rstd[:, two], ALU.mult)
                    pool.drain()
                    nc.gpsimd.tensor_scalar(veps[:, 1, two], veps[:, 1, two], EPS if n == 2 else EPS_RMS, None,
                                            ALU.add)
                    pool.drain()
                    i = nc.gpsimd.tensor_tensor(rms[:, two], veps[:, 1, two], half[:, two], ALU.pow)
                i.then_inc(rstd_ready, 1)

        def pe_norm(pe, n, work=None):
            if n == 0:
                pe.wait_ge(pool_consts, 1)
            for t in range(T + 2):
                if t >= 2:
                    pe.wait_ge(lo_ready, T * n + t - 1)
                if t < T:
                    pe.wait_ge(hn_ready, T * n + t + 1)
                    for c in range(C):
                        i = nc.tensor.transpose(norm_bank(n, t)[:, c * P:(c + 1) * P],
                                                hn_of(n, t)[:, c * P:(c + 1) * P], ident[:])
                    i.then_inc(hn_turned, 1)
                if t >= 2 and work is not None:
                    work(t - 2)

        def act_norm(act, n):
            for t in range(T):
                act.wait_ge(hn_turned, T * n + t + 1)
                nc.scalar.copy(HTh[:, :, t * P:(t + 1) * P], norm_bank(n, t).rearrange("p (c k) -> p c k", c=C))\
                    .then_inc(hi_ready, 1)

        def w3d(t_, lo, hi_):
            return t_[:].rearrange("p (c n) -> p c n", c=C)[:, :, lo:hi_]

        W_PIECES = ((WQ, WG), (0, 2 * DH), (2 * DH, WQ))
        N_NF = NBT * QB
        nf_in, nf_below, nf_m0, nf_m1, nf_above = (AR[:, k * N_NF:(k + 1) * N_NF] for k in range(5))
        nf_far = AR[:, 5 * N_NF:5 * N_NF + N_NF // 2].bitcast(BF16)
        NUP, NDOWN = len(UP), len(DOWN)

        def sp_attention(sp, a, l0):
            g0 = 0 if l0 else NG

            def load_w(g):
                sp.dma_start(WR[:], wl_d[g]).then_inc(a["w_in"], 16)

            def load_o(g):
                sp.dma_start(OR[:], ol_d[g]).then_inc(a["o_in"], 16)

            def load_nf(g):
                sp.dma_start(nf_in, nf_d[g]).then_inc(a["nf_in"], 16)

            def store(g, last_turn=False):
                sp.wait_ge(a["nf_out"], g + 2)
                if last_turn:
                    sp.dma_start(KR_W, l1kr_d).then_inc(A1["kr_in"], 16)
                n = NBU * QB
                sp.dma_start(scratch[:, :, bass.ds(g * n, n)], nf_below.rearrange("p (w n) -> p w n", w=3))\
                    .then_inc(a["nf_stored"], 16)
                sp.wait_ge(a["nf_stored"], g * 16 + 16)
                sp.sem_inc(a["nf_free"], 1)
            if not l0:
                sp.wait_ge(F2["t_mm"], 3 * NF)
            load_w(g0)
            load_o(g0)
            if l0:
                load_nf(0)
                sp.sem_inc(a["nf_free"], 1)
            else:
                sp.dma_start(mask_sb, mask_d).then_inc(a["mask_in"], 16)
            sp.wait_ge(a["w_split"], 3 * g0 + 3)
            load_w(g0 + 1)

            def turn(g, more):
                sp.wait_ge(a["o_split"], g)
                load_o(g)
                if more:
                    sp.wait_ge(a["w_split"], g * 3 + 3)
                    load_w(g + 1)
                if l0:
                    sp.wait_ge(a["nf_norm"], g)
                    load_nf(g)
                    store(g - 1)
            with sp.Fori(g0 + 1, g0 + NG - 1) as g:
                turn(g, True)
            turn(g0 + NG - 1, False)
            if l0:
                sp_f0(sp)
                store(NG - 1, True)

        def pool_low(hi, lo, raw):
            return nc.gpsimd.tensor_tensor(lo, raw, hi.bitcast(F32), ALU.subtract)

        def pool_attention(pool, a, l0):
            g0 = 0 if l0 else NG

            def split_w(g):
                for k, (lo, hi_) in enumerate(W_PIECES):
                    pool.wait_ge(a["w_hi"], g * 3 + (k + 1))
                    pool_low(w3d(Wh, lo, hi_), w3d(Wl, lo, hi_), w3d(WR, lo, hi_)).then_inc(a["w_split"], 1)

            def split_o(g):
                pool.wait_ge(a["o_hi"], g + 1)
                pool_low(Oh[:], Ol[:], OR[:]).then_inc(a["o_split"], 1)

            def key_scale(g):
                pool.wait_ge(a["ksq"], g - (NG - 1))
                ks = sm[:, 0, 0:2]
                nc.gpsimd.tensor_tensor(ks, ks, tiny[:, 0:2], ALU.add)
                pool.drain()
                nc.gpsimd.tensor_tensor(sm[:, 0, 2:4], ks, half[:, 0:2], ALU.pow).then_inc(a["krs"], 1)

            def query_scale(g, b):
                pool.wait_ge(a["qrs_in"], g * B + (b + 1 - NG * B))
                qs = sm[:, 0, 8:16]
                nc.gpsimd.tensor_tensor(qs, qs, tiny[:, 8:16], ALU.add)
                pool.drain()
                nc.gpsimd.tensor_tensor(sm[:, 0, 16:24], qs, half[:], ALU.pow).then_inc(a["qrs"], 1)

            def add_below(g, ks):
                for k in ks:
                    pool.wait_ge(a["nf_mask"], g * NDOWN + (k + 1))
                    if k == 1:
                        pool.wait_ge(a["nf_free"], g + 1)
                    nc.gpsimd.tensor_tensor(nf_below, nf_below if k > 1 else nf_m0, nf_m1 if k % 2 else nf_m0,
                                            ALU.add).then_inc(a["nf_added"], 1)
                    pool.drain()

            def nf_finish(g):
                pool.wait_ge(a["nf_summed"], g * NUP + (NUP + 1))
                nc.gpsimd.tensor_tensor(nf_below, nf_below, nf_above, ALU.add)
                pool.drain()
                v = nf_below.rearrange("p (n q) -> p n q", q=QB)
                nc.gpsimd.tensor_tensor(v, v, absmax[:].unsqueeze(2).to_broadcast([P, NBT, QB]),
                                        ALU.mult).then_inc(a["nf_out"], 1)
            if l0:
                pool.drain().then_inc(a["nf_added"], 1)
                pool.drain().then_inc(a["nf_out"], 1)
            split_w(g0)
            if not l0:
                pool_norm(pool, 6)
                key_scale(g0)
            split_o(g0)
            if not l0:
                query_scale(g0, 0)
                query_scale(g0, 1)

            def turn(g, more):
                if not l0:
                    query_scale(g, 2)
                if more:
                    split_w(g + 1)
                if not l0:
                    query_scale(g, 3)
                    if more:
                        key_scale(g + 1)
                        query_scale(g, 4)
                        query_scale(g, 5)
                else:
                    add_below(g, range(1, NDOWN))
                    nf_finish(g)
                if more:
                    split_o(g + 1)
            with pool.Fori(g0, g0 + NG - 1) as g:
                turn(g, True)
            turn(g0 + NG - 1, False)

        tiny = sb("tiny", [P, 16])
        hm = sb("hm", [P, HC1])
        b2 = sb("b2", [P, 2 * C])
        iot = sb("iot", [P, NE])
        bases = sb("bases", [P, NL])
        gate = sb("gate", [P, 1])
        absmax = sb("absmax", [P, NBT])
        absnew = sb("absnew", [P, NBT])
        rabs = sb("rabs", [P, NBT])
        nf_bias = sb("nf_bias", [P, NUP])

        mask_sb = AR[:, 2 * HG * S:2 * HG * S + 2 * SK]

        def pe_attention(pe, a, l0):
            g0 = 0 if l0 else NG

            def project_kv(g):
                pe.wait_ge(a["w_split"], g * 3 + 1)
                for j in range(2):
                    for c in range(C):
                        rows = slice(j * P, (j + 1) * P)
                        i = mm3(bank(4)[:, j * 256:(j + 1) * 256], CTh[:, c, rows], CTl[:, c, rows],
                                w3d(Wh, WQ, WG)[:, c], w3d(Wl, WQ, WG)[:, c], c == 0, c == C - 1)
                i.then_inc(a["kv_mm"], 1)

            def turn_k(g):
                if l0:
                    pe.wait_ge(a["kn_in"], g + 1)
                else:
                    pe.wait_ge(a["kn_ready"], g - (NG - 1))
                first_of_all = l0 and isinstance(g, int)
                pe.wait_ge(a["acc"], 1 if first_of_all else g * 2 * B - 3)
                for j in range(2):
                    i = nc.tensor.transpose(bank(7)[:, j * P:(j + 1) * P], kvs[:, j, 0:DH], ident[:])
                i.then_inc(a["kt_mm"], 1)

            def project_q(g, b, first=False):
                u = g * B + b
                for pr in range(HS):
                    if b % B == 0:
                        pe.wait_ge(a["w_split"], (g + b // B) * 3 + (2 + pr))
                    if not first:
                        pe.wait_ge(a["qT_ready"], g * 2 * B + (2 * b - 1 + pr))
                    if not l0 and pr == 1 and not first:
                        pe.wait_ge(a["qrs_in"], g * B + (b - NG * B))
                    for hh in range(2):
                        h = 2 * pr + hh
                        for c in range(C):
                            tok = slice((b % B) * S, (b % B + 1) * S)
                            i = mm3(bank(pr)[:, hh * S:(hh + 1) * S], w3d(Wh, h * DH, (h + 1) * DH)[:, c],
                                    w3d(Wl, h * DH, (h + 1) * DH)[:, c], HTh[:, c, tok], HTl[:, c, tok],
                                    c == 0, c == C - 1)
                    i.then_inc(a["q_mm"], 1)

            def scores(g, b):
                pe.wait_ge(a["qT_ready"], g * 2 * B + (2 * b + 2))
                if b % B == 0:
                    pe.wait_ge(a["kt_ready"], g + (b // B + 1))
                pe.wait_ge(a["s_read"], g * B + (b + 1))
                if not l0:
                    for tt in range(2):
                        for h in range(HG):
                            nc.tensor.matmul(bank(1)[:, tt * HG + h:tt * HG + h + 1],
                                             qsq(b)[:, h * S + tt * P:h * S + tt * P + P], ones[:, 0:1],
                                             start=True, stop=True)
                for tt in range(2):
                    for h in range(HG):
                        col = (tt * HG + h) * SK
                        i = nc.tensor.matmul(bank(2)[:, col:col + SK],
                                             qT[:, b % 2, h * S + tt * P:h * S + tt * P + P],
                                             kT[:, (b % B) * SK:(b % B + 1) * SK], start=True, stop=True)
                i.then_inc(a["s_mm"], 1)

            def turn_p(g, b, more=True):
                pe.wait_ge(a["probs"], g * B + (b + 1))
                if more and b == 2:
                    pe.wait_ge(a["kn_in"], g + 2)
                for pr in range(HS):
                    for tt in range(2):
                        i = nc.tensor.transpose(
                            bank(4)[:, (pr * 2 + tt) * P:(pr * 2 + tt + 1) * P],
                            s_sb[:, b % 2, tt * 256 + pr * P:tt * 256 + (pr + 1) * P], ident[:])
                i.then_inc(a["t_mm"], 1)

            def weigh(g, b):
                pe.wait_ge(a["pt_ready"], g * B + (b + 1))
                if b % B == 0:
                    pe.wait_ge(a["v_ready"], g + (b // B + 1))
                for h in range(HG):
                    half_ = slice(SK * (h % 2), SK * (h % 2 + 1))
                    i = nc.tensor.matmul(bank(5 + h % 2)[:, (h // 2) * S:(h // 2 + 1) * S],
                                         v_sb[half_, b % B, :], PT[half_, (h // 2) * S:(h // 2 + 1) * S],
                                         start=True, stop=True)
                i.then_inc(a["pv_mm"], 1)

            def project_o(g, b):
                pe.wait_ge(a["olo"], g * B + (b + 1))
                if b % B == 0:
                    pe.wait_ge(a["o_split"], g + 1)
                for tt in range(2):
                    pe.wait_ge(a["acc"], g * 2 * B + (2 * b + tt + 1))
                    for h in range(HG):
                        tok = slice(h * S + tt * P, h * S + tt * P + P)
                        i = mm3(bank(7 if tt == 0 else 3), OTh[:, tok], OTl[:, tok],
                                Oh[:, h * D:(h + 1) * D], Ol[:, h * D:(h + 1) * D], h == 0, h == HG - 1)
                    i.then_inc(a["wo_mm"], 1)

            def first_products(t):
                if t == (T - 1 if l0 else 1):
                    if l0:
                        pe.wait_ge(ctx_split, 1)
                    project_kv(g0)
                    project_q(g0, 0, True)
            pe_norm(pe, 0 if l0 else 6, first_products)
            turn_k(g0)
            scores(g0, 0)
            project_q(g0, 1)
            scores(g0, 1)
            project_q(g0, 2)
            turn_p(g0, 0)
            weigh(g0, 0)

            def turn(g, more):
                scores(g, 2)
                project_q(g, 3)
                turn_p(g, 1)
                project_o(g, 0)
                weigh(g, 1)
                scores(g, 3)
                if more:
                    project_kv(g + 1)
                    project_q(g, 4)
                turn_p(g, 2, more)
                project_o(g, 1)
                weigh(g, 2)
                if more:
                    turn_k(g + 1)
                    scores(g, 4)
                    project_q(g, 5)
                turn_p(g, 3)
                project_o(g, 2)
                weigh(g, 3)
                if more:
                    scores(g, 5)
                    project_q(g, 6)
                    turn_p(g, 4)
                project_o(g, 3)
                if more:
                    weigh(g, 4)
            with pe.Fori(g0, g0 + NG - 1) as g:
                turn(g, True)
            turn(g0 + NG - 1, False)

        def qsq(b):
            return AR[:, (b % 2) * HG * S:(b % 2 + 1) * HG * S]

        def act_attention(act, a, l0):
            g0 = 0 if l0 else NG

            def high_w(g):
                act.wait_ge(a["w_in"], g * 16 + 16)
                for lo, hi_ in W_PIECES:
                    nc.scalar.copy(w3d(Wh, lo, hi_), w3d(WR, lo, hi_)).then_inc(a["w_hi"], 1)

            def high_o(g):
                act.wait_ge(a["o_in"], g * 16 + 16)
                nc.scalar.copy(Oh[:], OR[:]).then_inc(a["o_hi"], 1)

            def keys_values(g):
                act.wait_ge(a["kv_mm"], g + 1)
                nc.scalar.copy(kvs[:], bank(4).rearrange("p (j n) -> p j n", j=2)).then_inc(a["kn_in"], 1)

            def keys(g):
                act.wait_ge(a["kt_mm"], g + 1)
                nc.scalar.activation(kT[:], bank(7)[:, 0:B * SK], ACT.Copy, scale=1.0 if l0 else qkw[:, 0:1])\
                    .then_inc(a["kt_ready"], 1)

            def values(g):
                for par in range(2):
                    for hf in range(2):
                        i = nc.scalar.copy(v_sb[SK * hf:SK * (hf + 1), par::2, :],
                                           kvs[SK * par:SK * (par + 1), :, DH:2 * DH])
                i.then_inc(a["v_ready"], 1)

            def queries(g, b):
                for pr in range(HS):
                    act.wait_ge(a["q_mm"], g * 2 * B + (2 * b + pr + 1))
                    cols = slice(pr * 2 * S, (pr + 1) * 2 * S)
                    if not l0:
                        nc.scalar.square(qsq(b)[:, cols], bank(pr))
                    nc.scalar.copy(qT[:, b % 2, cols], bank(pr)).then_inc(a["qT_ready"], 1)

            def exps(g, b):
                act.wait_ge(a["shifted"], g * B + (b + 1))
                s = s_sb[:, b % 2, 0:512]
                nc.scalar.activation(s, s, ACT.Exp, scale=float(DH) ** -0.5 if l0 else 1.0).then_inc(a["exps"], 1)

            def probs_t(g, b):
                act.wait_ge(a["t_mm"], g * B + (b + 1))
                nc.scalar.copy(PT[:, 0:512], bank(4)).then_inc(a["pt_ready"], 1)

            def heads(g, b):
                act.wait_ge(a["pv_mm"], g * B + (b + 1))
                for par in range(2):
                    i = nc.scalar.copy(OTh[:].rearrange("p (r q s) -> p q r s", q=2, s=S)[:, par],
                                       bank(5 + par).rearrange("p (r s) -> p r s", s=S))
                i.then_inc(a["ohi"], 1)

            def far_above(g, k):
                if l0:
                    if k == 1:
                        act.wait_ge(a["nf_v"], g + 1)
                    act.wait_ge(a["nf_summed"], g * NUP + (k + 1))
                    nc.scalar.activation(nf_far, nf_in, ACT.Relu, scale=FAR, bias=nf_bias[:, k:k + 1])\
                        .then_inc(a["nf_rise"], 1)
            if not l0:
                act.wait_ge(F2["mm"], T * NF)
            high_w(g0)
            if not l0:
                act_norm(act, 6)
            keys_values(g0)
            queries(g0, 0)
            keys(g0)
            values(g0)
            high_o(g0)
            queries(g0, 1)
            exps(g0, 0)
            queries(g0, 2)
            probs_t(g0, 0)
            exps(g0, 1)
            heads(g0, 0)

            def turn(g, more):
                queries(g, 3)
                far_above(g, 1)
                if more:
                    high_w(g + 1)
                probs_t(g, 1)
                exps(g, 2)
                far_above(g, 2)
                heads(g, 1)
                far_above(g, 3)
                if more:
                    keys_values(g + 1)
                    queries(g, 4)
                probs_t(g, 2)
                exps(g, 3)
                far_above(g, 4)
                heads(g, 2)
                if more:
                    keys(g + 1)
                far_above(g, 5)
                if more:
                    queries(g, 5)
                probs_t(g, 3)
                if more:
                    exps(g, 4)
                far_above(g, 6)
                heads(g, 3)
                if more:
                    values(g + 1)
                far_above(g, 7)
                if more:
                    queries(g, 6)
                    probs_t(g, 4)
                    exps(g, 5)
                    act.wait_ge(a["wo_mm"], g * 2 * B + 2 * B)
                    high_o(g + 1)
                    heads(g, 4)
            with act.Fori(g0, g0 + NG - 1) as g:
                turn(g, True)
            turn(g0 + NG - 1, False)

        def softmax_shift(dve, out, src, n, w, stat):
            m = stat[:, 0:n]
            nc.vector.tensor_reduce(m, src.rearrange("p (n w) -> p n w", w=w), AX.X, ALU.max)
            dve.drain()
            return nc.vector.tensor_tensor(out.rearrange("p (n w) -> p n w", w=w),
                                           src.rearrange("p (n w) -> p n w", w=w),
                                           m.unsqueeze(2).to_broadcast([P, n, w]), ALU.subtract)

        def softmax_norm(dve, buf, n, w, stat):
            v = buf.rearrange("p (n w) -> p n w", w=w)
            nc.vector.reduce_sum(stat[:, 0:n], v, AX.X)
            dve.drain()
            nc.vector.reciprocal(stat[:, 0:n], stat[:, 0:n])
            dve.drain()
            return nc.vector.tensor_tensor(v, v, stat[:, 0:n].unsqueeze(2).to_broadcast([P, n, w]), ALU.mult)

        def dve_attention(dve, a, l0):
            g0 = 0 if l0 else NG
            li = 0 if l0 else 3

            def key_norm(g):
                dve.wait_ge(a["kn_in"], g + 1)
                for j in range(2):
                    nc.vector.tensor_tensor(s_sb[:, 1, 512 + j * P:512 + (j + 1) * P], kvs[:, j, 0:DH],
                                            kvs[:, j, 0:DH], ALU.mult)
                dve.drain()
                nc.vector.reduce_sum(sm[:, 0, 4:6], s_sb[:, 1, 512:768].rearrange("p (j n) -> p j n", j=2), AX.X)
                dve.drain()
                nc.vector.tensor_scalar(sm[:, 0, 0:2], sm[:, 0, 4:6], 1.0 / DH, None, ALU.mult)\
                    .then_inc(a["ksq"], 1)
                dve.wait_ge(a["krs"], g - (NG - 1))
                for j in range(2):
                    i = nc.vector.tensor_scalar(kvs[:, j, 0:DH], kvs[:, j, 0:DH], sm[:, 0, 2 + j:3 + j], None,
                                                ALU.mult)
                i.then_inc(a["kn_ready"], 1)

            def nf_start(g):
                dve.wait_ge(a["nf_in"], g * 16 + 16)
                blocks = nf_in.rearrange("p (n q) -> p n q", q=QB)
                nc.vector.tensor_reduce(absnew[:], blocks, AX.X, ALU.max, apply_absolute_value=True)
                dve.drain()
                nc.vector.scalar_tensor_tensor(rabs[:], absnew[:], 0.0, absnew[:], ALU.is_equal, ALU.add)
                dve.drain()
                nc.vector.reciprocal(rabs[:], rabs[:])
                dve.drain()
                nc.vector.tensor_tensor(blocks, blocks, rabs[:].unsqueeze(2).to_broadcast([P, NBT, QB]), ALU.mult)
                dve.drain().then_inc(a["nf_v"], 1)

            def up(g, k):
                if not l0:
                    return
                bound, rise = UP[k]
                if k == 0:
                    dve.wait_ge(a["nf_out"], g + 1)
                    nc.vector.tensor_copy(absmax[:], absnew[:])
                    nc.vector.tensor_scalar(nf_above, nf_in, bound, rise, ALU.is_gt, ALU.mult)\
                        .then_inc(a["nf_summed"], 1)
                else:
                    dve.drain()
                    dve.wait_ge(a["nf_rise"], g * (NUP - 1) + k)
                    nc.vector.scalar_tensor_tensor(nf_above, nf_far, rise, nf_above, ALU.min, ALU.add)\
                        .then_inc(a["nf_summed"], 1)

            def down(g, k):
                if l0:
                    dve.wait_ge(a["nf_added"], g * (NDOWN - 1) + (1 if k < 2 else max(k - 1, 2)))
                    bound, fall = DOWN[k]
                    nc.vector.tensor_scalar(nf_m1 if k % 2 else nf_m0, nf_in, bound, fall, ALU.is_le, ALU.mult)\
                        .then_inc(a["nf_mask"], 1)

            def shift(g, b):
                dve.wait_ge(a["s_mm"], g * B + (b + 1))
                s = s_sb[:, b % 2, 0:512]
                src = bank(2)
                if not l0:
                    nc.vector.tensor_copy(sm[:, 0, 8:16], bank(1)[:, 0:8]).then_inc(a["qrs_in"], 1)
                    dve.wait_ge(a["qrs"], g * B + (b + 1 - NG * B))
                    nc.vector.tensor_tensor(s.rearrange("p (n w) -> p n w", w=SK),
                                            src.rearrange("p (n w) -> p n w", w=SK),
                                            sm[:, 0, 16:24].unsqueeze(2).to_broadcast([P, 8, SK]), ALU.mult)\
                        .then_inc(a["s_read"], 1)
                    dve.drain()
                    s4 = s.rearrange("p (t h k) -> p t h k", t=2, h=HG)
                    nc.vector.tensor_tensor(s4, s4, mask_sb.rearrange("p (t k) -> p t k", t=2).unsqueeze(2)
                                            .to_broadcast([P, 2, HG, SK]), ALU.add)
                    dve.drain()
                    softmax_shift(dve, s, s, 8, SK, sm[:, 1, :]).then_inc(a["shifted"], 1)
                else:
                    softmax_shift(dve, s, src, 8, SK, sm[:, 1, :]).then_inc(a["shifted"], 1)
                    dve.drain().then_inc(a["s_read"], 1)

            def norm(g, b):
                dve.wait_ge(a["exps"], g * B + (b + 1))
                softmax_norm(dve, s_sb[:, b % 2, 0:512], 8, SK, sm[:, 2, :]).then_inc(a["probs"], 1)

            def low(g, b):
                dve.wait_ge(a["ohi"], g * B + (b + 1))
                for par in range(2):
                    v = [o[:].rearrange("p (r q s) -> p q r s", q=2, s=S)[:, par] for o in (OTh, OTl)]
                    i = nc.vector.tensor_tensor(v[1], bank(5 + par).rearrange("p (r s) -> p r s", s=S),
                                                v[0].bitcast(F32), ALU.subtract)
                i.then_inc(a["olo"], 1)

            def add(g, b):
                for tt in range(2):
                    dve.wait_ge(a["wo_mm"], g * 2 * B + (2 * b + tt + 1))
                    xt = X[:, 2 * b + tt, :]
                    nc.vector.scalar_tensor_tensor(xt, bank(7 if tt == 0 else 3), tg[:, 0, li:li + 1], xt,
                                                   ALU.mult, ALU.add).then_inc(a["acc"], 1)
            if l0:
                for _ in range(2):
                    dve.drain().then_inc(a["acc"], 1)
                dve.drain().then_inc(a["s_read"], 1)
                dve.drain().then_inc(a["nf_summed"], 1)
                nf_start(0)
            else:
                dve.wait_ge(a["mask_in"], 16)
                nc.vector.tensor_tensor(qkw[:], qkn[:, 0:1], qkn[:, 1:2], ALU.mult)
                dve.drain()
                key_norm(g0)
            shift(g0, 0)
            norm(g0, 0)
            shift(g0, 1)
            norm(g0, 1)
            low(g0, 0)

            def nf_done():
                if l0:
                    dve.drain().then_inc(a["nf_norm"], 1)

            def turn(g, more):
                shift(g, 2)
                up(g, 0)
                up(g, 1)
                down(g, 0)
                norm(g, 2)
                up(g, 2)
                down(g, 1)
                add(g, 0)
                if not more:
                    dve_stats(dve, 0)
                low(g, 1)
                shift(g, 3)
                if more and not l0:
                    key_norm(g + 1)
                up(g, 3)
                down(g, 2)
                norm(g, 3)
                up(g, 4)
                down(g, 3)
                add(g, 1)
                low(g, 2)
                if not more:
                    dve_stats(dve, 1)
                if more:
                    shift(g, 4)
                up(g, 5)
                down(g, 4)
                down(g, 5)
                if more:
                    norm(g, 4)
                up(g, 6)
                down(g, 6)
                add(g, 2)
                low(g, 3)
                if not more:
                    dve_stats(dve, 2)
                if more:
                    shift(g, 5)
                up(g, 7)
                nf_done()
                if l0 and not more:
                    dve_f0_dequant(dve)
                if more:
                    norm(g, 5)
                add(g, 3)
                if more:
                    if l0:
                        nf_start(g + 1)
                    low(g, 4)
                dve.drain()
            with dve.Fori(g0, g0 + NG - 1) as g:
                turn(g, True)
            turn(g0 + NG - 1, False)

        F0_BANKS = (5, 7, 3)

        def pe_f0(pe):
            def product(t):
                if t == 0:
                    pe.wait_ge(F0["split"], 1)
                    pe.wait_ge(A["acc"], 2 * B * NG + 2)
                if t >= 3:
                    pe.wait_ge(F0["acc"], t - 2)
                for c in range(C):
                    tok = slice(t * P, (t + 1) * P)
                    i = mm3(bank(F0_BANKS[t % 3]), HTh[:, c, tok], HTl[:, c, tok], Oh[:, c * D:(c + 1) * D],
                            Ol[:, c * D:(c + 1) * D], c == 0, c == C - 1)
                i.then_inc(F0["mm"], 1)
                if t == 1:
                    pe_a1_keys(pe)
            pe_norm(pe, 1, lambda t: product(t) if t < 3 else None)
            for t in range(3, T):
                product(t)

        Ze = WR[:, 0:2048]
        w4_sb = WR[:, 2048:2304]
        nibbles = WR[:, 2304:2816]
        Sc = OR[:]

        def dve_f0_dequant(dve):
            dve.wait_ge(F0["w_in"], 16 * 5)
            n3 = nibbles.bitcast(U8).rearrange("p (c o) -> p c o", c=C)
            w3 = w4_sb.bitcast(U8).rearrange("p (c o) -> p c o", c=C)
            nc.vector.tensor_scalar(n3[:, :, 0:256], w3, 4, None, ALU.logical_shift_right)
            nc.vector.tensor_scalar(n3[:, :, 256:512], w3, 15, None, ALU.bitwise_and)
            dve.drain()
            nc.vector.tensor_tensor(Ze, nibbles.bitcast(U8), Ze, ALU.subtract)
            dve.drain()
            nc.vector.tensor_tensor(OR[:], Ze, Sc, ALU.mult).then_inc(F0["packed"], 1)

        def sp_f0(sp):
            sp.wait_ge(A["w_split"], 3 * NG)
            sp.dma_start(w4_sb.bitcast(mybir.dt.int32), w4_d).then_inc(F0["w_in"], 16)
            for dst, src, used in ((Ze, ze4_d, None), (Sc, sc4_d, "o_split")):
                if used:
                    sp.wait_ge(A[used], NG)
                for hf in range(2):
                    d = dst[64 * hf:64 * hf + 64, :]
                    sp.dma_start(d, src[hf:hf + 1, :].to_broadcast([64, 2048])).then_inc(F0["w_in"], 16)

        def dve_sum(dve, s, stage, kind, banks):
            for t in range(T):
                dve.wait_ge(s["mm"], t + 1)
                nc.vector.scalar_tensor_tensor(X[:, t, :], bank(banks[t % len(banks)]), tg[:, kind, stage:stage + 1],
                                               X[:, t, :], ALU.mult, ALU.add).then_inc(s["acc"], 1)
                if t % 2 and t < T - 1:
                    dve_stats(dve, t // 2)

        Kbd = AR[:, 0:C * B * HC1 * SK]
        Vbd = AR[:, C * B * HC1 * SK:C * B * HC1 * SK + B * NKV1 * 2 * DH1]
        NU = B * C

        KR_W = AR[:, 9216:9216 + C * D]
        kr = qT[:, 1, :]

        def sp_a1(sp):
            sp.wait_ge(F0["packed"], 1)
            sp.dma_start(WR[:, 0:2560], l1wqv_d).then_inc(A1["w_in"], 16)
            sp.wait_ge(F0["split"], 1)
            sp.dma_start(OR[:], l1o_d).then_inc(A1["o_in"], 16)

        def pool_a1(pool):
            pool.wait_ge(A["nf_stored"], 16 * NG)
            pool.memset(Vbd, 0.0).then_inc(A1["v_out"], 1)
            pool.wait_ge(A1["w_hi"], 1)
            pool_low(Wh[:, 0:2048], Wl[:, 0:2048], WR[:, 0:2048]).then_inc(A1["w_split"], 1)

            def spread_keys(hc):
                src = kr[:, hc * 256:(hc + 1) * 256].rearrange("p (b k) -> p b k", b=B)
                for b in range(B):
                    i = nc.gpsimd.tensor_tensor(
                        Kbd[:, u_kbd(hc, b)].rearrange("p (h k) -> p h k", h=HC1),
                        src[:, b].unsqueeze(1).to_broadcast([P, HC1, SK]),
                        hm[:].unsqueeze(2).to_broadcast([P, HC1, SK]), ALU.mult)
                i.then_inc(A1["kr_out"], 1)
            pool.wait_ge(A1["kr_sb"], 1)
            spread_keys(0)
            spread_keys(1)
            pool_norm(pool, 2)
            spread_keys(2)
            spread_keys(3)
            pool.wait_ge(A1["o_hi"], 1)
            pool_low(Oh[:], Ol[:], OR[:]).then_inc(A1["o_split"], 1)

        def u_kbd(hc, b):
            at = (hc * B + b) * HC1 * SK
            return slice(at, at + HC1 * SK)

        def pe_a1_keys(pe):
            pe.wait_ge(A1["kr_in"], 16)
            for hc in range(C):
                for c in range(C):
                    nc.tensor.matmul(bank(2 + hc // 2 * 2)[:, (hc % 2) * 256:(hc % 2 + 1) * 256],
                                     KR_W[:, c * D + hc * P:c * D + (hc + 1) * P], CT[:, c, :],
                                     start=c == 0, stop=c == C - 1)
            pe.wait_ge(A1["w_in"], 16)
            for j in range(2):
                for c in range(C):
                    i = nc.tensor.matmul(bank(6)[:, j * P:(j + 1) * P], CT[:, c, j * P:(j + 1) * P],
                                         WR[:, 2048 + c * P:2048 + (c + 1) * P], start=c == 0, stop=c == C - 1)
            i.then_inc(A1["kr_mm"], 1)

        def pe_a1(pe):
            def project_q(b, pr):
                if b:
                    pe.wait_ge(A1["qT_ready"], 2 * b - 1 + pr)
                if b >= 2 and pr == 0:
                    pe.wait_ge(A1["acc"], 2 * b - 2)
                for hh in range(2):
                    hc = 2 * pr + hh
                    for c in range(C):
                        w = slice(c * D + hc * P, c * D + (hc + 1) * P)
                        tok = slice(b * S, (b + 1) * S)
                        i = mm3(bank(pr)[:, hh * S:(hh + 1) * S], Wh[:, w], Wl[:, w], HTh[:, c, tok],
                                HTl[:, c, tok], c == 0, c == C - 1)
                i.then_inc(A1["q_mm"], 1)

            def scores(u):
                b, hc = divmod(u, C)
                if u < C:
                    pe.wait_ge(A1["kr_out"], u + 1)
                if u == 0:
                    pe.wait_ge(F0["acc"], T)
                if hc == 0:
                    pe.wait_ge(A1["qT_ready"], 2 * b + 2)
                if u:
                    pe.wait_ge(A1["shifted"], u)
                for tt in range(2):
                    i = nc.tensor.matmul(bank(2 + tt), qT[:, b % 2, hc * S + tt * P:hc * S + tt * P + P],
                                         Kbd[:, u_kbd(hc, b)], start=True, stop=True)
                i.then_inc(A1["s_mm"], 1)

            def turn_p(u):
                pe.wait_ge(A1["probs"], u + 1)
                for pr in range(4):
                    for tt in range(2):
                        i = nc.tensor.transpose(bank(4, 2)[:, (pr * 2 + tt) * P:(pr * 2 + tt + 1) * P],
                                                s_sb[:, u % 2, tt * 512 + pr * P:tt * 512 + (pr + 1) * P], ident[:])
                i.then_inc(A1["t_mm"], 1)

            def weigh(u):
                b, hc = divmod(u, C)
                pe.wait_ge(A1["pt_ready"], u + 1)
                if u:
                    pe.wait_ge(A1["olo"], u)
                for pr in range(4):
                    at = (b * NKV1 + 2 * hc + pr // 2) * 2 * DH1
                    i = nc.tensor.matmul(bank(6)[32 * pr:32 * pr + 32, 0:S], Vbd[:, at:at + 2 * DH1],
                                         PT[:, pr * S:(pr + 1) * S], start=True, stop=True)
                i.then_inc(A1["pv_mm"], 1)

            def project_o(b):
                pe.wait_ge(A1["olo"], (b + 1) * C)
                if b == 0:
                    pe.wait_ge(A1["o_split"], 1)
                for tt in range(2):
                    if b and tt == 0:
                        pe.wait_ge(A1["acc"], 2 * b - 1)
                    for hc in range(C):
                        tok = slice(hc * S + tt * P, hc * S + tt * P + P)
                        i = mm3(bank(7 if tt == 0 else 0), OTh[:, tok], OTl[:, tok], Oh[:, hc * D:(hc + 1) * D],
                                Ol[:, hc * D:(hc + 1) * D], hc == 0, hc == C - 1)
                    i.then_inc(A1["wo_mm"], 1)

            def first_products(t):
                if t == 1:
                    pe.wait_ge(A1["w_split"], 1)
                    project_q(0, 0)
                    project_q(0, 1)
            pe.wait_ge(A1["v_out"], 2)
            pe_norm(pe, 2, first_products)
            scores(0)
            for u in range(NU):
                b, at = divmod(u, C)
                if u + 1 < NU:
                    scores(u + 1)
                turn_p(u)
                if at == 0 and b:
                    if b < B - 1:
                        pe.wait_ge(A1["qT_ready"], 2 * b + 2)
                    project_o(b - 1)
                if at in (1, 2) and b < B - 1:
                    project_q(b + 1, at - 1)
                weigh(u)
            project_o(B - 1)

        def act_a1(act):
            act.wait_ge(A1["kr_mm"], 1)
            for k in range(2):
                i = nc.scalar.copy(kr[:, k * 512:(k + 1) * 512], bank(2 + 2 * k))
            i.then_inc(A1["kr_sb"], 1)
            nc.scalar.copy(Wh[:, 0:2048], WR[:, 0:2048]).then_inc(A1["w_hi"], 1)
            act.wait_ge(A1["v_out"], 1)
            V5 = Vbd.rearrange("p (b v q d) -> p b v q d", b=B, v=NKV1, q=2)
            vv = bank(6)[:, 0:256].rearrange("p (j v d) -> p j v d", j=2, v=NKV1)
            for par in range(2):
                for hf in range(2):
                    i = nc.scalar.copy(V5[SK * hf:SK * (hf + 1), par::2, :, hf, :], vv[SK * par:SK * (par + 1)])
            i.then_inc(A1["v_out"], 1)
            act_norm(act, 2)
            act.wait_ge(A1["o_in"], 16)
            nc.scalar.copy(Oh[:], OR[:]).then_inc(A1["o_hi"], 1)

            def queries(b, pr):
                act.wait_ge(A1["q_mm"], 2 * b + pr + 1)
                if b == 1 and pr == 0:
                    act.wait_ge(A1["kr_out"], C)
                nc.scalar.copy(qT[:, b % 2, pr * 512:(pr + 1) * 512], bank(pr)).then_inc(A1["qT_ready"], 1)

            def exps(u):
                act.wait_ge(A1["shifted"], u + 1)
                nc.scalar.activation(s_sb[:, u % 2, :], s_sb[:, u % 2, :], ACT.Exp, scale=float(DH1) ** -0.5)\
                    .then_inc(A1["exps"], 1)

            queries(0, 0)
            queries(0, 1)
            exps(0)
            for u in range(NU):
                b, at = divmod(u, C)
                act.wait_ge(A1["t_mm"], u + 1)
                nc.scalar.copy(PT[:], bank(4, 2)).then_inc(A1["pt_ready"], 1)
                if u + 1 < NU:
                    exps(u + 1)
                if at in (1, 2) and b < B - 1:
                    queries(b + 1, at - 1)
                act.wait_ge(A1["pv_mm"], u + 1)
                nc.scalar.copy(OTh[:, at * S:(at + 1) * S], bank(6)[:, 0:S]).then_inc(A1["ohi"], 1)

        def dve_a1(dve):
            dve_norm(dve, 2, PAIRS - 1)

            def shift(u):
                dve.wait_ge(A1["s_mm"], u + 1)
                softmax_shift(dve, s_sb[:, u % 2, :], bank(2, 2), 16, SK, sm[:, 1, :]).then_inc(A1["shifted"], 1)

            def norm(u):
                dve.wait_ge(A1["exps"], u + 1)
                softmax_norm(dve, s_sb[:, u % 2, :], 16, SK, sm[:, 2, :]).then_inc(A1["probs"], 1)

            def add(b):
                for tt in range(2):
                    dve.wait_ge(A1["wo_mm"], 2 * b + tt + 1)
                    xt = X[:, 2 * b + tt, :]
                    nc.vector.scalar_tensor_tensor(xt, bank(7 if tt == 0 else 0), tg[:, 0, 1:2], xt, ALU.mult, ALU.add)\
                        .then_inc(A1["acc"], 1)
            shift(0)
            norm(0)
            for u in range(NU):
                b, hc = divmod(u, C)
                if u + 1 < NU:
                    shift(u + 1)
                    norm(u + 1)
                if hc == 0 and b:
                    add(b - 1)
                dve.wait_ge(A1["ohi"], u + 1)
                cols = slice(hc * S, (hc + 1) * S)
                nc.vector.tensor_tensor(OTl[:, cols], bank(6)[:, 0:S], OTh[:, cols].bitcast(F32), ALU.subtract)\
                    .then_inc(A1["olo"], 1)
                if hc == 0 and b:
                    dve_stats(dve, b - 1)
            add(B - 1)

        NWF = D + NE + ER
        G = AR[:, 0:T * (NE + ER)]
        TK = AR[:, 2048:2048 + 8 * T * NE]

        def tk(i):
            return TK[:, i * T * NE:(i + 1) * T * NE]

        def sp_f1(sp):
            sp.wait_ge(A1["w_split"], 1)
            sp.wait_ge(A1["kr_mm"], 1)
            sp.dma_start(WR[:, 0:C * NWF], l1f_d).then_inc(F1["w_in"], 16)
            sp.wait_ge(A1["o_split"], 1)
            sp.dma_start(OR[0:EH, 0:2 * D], lb_d).then_inc(F1["b_in"], 16)

        def pool_f1(pool):
            pool.wait_ge(F1["w_hi"], 1)
            pool_low(Wh[:, 0:C * NWF], Wl[:, 0:C * NWF], WR[:, 0:C * NWF]).then_inc(F1["split"], 1)
            pool_norm(pool, 3)

        def wf(t_, c, lo, hi_):
            return t_[:, c * NWF + lo:c * NWF + hi_]

        def pe_f1(pe):
            def logits(t):
                if t == 0:
                    pe.wait_ge(F1["split"], 1)
                if t >= 2:
                    pe.wait_ge(F1["lg_ready"], t - 1)
                for c in range(C):
                    tok = slice(t * P, (t + 1) * P)
                    i = mm3(bank(6 + t % 2)[:, 0:NE + ER], HTh[:, c, tok], HTl[:, c, tok],
                            wf(Wh, c, D, NWF), wf(Wl, c, D, NWF), c == 0, c == C - 1)
                i.then_inc(F1["lg_mm"], 1)
            pe_norm(pe, 3, lambda t: logits(t) if t < 2 else None)
            for t in range(2, T):
                logits(t)

            def base(t):
                if t >= 4:
                    pe.wait_ge(F1["acc"], t - 3)
                for c in range(C):
                    tok = slice(t * P, (t + 1) * P)
                    mm3(bank(2 + t % 4), HTh[:, c, tok], HTl[:, c, tok], wf(Wh, c, 0, D), wf(Wl, c, 0, D),
                        c == 0, False)
            for t in range(3):
                base(t)
            pe.wait_ge(F1["h_ready"], 1)
            pe.wait_ge(F1["b_in"], 16)
            for t in range(T):
                if t == 0:
                    pe.wait_ge(F1["lg_ready"], T)
                for e in range(2):
                    at = t * (NE + ER) + NE + e * EH
                    i = nc.tensor.transpose(bank(6 + t % 2)[0:EH, e * P:(e + 1) * P], G[:, at:at + EH], ident[:])
                i.then_inc(F1["t_mm"], 1)
                if t + 3 < T:
                    base(t + 3)
                pe.wait_ge(F1["ht_ready"], t + 1)
                for e in range(2):
                    at = (t % 2) * 256 + e * P
                    i = nc.tensor.matmul(bank(2 + t % 4), PT[0:EH, at:at + P], OR[0:EH, e * D:(e + 1) * D],
                                         start=False, stop=e == 1)
                i.then_inc(F1["mm"], 1)

        def act_f1(act):
            act.wait_ge(F1["w_in"], 16)
            act.wait_ge(A1["wo_mm"], T)
            nc.scalar.copy(Wh[:, 0:C * NWF], WR[:, 0:C * NWF]).then_inc(F1["w_hi"], 1)
            act_norm(act, 3)
            for t in range(T):
                act.wait_ge(F1["lg_mm"], t + 1)
                nc.scalar.copy(G[:, t * (NE + ER):(t + 1) * (NE + ER)], bank(6 + t % 2)[:, 0:NE + ER])\
                    .then_inc(F1["lg_ready"], 1)
            act.wait_ge(F1["gap"], 1)
            nc.scalar.activation(sm[:, 0, 16:24], sm[:, 0, 16:24], ACT.Exp).then_inc(F1["egap"], 1)
            for t in range(T):
                act.wait_ge(F1["t_mm"], t + 1)
                nc.scalar.copy(PT[0:EH, (t % 2) * 256:(t % 2 + 1) * 256], bank(6 + t % 2)[0:EH, 0:256])\
                    .then_inc(F1["ht_ready"], 1)

        def dve_f1(dve):
            dve_norm(dve, 3, PAIRS - 1)
            dve.wait_ge(F1["lg_ready"], T)
            G3 = G.rearrange("p (t n) -> p t n", t=T)

            def v3(i):
                return tk(i).rearrange("p (t n) -> p t n", t=T)
            L = G3[:, :, 0:NE]
            iob = iot[:].unsqueeze(1).to_broadcast([P, T, NE])

            def col(k):
                return sm[:, 0, k * T:(k + 1) * T]

            def bc(k):
                return col(k).unsqueeze(2).to_broadcast([P, T, NE])

            def pick(src, top, at, one):
                nc.vector.tensor_reduce(col(top), src, AX.X, ALU.max)
                dve.drain()
                nc.vector.tensor_tensor(v3(5), src, bc(top), ALU.is_equal)
                dve.drain()
                nc.vector.tensor_tensor(v3(5), v3(5), iob, ALU.mult)
                dve.drain()
                nc.vector.tensor_reduce(col(at), v3(5), AX.X, ALU.min)
                dve.drain()
                nc.vector.tensor_tensor(v3(one), iob, bc(at), ALU.is_equal)
                dve.drain()
            pick(L, 0, 1, 0)
            nc.vector.tensor_scalar(tk(2), tk(0), -2.0 * HALF_MAX, HALF_MAX, ALU.mult, ALU.add)
            dve.drain()
            nc.vector.tensor_tensor(v3(2), L, v3(2), ALU.min)
            dve.drain()
            pick(v3(2), 3, 1, 1)
            nc.vector.tensor_tensor(col(2), col(3), col(0), ALU.subtract).then_inc(F1["gap"], 1)
            dve.wait_ge(F1["egap"], 1)
            nc.vector.tensor_scalar(col(0), col(2), 1.0, None, ALU.add)
            dve.drain()
            nc.vector.reciprocal(col(0), col(0))
            dve.drain()
            nc.vector.tensor_scalar(col(0), col(0), LORA_SCALE, None, ALU.mult)
            dve.drain()
            nc.vector.tensor_tensor(col(2), col(2), col(0), ALU.mult)
            dve.drain()
            nc.vector.tensor_tensor(v3(0), v3(0), bc(0), ALU.mult)
            nc.vector.tensor_tensor(v3(1), v3(1), bc(2), ALU.mult)
            dve.drain()
            nc.vector.tensor_tensor(tk(0), tk(0), tk(1), ALU.add)
            dve.drain()
            for t in range(T):
                h = G3[:, t, NE:NE + ER].rearrange("p (e r) -> p e r", r=RANK)
                i = nc.vector.tensor_tensor(h, h, v3(0)[:, t, :].unsqueeze(2).to_broadcast([P, NE, RANK]), ALU.mult)
            i.then_inc(F1["h_ready"], 1)
            dve_sum(dve, F1, 1, 1, (2, 3, 4, 5))

        CB = AR[0:SK, 0:B * D]
        KT2 = AR[:, B * D:B * D + C * B * SK]
        BK = AR[0:1, 3072:3072 + B * SK]

        def sp_a2(sp):
            sp.wait_ge(F1["split"], 1)
            sp.dma_start(WR[:, 0:2048], l2k_d).then_inc(A2["k_in"], 16)
            sp.wait_ge(F1["mm"], T)
            sp.dma_start(CB, ctxB_d.rearrange("k b n -> k (b n)")).then_inc(A2["b_in"], 16)
            sp.dma_start(OR[:], l2q_d).then_inc(A2["q_in"], 16)

        def pe_a2(pe):
            pe.wait_ge(A2["k_in"], 16)
            pe.wait_ge(F1["acc"], T)
            for dc in range(C):
                for c in range(C):
                    i = nc.tensor.matmul(bank(2 + dc // 2)[:, (dc % 2) * 256:(dc % 2 + 1) * 256],
                                         WR[:, c * D + dc * P:c * D + (dc + 1) * P], CT[:, c, :],
                                         start=c == 0, stop=c == C - 1)
            i.then_inc(A2["k_mm"], 1)
            pe.wait_ge(A2["kt_ready"], 1)
            pe.wait_ge(A2["q_in"], 16)
            for ic in range(C):
                for dc in range(C):
                    nc.tensor.matmul(bank(4 + ic // 2)[:, (ic % 2) * 256:(ic % 2 + 1) * 256],
                                     OR[:, dc * D + ic * P:dc * D + (ic + 1) * P],
                                     KT2[:, dc * 256:(dc + 1) * 256], start=dc == 0, stop=dc == C - 1)
            for dc in range(C):
                i = nc.tensor.matmul(bank(6)[0:1, 0:256], b2[:, dc:dc + 1], KT2[:, dc * 256:(dc + 1) * 256],
                                     start=dc == 0, stop=dc == C - 1)
            i.then_inc(A2["m_mm"], 1)

            def scores(t):
                if t == 0:
                    pe.wait_ge(A2["mlo"], 1)
                tok = slice(t * P, (t + 1) * P)
                o = bank(7)[:, t * SK:(t + 1) * SK]
                b = t // 2
                nc.tensor.matmul(o, ones[0:1, :], BK[:, b * SK:(b + 1) * SK], start=True, stop=False)
                for c in range(C):
                    m = slice(c * 256 + b * SK, c * 256 + (b + 1) * SK)
                    i = mm3(o, HTh[:, c, tok], HTl[:, c, tok], OTh[:, m], OTl[:, m], False, c == C - 1)
                i.then_inc(A2["s_mm"], 1)
            pe_norm(pe, 4, scores)
            pe.wait_ge(A2["probs"], 1)
            for t in range(T):
                i = nc.tensor.transpose(bank(2 + t // 4)[0:SK, (t % 4) * P:(t % 4 + 1) * P],
                                        s_sb[:, 0, t * SK:(t + 1) * SK], ident[:])
            i.then_inc(A2["t_mm"], 1)
            pe.wait_ge(A2["pt_ready"], 1)
            pe.wait_ge(A2["b_in"], 16)
            for t in range(T):
                if t >= 2:
                    pe.wait_ge(A2["acc"], t - 1)
                b = t // 2
                nc.tensor.matmul(bank(4 + t % 2), PT[0:SK, t * P:(t + 1) * P], CB[:, b * D:(b + 1) * D],
                                 start=True, stop=True).then_inc(A2["mm"], 1)

        def act_a2(act):
            act.wait_ge(A2["k_mm"], 1)
            act.wait_ge(F1["mm"], T)
            for dc in range(C):
                i = nc.scalar.activation(KT2[:, dc * 256:(dc + 1) * 256],
                                         bank(2 + dc // 2)[:, (dc % 2) * 256:(dc % 2 + 1) * 256], ACT.Identity,
                                         bias=b2[:, C + dc:C + dc + 1])
            i.then_inc(A2["kt_ready"], 1)
            act.wait_ge(A2["m_mm"], 1)
            nc.scalar.copy(BK, bank(6)[0:1, 0:256])
            nc.scalar.copy(OTh[:], bank(4, 2)).then_inc(A2["mhi"], 1)
            act_norm(act, 4)
            act.wait_ge(A2["shifted"], 1)
            nc.scalar.activation(s_sb[:, 0, 0:512], s_sb[:, 0, 0:512], ACT.Exp, scale=float(D) ** -0.5)\
                .then_inc(A2["exps"], 1)
            act.wait_ge(A2["t_mm"], 1)
            nc.scalar.copy(PT[0:SK, :], bank(2, 2)[0:SK, :]).then_inc(A2["pt_ready"], 1)

        def dve_a2(dve):
            dve.wait_ge(A2["mhi"], 1)
            nc.vector.tensor_tensor(OTl[:], bank(4, 2), OTh[:].bitcast(F32), ALU.subtract).then_inc(A2["mlo"], 1)
            dve_norm(dve, 4, PAIRS - 1)
            dve.wait_ge(A2["s_mm"], T)
            softmax_shift(dve, s_sb[:, 0, 0:512], bank(7), T, SK, sm[:, 1, :]).then_inc(A2["shifted"], 1)
            dve.wait_ge(A2["exps"], 1)
            softmax_norm(dve, s_sb[:, 0, 0:512], T, SK, sm[:, 2, :]).then_inc(A2["probs"], 1)
            dve_sum(dve, A2, 2, 0, (4, 5))

        HW = 3 * D

        def sp_f2(sp):
            def load(f, par):
                at = par * HW
                nc_sem = F2["in0"] if par == 0 else F2["in1"]
                for k in range(2):
                    sp.dma_start(WR[:, at + k * D:at + (k + 1) * D], scratch[:, k, bass.ds(f * D, D)])\
                        .then_inc(nc_sem, 16)
                w3v = WR[:, at + 2 * D:at + 3 * D].rearrange("p (r h) -> p r h", r=4)
                for r in range(4):
                    sp.dma_start(w3v[:, r, :], scratch[:, 2, bass.ds(f * P + r * HF, P)]).then_inc(nc_sem, 16)
            sp.wait_ge(A["nf_stored"], 16 * NG)
            sp.wait_ge(A2["k_mm"], 1)
            load(0, 0)
            load(1, 1)
            with sp.Fori(0, 4) as k:
                for par in range(2):
                    f = k * 2 + (par + 2)
                    sp.wait_ge(F2["t_mm"], f * 3 - 3)
                    load(f, par)
            sp.wait_ge(F2["t_mm"], 3 * (NF - 2))
            load(NF - 1, 0)

        def pe_f2(pe):
            def turn_w(f, par, first=False):
                pe.wait_ge(F2["in0"] if par == 0 else F2["in1"], f * 48 + (96 - 48 * par))
                for k in range(3):
                    if k == 0 and not first:
                        pe.wait_ge(F2["wlo"], f * 3)
                    if k == 2:
                        pe.wait_ge(F2["wlo"], f * 3 + 1)
                    for c in range(C):
                        at = par * HW + k * D + c * P
                        i = nc.tensor.transpose(bank(5 + k % 2)[:, c * P:(c + 1) * P], WR[:, at:at + P], ident[:])
                    i.then_inc(F2["t_mm"], 1)

            def half_gate_up(par, k, th):
                for c in range(C):
                    w = slice(par * HW + k * D + c * P, par * HW + k * D + (c + 1) * P)
                    tok = slice(th * 512, (th + 1) * 512)
                    i = mm3(bank(2 * k + th), Wh[:, w], Wl[:, w], HTh[:, c, tok], HTl[:, c, tok],
                            c == 0, c == C - 1)
                return i

            def gate_up(f, par):
                pe.wait_ge(F2["wlo"], f * 3 + 2)
                pe.wait_ge(F2["act"], f)
                for k in range(2):
                    half_gate_up(par, k, 0)
                    i = half_gate_up(par, k, 1)
                    i.then_inc(F2["g_mm" if k == 0 else "u_mm"], 1)

            def down(f, par):
                pe.wait_ge(F2["alo"], f + 1)
                pe.wait_ge(F2["wlo"], f * 3 + 3)
                w = slice(par * HW + 2 * D, (par + 1) * HW)
                for t in range(T):
                    pe.wait_ge(F2["acc"], f * T + (t + 1))
                    tok = slice(par * 1024 + t * P, par * 1024 + (t + 1) * P)
                    mm3(bank(7 if t % 2 == 0 else 4), Oh[:, tok], Ol[:, tok], Wh[:, w], Wl[:, w], True, True)\
                        .then_inc(F2["mm"], 1)
            pe.wait_ge(A2["acc"], T)
            turn_w(0, 0, True)
            turn_w(1, 1)

            def first_products(t):
                if t % 4 == 3:
                    pe.wait_ge(F2["wlo"], 2)
                    for k in range(2):
                        i = half_gate_up(0, k, t // 4)
                        if t // 4 == 1:
                            i.then_inc(F2["g_mm" if k == 0 else "u_mm"], 1)
            pe_norm(pe, 5, first_products)
            with pe.Fori(0, 4) as k:
                for par in range(2):
                    f = k * 2 + par
                    gate_up(f + 1, 1 - par)
                    down(f, par)
                    turn_w(f + 2, par)
            gate_up(NF - 2, 1)
            down(NF - 3, 0)
            turn_w(NF - 1, 0)
            gate_up(NF - 1, 0)
            down(NF - 2, 1)
            down(NF - 1, 0)

        def w_parts(par, k):
            v = [t_[:, par * HW + k * D:par * HW + (k + 1) * D] for t_ in (Wh, Wl)]
            if k < 2:
                return v
            return [x.rearrange("p (q r) -> p r q", r=4) for x in v]

        def w_bank(k):
            return bank(5 + k % 2) if k < 2 else bank(5).rearrange("p (r q) -> p r q", r=4)

        def act_f2(act):
            def high(f, par):
                for k in range(3):
                    act.wait_ge(F2["t_mm"], f * 3 + (k + 1))
                    nc.scalar.copy(w_parts(par, k)[0], w_bank(k)).then_inc(F2["whi"], 1)

            def silu(f, par):
                act.wait_ge(F2["g_mm"], f + 1)
                nc.scalar.activation(s_sb[:, 0, :], bank(0, 2), ACT.Silu).then_inc(F2["silu"], 1)
                act.wait_ge(F2["act"], f + 1)
                nc.scalar.copy(Oh[:, par * 1024:(par + 1) * 1024], s_sb[:, 1, :]).then_inc(F2["ahi"], 1)
            silu(0, 0)
            with act.Fori(0, 4) as k:
                for par in range(2):
                    f = k * 2 + par
                    silu(f + 1, 1 - par)
                    high(f + 2, par)
            silu(NF - 2, 1)
            high(NF - 1, 0)
            silu(NF - 1, 0)

        def act_f2_first(act):
            for f in range(2):
                for k in range(3):
                    act.wait_ge(F2["t_mm"], f * 3 + k + 1)
                    nc.scalar.copy(w_parts(f, k)[0], w_bank(k)).then_inc(F2["whi"], 1)

        def dve_f2(dve):
            def low(f, par):
                for k in range(3):
                    dve.wait_ge(F2["whi"], f * 3 + (k + 1))
                    hi, lo = w_parts(par, k)
                    nc.vector.tensor_tensor(lo, w_bank(k), hi.bitcast(F32), ALU.subtract).then_inc(F2["wlo"], 1)

            def product(f):
                dve.drain()
                dve.wait_ge(F2["silu"], f + 1)
                dve.wait_ge(F2["u_mm"], f + 1)
                nc.vector.tensor_tensor(s_sb[:, 1, :], bank(2, 2), s_sb[:, 0, :], ALU.mult).then_inc(F2["act"], 1)

            def low_act(f, par):
                dve.wait_ge(F2["ahi"], f + 1)
                cols = slice(par * 1024, (par + 1) * 1024)
                nc.vector.tensor_tensor(Ol[:, cols], s_sb[:, 1, :], Oh[:, cols].bitcast(F32), ALU.subtract)\
                    .then_inc(F2["alo"], 1)

            def add(f, ts):
                for t in ts:
                    dve.wait_ge(F2["mm"], f * T + (t + 1))
                    nc.vector.scalar_tensor_tensor(X[:, t, :], bank(7 if t % 2 == 0 else 4), tg[:, 1, 2:3],
                                                   X[:, t, :], ALU.mult, ALU.add).then_inc(F2["acc"], 1)
                    if isinstance(f, int) and f == NF - 1 and t % 2 and t < T - 1:
                        dve_stats(dve, t // 2)
            low(0, 0)
            low(1, 1)
            dve.drain().then_inc(F2["acc"], 1)
            dve.drain().then_inc(F2["acc"], 1)
            dve_norm(dve, 5, PAIRS - 1)
            product(0)
            low_act(0, 0)

            def step(f, par, more):
                if more:
                    product(f + 1)
                add(f, range(0, 4))
                if more:
                    low_act(f + 1, 1 - par)
                add(f, range(4, 8))
            with dve.Fori(0, 4) as k:
                for par in range(2):
                    f = k * 2 + par
                    step(f, par, True)
                    low(f + 2, par)
                dve.drain()
            step(NF - 3, 0, True)
            low(NF - 1, 0)
            step(NF - 2, 1, True)
            step(NF - 1, 0, False)

        def at3(lo, n):
            return AR[:, lo:lo + n]
        NM = NS * NS
        LG = at3(4096, T * NL)
        Z = at3(4352, T * NM)
        K3 = at3(4480, T * NM)
        TM = at3(4608, T * NM)
        PP = at3(4736, T * 2 * NS)
        RR = at3(4800, T * NS)
        CC = at3(4832, T * NS)
        MX = at3(4864, T * 2 * NS)
        SG = at3(4928, 4)
        XP = at3(5120, T * P)
        WB = at3(6144, P)

        def sp_f3(sp):
            sp.wait_ge(A["w_split"], 6 * NG)
            sp.wait_ge(A["acc"], 16 * NG + 2)
            sp.dma_start(WR[:, 0:C * NL], w24_d).then_inc(F3["w_in"], 16)
            sp.dma_start(WB, wbr_d).then_inc(F3["w_in"], 16)

        Y = at3(6400, T * P)
        PTMP = at3(7424, D)
        XTMP = at3(8192, T * P)
        T_DVE = 6

        def pool_f3(pool):
            pool_norm(pool, 7)
            tmp = PTMP.rearrange("p (i c) -> p i c", i=NS)

            def add_spread(t, src, weights):
                nc.gpsimd.tensor_tensor(tmp, src.unsqueeze(1).to_broadcast([P, NS, P]),
                                        weights.unsqueeze(2).to_broadcast([P, NS, P]), ALU.mult)
                pool.drain()
                i = nc.gpsimd.tensor_tensor(X[:, t, :], X[:, t, :], PTMP, ALU.add)
                return i
            pool.wait_ge(F3["post"], 1)
            P3 = PP.rearrange("p (t n) -> p t n", t=T)
            H4 = AR[:, 0:T * D].rearrange("p (t n c) -> p t n c", t=T, n=NS)
            for n in range(NS):
                dst = XP if n == 0 else XTMP
                nc.gpsimd.tensor_tensor(dst.rearrange("p (t c) -> p t c", t=T), H4[:, :, n, :],
                                        P3[:, :, n].unsqueeze(2).to_broadcast([P, T, P]), ALU.mult)
                pool.drain()
                if n:
                    nc.gpsimd.tensor_tensor(XP, XP, XTMP, ALU.add)
                    pool.drain()
            pool.drain().then_inc(F3["pre"], 1)
            nc.gpsimd.tensor_tensor(PP, PP, tg[:, 1, 3:4].to_broadcast([P, T * 2 * NS]), ALU.mult)
            pool.drain()
            pool.wait_ge(F3["y_sb"], 1)
            for t in range(T):
                i = add_spread(t, Y[:, t * P:(t + 1) * P], P3[:, t, NS:2 * NS])
                pool.drain()
            pool.drain().then_inc(F3["posted"], 1)
            pool.wait_ge(F3["mixed"], 1)
            H3 = K3.rearrange("p (t n) -> p t n", t=T)
            for t in range(T_DVE, T):
                for j in range(NS):
                    add_spread(t, hn_of(7, t)[:, j * P:(j + 1) * P], H3[:, t, j:NM:NS])
                    pool.drain()
                pool.drain().then_inc(F3["done_pool"], 1)

        def pe_f3(pe):
            def logits(t):
                if t == 0:
                    pe.wait_ge(F3["wlo"], 1)
                tok = slice(t * P, (t + 1) * P)
                for c in range(C):
                    w = slice(c * NL, (c + 1) * NL)
                    i = mm3(bank(7)[:, t * NL:(t + 1) * NL], HTh[:, c, tok], HTl[:, c, tok], Wh[:, w], Wl[:, w],
                            c == 0, c == C - 1)
                i.then_inc(F3["lg_mm"], 1)
            pe_norm(pe, 7, logits)
            pe.wait_ge(F3["pre"], 1)
            for t in range(T):
                i = nc.tensor.transpose(bank(2, 2)[:, t * P:(t + 1) * P], XP[:, t * P:(t + 1) * P], ident[:])
            i.then_inc(F3["preT_mm"], 1)
            pe.wait_ge(F3["preT"], 1)
            for t in range(T):
                i = nc.tensor.matmul(bank(4, 2)[:, t * P:(t + 1) * P], PT[:, t * P:(t + 1) * P], WB,
                                     start=True, stop=True)
            i.then_inc(F3["y_mm"], 1)

        def act_f3(act):
            act.wait_ge(F3["w_in"], 32)
            nc.scalar.copy(Wh[:, 0:C * NL], WR[:, 0:C * NL]).then_inc(F3["w_hi"], 1)
            act_norm(act, 7)
            asked = [0]

            def run(out, in_, f, **kw):
                asked[0] += 1
                act.wait_ge(F3["to_act"], asked[0])
                nc.scalar.activation(out, in_, f, **kw).then_inc(F3["from_act"], 1)
            run(PP, PP, ACT.Exp)
            run(SG[:, 0:1], gate[:], ACT.Exp, scale=-1.0)
            for _ in range(2):
                run(K3, Z, ACT.Exp)
                run(MX[:, 0:T * NS], MX[:, 0:T * NS], ACT.Ln)
            run(K3, Z, ACT.Exp)
            act.wait_ge(F3["preT_mm"], 1)
            nc.scalar.copy(PT[:], bank(2, 2)).then_inc(F3["preT"], 1)
            act.wait_ge(F3["y_mm"], 1)
            nc.scalar.copy(Y, bank(4, 2)).then_inc(F3["y_sb"], 1)
            run(AR[:, 4800:4864], AR[:, 4800:4864], ACT.Ln)
            run(K3, Z, ACT.Exp)

        def dve_f3(dve):
            dve.wait_ge(F3["w_hi"], 1)
            nc.vector.tensor_tensor(Wl[:, 0:C * NL], WR[:, 0:C * NL], Wh[:, 0:C * NL].bitcast(F32), ALU.subtract)\
                .then_inc(F3["wlo"], 1)
            dve_norm(dve, 7, PAIRS - 1)
            dve.wait_ge(F3["lg_mm"], T)
            asked = [0]

            def ask(i):
                asked[0] += 1
                i.then_inc(F3["to_act"], 1)

            def answered():
                dve.wait_ge(F3["from_act"], asked[0])
            LG3 = LG.rearrange("p (t n) -> p t n", t=T)
            nc.vector.tensor_tensor(LG3, bank(7)[:, 0:T * NL].rearrange("p (t n) -> p t n", t=T),
                                    rms[:].unsqueeze(2).to_broadcast([P, T, NL]), ALU.mult)
            dve.drain()
            nc.vector.tensor_tensor(LG3, LG3, bases[:].unsqueeze(1).to_broadcast([P, T, NL]), ALU.add)
            dve.drain()
            Z4 = Z.rearrange("p (t i j) -> p t i j", t=T, i=NS)
            K4 = K3.rearrange("p (t i j) -> p t i j", t=T, i=NS)
            T4 = TM.rearrange("p (t i j) -> p t i j", t=T, i=NS)
            nc.vector.tensor_scalar(Z.rearrange("p (t n) -> p t n", t=T), LG3[:, :, 0:NM], 10.0, None, ALU.mult)
            nc.vector.tensor_copy(PP.rearrange("p (t n) -> p t n", t=T), LG3[:, :, NM:NL])
            dve.drain()
            ask(softmax_shift(dve, PP, PP, 2 * T, NS, MX))
            dve.drain()

            def view(x, rows):
                return x if rows else x.rearrange("p t i j -> p t j i")

            def spread(v, rows):
                v = v.rearrange("p (t n) -> p t n", t=T)
                return (v.unsqueeze(3) if rows else v.unsqueeze(2)).to_broadcast([P, T, NS, NS])
            asked[0] += 1
            nc.vector.tensor_copy(SG[:, 1:2], gate[:]).then_inc(F3["to_act"], 1)
            for rows in (True, False):
                M = MX[:, 0:T * NS]
                nc.vector.tensor_reduce(M, view(Z4, rows), AX.X, ALU.max)
                dve.drain()
                ask(nc.vector.tensor_tensor(Z4, Z4, spread(M, rows), ALU.subtract))
                answered()
                ask(nc.vector.tensor_reduce(M, view(K4, rows), AX.X, ALU.add))
                answered()
                i = nc.vector.tensor_tensor(Z4, Z4, spread(M, rows), ALU.subtract)
                dve.drain()
            ask(nc.vector.memset(CC, 1.0))
            softmax_norm(dve, PP, 2 * T, NS, MX).then_inc(F3["post"], 1)
            dve.drain()
            answered()

            def balance():
                for rows, given, got in ((True, CC, RR), (False, RR, CC)):
                    nc.vector.tensor_tensor(T4, K4, spread(given, not rows), ALU.mult)
                    dve.drain()
                    nc.vector.tensor_reduce(got, view(T4, rows), AX.X, ALU.add)
                    dve.drain()
                    nc.vector.reciprocal(got, got)
                    dve.drain()
            with dve.Fori(0, SK_LINEAR // SK_UNROLL) as _:
                for _ in range(SK_UNROLL):
                    balance()
            ask(dve.drain())
            answered()
            nc.vector.tensor_tensor(Z4, Z4, spread(RR, True), ALU.add)
            dve.drain()
            ask(nc.vector.tensor_tensor(Z4, Z4, spread(CC, False), ALU.add))
            answered()
            dve.drain()
            nc.vector.memset(CC, 1.0)
            dve.drain()
            balance()
            with dve.Fori(0, SK_LINEAR // SK_UNROLL) as _:
                for _ in range(SK_UNROLL):
                    balance()
            nc.vector.tensor_tensor(K4, K4, spread(RR, True), ALU.mult)
            nc.vector.tensor_scalar(SG[:, 0:1], SG[:, 0:1], 1.0, None, ALU.add)
            dve.drain()
            nc.vector.tensor_tensor(K4, K4, spread(CC, False), ALU.mult)
            nc.vector.reciprocal(SG[:, 0:1], SG[:, 0:1])
            dve.drain()
            nc.vector.tensor_tensor(SG[:, 1:2], SG[:, 0:1], tg[:, 1, 3:4], ALU.mult)
            dve.drain()
            nc.vector.tensor_tensor(SG[:, 2:3], tg[:, 1, 3:4], SG[:, 1:2], ALU.subtract)
            nc.vector.tensor_scalar(K3, K3, SG[:, 1:2], None, ALU.mult)
            dve.drain()
            diag = K3.rearrange("p (t n) -> p t n", t=T)[:, :, 0:NM:NS + 1]
            nc.vector.tensor_scalar(diag, diag, SG[:, 2:3], None, ALU.add)
            dve.drain().then_inc(F3["mixed"], 1)
            dve.wait_ge(F3["posted"], 1)
            H3 = K3.rearrange("p (t n) -> p t n", t=T)
            for t0 in range(0, T_DVE, 2):
                for j in range(NS):
                    for t in (t0, t0 + 1):
                        for i_ in range(NS):
                            xt = X[:, t, i_ * P:(i_ + 1) * P]
                            nc.vector.scalar_tensor_tensor(xt, hn_of(7, t)[:, j * P:(j + 1) * P],
                                                           H3[:, t, i_ * NS + j:i_ * NS + j + 1], xt,
                                                           ALU.mult, ALU.add)
                    if j < NS - 1:
                        dve.drain()
                dve.drain().then_inc(F3["done"], 1)

        CONSTS = 16 * 8

        @block.sync
        def _(sp):
            sp.dma_start(X[:], x_d.rearrange("(t p) n -> p t n", p=P)).then_inc(x_in, 16)
            sp.dma_start(CT[:], ctxT_d).then_inc(ctx_in, 16)
            sp.dma_start(gates[:, 0, :], gx_d.to_broadcast([P, 4])).then_inc(consts_in, 16)
            sp.dma_start(gates[:, 1, :], gf_d.to_broadcast([P, 4])).then_inc(consts_in, 16)
            sp.dma_start(lnw[:], lnw_d.to_broadcast([P, D])).then_inc(consts_in, 16)
            sp.dma_start(qkn[:], qkn_d).then_inc(consts_in, 16)
            sp.dma_start(b2[:], b2_d).then_inc(consts_in, 16)
            sp.dma_start(iot[:], iota_d.to_broadcast([P, NE])).then_inc(consts_in, 16)
            sp.dma_start(bases[:], bases_d.to_broadcast([P, NL])).then_inc(consts_in, 16)
            sp.dma_start(gate[:], gate_d.to_broadcast([P, 1])).then_inc(consts_in, 16)
            sp_attention(sp, A, True)
            sp_a1(sp)
            sp_f1(sp)
            sp_a2(sp)
            sp_f2(sp)
            sp_attention(sp, A, False)
            sp_f3(sp)
            for t in range(T):
                if t < T_DVE:
                    sp.wait_ge(F3["done"], t // 2 + 1)
                else:
                    sp.wait_ge(F3["done_pool"], t - T_DVE + 1)
                sp.dma_start(out_d[t * P:(t + 1) * P, :], X[:, t, :]).then_inc(out_stored, 16)
            sp.wait_ge(out_stored, 16 * T)

        @block.gpsimd
        def _(pool):
            nc.gpsimd.memset(ident[:], 0.0)
            nc.gpsimd.memset(ones[:], 1.0)
            nc.gpsimd.memset(half[:], -0.5)
            nc.gpsimd.memset(tiny[:, 0:8], EPS)
            nc.gpsimd.memset(tiny[:, 8:16], EPS * DH)
            nc.gpsimd.memset(hm[:], 1.0)
            for k in range(1, NUP):
                nc.gpsimd.memset(nf_bias[:, k:k + 1], -UP[k][0] * FAR)
            pool.drain()
            nc.gpsimd.affine_select(out=ident[:], in_=ident[:], compare_op=ALU.not_equal, fill=1.0, base=0,
                                    pattern=[[-1, P]], channel_multiplier=1)
            nc.gpsimd.affine_select(out=hm[:], in_=hm[:], compare_op=ALU.is_ge, fill=0.0, base=0,
                                    pattern=[[-DH1, HC1]], channel_multiplier=1)
            pool.drain()
            nc.gpsimd.affine_select(out=hm[:], in_=hm[:], compare_op=ALU.is_ge, fill=0.0, base=DH1 - 1,
                                    pattern=[[DH1, HC1]], channel_multiplier=-1)
            pool.drain().then_inc(pool_consts, 1)
            pool.wait_ge(ctx_hi, 1)
            pool_low(CTh[:], CTl[:], CT[:]).then_inc(ctx_split, 1)
            pool_norm(pool, 0)
            pool_attention(pool, A, True)
            def low_f0():
                pool.wait_ge(F0["w_hi"], 1)
                pool_low(Oh[:], Ol[:], OR[:]).then_inc(F0["split"], 1)
            pool_norm(pool, 1, low_f0)
            pool_a1(pool)
            pool_f1(pool)
            pool_norm(pool, 4)
            pool_norm(pool, 5)
            pool_attention(pool, A, False)
            pool_f3(pool)

        @block.scalar
        def _(act):
            act.wait_ge(consts_in, CONSTS)
            nc.scalar.activation(tg[:], gates[:], ACT.Tanh).then_inc(gates_ready, 1)
            act.wait_ge(ctx_in, 16)
            nc.scalar.copy(CTh[:], CT[:]).then_inc(ctx_hi, 1)
            act_norm(act, 0)
            act_attention(act, A, True)
            act.wait_ge(F0["packed"], 1)
            act.wait_ge(A["wo_mm"], 2 * B * NG)
            nc.scalar.copy(Oh[:], OR[:]).then_inc(F0["w_hi"], 1)
            act_norm(act, 1)
            act_a1(act)
            act_f1(act)
            act_a2(act)
            act_f2_first(act)
            act_norm(act, 5)
            act_f2(act)
            act_attention(act, A, False)
            act_f3(act)

        @block.tensor
        def _(pe):
            pe_attention(pe, A, True)
            pe_f0(pe)
            pe_a1(pe)
            pe_f1(pe)
            pe_a2(pe)
            pe_f2(pe)
            pe_attention(pe, A, False)
            pe_f3(pe)

        @block.vector
        def _(dve):
            dve_norm(dve, 0)
            dve.wait_ge(gates_ready, 1)
            dve_attention(dve, A, True)
            dve_norm(dve, 1, PAIRS - 1)
            dve_sum(dve, F0, 0, 1, F0_BANKS)
            dve_a1(dve)
            dve_f1(dve)
            dve_a2(dve)
            dve_f2(dve)
            dve_norm(dve, 6, PAIRS - 1)
            dve_attention(dve, A, False)
            dve_f3(dve)


def lay_out(i):
    f = {k: np.asarray(v) for k, v in i.items()}

    def chunks(w):
        return w.reshape(C, P, -1).transpose(1, 0, 2)

    def group(wq, wk, wv):
        g = [np.concatenate([wq[:, k * WQ:(k + 1) * WQ], wk[:, k * DH:(k + 1) * DH], wv[:, k * DH:(k + 1) * DH]], 1)
             for k in range(NG)]
        return np.stack([chunks(w).reshape(P, -1) for w in g])

    def rows(wo):
        return wo.reshape(NG, HG, DH, D).transpose(0, 2, 1, 3).reshape(NG, P, -1)

    ctxf = f['ctx_4096'].reshape(B * SK, D)
    w1, w2 = (np.concatenate([f[f'L2_ffn_{k}'], np.zeros((NF * P - HF, D), np.float32)])
              .reshape(NF, P, D).transpose(1, 0, 2).reshape(P, NG, NBU * QB) for k in ('w1', 'w2'))
    w3 = np.concatenate([f['L2_ffn_w3'].reshape(P, NB3 * QB), np.zeros((P, NFW - NB3 * QB), np.float32)], 1)\
        .reshape(P, NG, NBU * QB)
    kr = f['L1_xattn_wk'].reshape(NKV1, DH1, D)
    kr = np.stack([np.concatenate([kr[2 * c + h // 4] for h in range(HC1)]) for c in range(C)])
    packed = f['L0_ffn_W_q'].reshape(D // 2, D).T

    def groups(z):
        return z.reshape(D, C, 2).transpose(2, 1, 0).reshape(2, -1)
    out = {
        'x': f['x'].reshape(B * S, D),
        'ctxT': chunks(ctxf.T),
        'ctxB': f['ctx_4096'].transpose(1, 0, 2),
        'gx': f['g_xattn'].reshape(1, 4), 'gf': f['g_ffn'].reshape(1, 4),
        'wl': np.concatenate([group(f['L0_xattn_wq'], f['L0_xattn_wk'], f['L0_xattn_wv']),
                        group(f['L3_xattn_q_proj_w'].T, f['L3_xattn_k_proj_w'].T, f['L3_xattn_v_proj_w'].T)]),
        'ol': np.concatenate([rows(f['L0_xattn_wo']), rows(f['L3_xattn_o_proj_w'].T)]),
        'w4': np.ascontiguousarray(chunks(packed).reshape(P, -1)).view(np.int32),
        'sc4': groups(f['L0_ffn_scale']), 'ze4': groups(f['L0_ffn_zero']),
        'l1wqv': np.concatenate([chunks(f['L1_xattn_wq'].T).reshape(P, -1), chunks(f['L1_xattn_wv'].T).reshape(P, -1)], 1),
        'l1kr': chunks(kr.reshape(C * P, D).T).reshape(P, -1),
        'l1o': chunks(f['L1_xattn_wo'].T).reshape(P, -1),
        'lnw': f['L1_xattn_ln_w'].reshape(1, D),
        'l1f': chunks(np.concatenate([f['L1_ffn_base_W'], f['L1_ffn_gate_W'], f['L1_ffn_lora_A'].reshape(ER, D)]).T)
        .reshape(P, -1),
        'lb': f['L1_ffn_lora_B'].transpose(0, 2, 1).reshape(2, EH, D).transpose(1, 0, 2).reshape(EH, -1),
        'l2k': chunks(f['L2_xattn_Wk'].T).reshape(P, -1), 'l2q': chunks(f['L2_xattn_Wq']).reshape(P, -1),
        'b2': np.stack([f['L2_xattn_bq'].reshape(C, P).T, f['L2_xattn_bk'].reshape(C, P).T], 1).reshape(P, -1),
        'nf': np.stack([w1, w2, w3], 2).transpose(1, 0, 2, 3).reshape(NG, P, NBT * QB),
        'qkn': np.stack([f['L3_xattn_q_norm_w'], f['L3_xattn_k_norm_w']], 1),
        'mask': f['mask_1x1xSxS2_ff0'].reshape(2, P, SK).transpose(1, 0, 2).reshape(P, -1),
        'iota': (np.arange(NE, dtype=np.float32) - BIG_INDEX).reshape(1, NE).astype(np.float32),
        'w24': chunks(np.concatenate([f['L3_ffn_W_res'], f['L3_ffn_W_pre'], f['L3_ffn_W_post']]).T).reshape(P, -1),
        'bases': np.concatenate([f['L3_ffn_H_res_base'].reshape(-1), f['L3_ffn_H_pre_base'],
                                 f['L3_ffn_H_post_base']]).reshape(1, NL),
        'gate': f['L3_ffn_gate'].reshape(1, 1),
        'wbr': f['L3_ffn_W_branch'],
    }
    return {k: np.ascontiguousarray(v) for k, v in out.items()}


def kernel(**inputs):
    import concourse.bacc as _bacc
    from concourse import mybir as _mybir
    from concourse.bass_utils import run_bass_kernel_spmd as _run

    nc = _bacc.Bacc("TRN2", target_bir_lowering=False, num_devices=1)
    arrays, args = {}, []
    for name, a in lay_out(inputs).items():
        arrays[f"in_{name}"] = a
        args.append(nc.dram_tensor(f"in_{name}", a.shape, _mybir.dt.from_np(a.dtype), kind="ExternalInput").ap())
    out = nc.dram_tensor("out", (B * S, D), _mybir.dt.float32, kind="ExternalOutput").ap()
    build(nc, *args, out)
    r = _run(nc, [arrays], core_ids=[0])
    return r.results[0]["out"].reshape(B, S, D)
```
